# Optimizing a Trainium2 kernel written in Bass

```python
import numpy as np
import jax
import jax.numpy as jnp

def _softmax(x, axis=-1):
    return jax.nn.softmax(x, axis=axis)

def _gelu(x):
    return jax.nn.gelu(x, approximate=True)

def _silu(x):
    return jax.nn.silu(x)

def _sigmoid(x):
    return jax.nn.sigmoid(x)

def _layernorm(x, axis=-1, eps=1e-05):
    m = jnp.mean(x, axis=axis, keepdims=True)
    v = jnp.var(x, axis=axis, keepdims=True)
    return (x - m) / jnp.sqrt(v + eps)

def _scatter_add(tgt, idx, src, axis=0):
    return tgt.at[idx].add(src)

def _segment_sum(src, seg, n):
    return jax.ops.segment_sum(src, seg, n)
kernel_name = 'mk_sandwich_d2_jaxref_r4_243eb2'

def setup_inputs(seed: int=0):
    np.random.seed(seed)
    _w = jnp.asarray

    def _L0_attn_setup():
        import jax, jax.numpy as jnp
        import numpy as np
        import math
        H = 512
        NH = 16
        HD = H // NH
        THETA = 10000.0

        def rotate_half(x):
            x1, x2 = (x[..., :HD // 2], x[..., HD // 2:])
            return jnp.concatenate((-x2, x1), axis=-1)

        def rope_tables(seq_len, dtype):
            inv_freq = 1.0 / THETA ** (np.arange(0, HD, 2, dtype=np.float32) / HD)
            t = np.arange(seq_len, dtype=np.float32)
            freqs = np.einsum('i,j->ij', t, inv_freq)
            emb = np.concatenate((freqs, freqs), axis=-1)
            return (jnp.asarray(np.cos(emb), dtype), jnp.asarray(np.sin(emb), dtype))
        key = jax.random.key(seed)
        ks = jax.random.split(key, 5)
        B, S = (2, 512)
        scale = 1.0 / math.sqrt(H)
        return {'hidden_states': jax.random.normal(ks[0], (B, S, H), jnp.float32), 'Wq': jax.random.normal(ks[1], (H, H), jnp.float32) * scale, 'Wk': jax.random.normal(ks[2], (H, H), jnp.float32) * scale, 'Wv': jax.random.normal(ks[3], (H, H), jnp.float32) * scale, 'Wo': jax.random.normal(ks[4], (H, H), jnp.float32) * scale}
    _L0_attn_in = _L0_attn_setup()

    def _L0_ffn_setup():
        import jax, jax.numpy as jnp
        import numpy as np
        DIM_IN = 512
        DIM_HIDDEN = 2048
        key = jax.random.key(seed)
        k_x, k_g, k_u, k_d = jax.random.split(key, 4)
        s_in = 1.0 / np.sqrt(DIM_IN)
        s_hid = 1.0 / np.sqrt(DIM_HIDDEN)
        x = jax.random.normal(k_x, (4, 512, DIM_IN), dtype=jnp.float32)
        w_gate = jax.random.uniform(k_g, (DIM_HIDDEN, DIM_IN), jnp.float32, -s_in, s_in)
        w_up = jax.random.uniform(k_u, (DIM_HIDDEN, DIM_IN), jnp.float32, -s_in, s_in)
        w_down = jax.random.uniform(k_d, (DIM_IN, DIM_HIDDEN), jnp.float32, -s_hid, s_hid)
        return {'x': x, 'w_gate': w_gate, 'w_up': w_up, 'w_down': w_down}
    _L0_ffn_in = _L0_ffn_setup()

    def _L1_attn_setup():
        import jax, jax.numpy as jnp
        import numpy as np
        EPS = 1e-06
        H, NOPE, ROPE, VD = (16, 128, 64, 128)
        QHD = NOPE + ROPE
        SCALE = QHD ** (-0.5)
        THETA = 10000.0

        def rmsnorm(x, w):
            x32 = x.astype(jnp.float32)
            var = jnp.mean(x32 * x32, axis=-1, keepdims=True)
            return (w * (x32 * jax.lax.rsqrt(var + EPS))).astype(x.dtype)

        def rope_cos_sin(seq_len):
            inv_freq = 1.0 / THETA ** (jnp.arange(0, ROPE, 2, dtype=jnp.float32) / ROPE)
            t = jnp.arange(seq_len, dtype=jnp.float32)
            freqs = jnp.outer(t, inv_freq)
            emb = jnp.concatenate([freqs, freqs], -1)
            return (jnp.cos(emb), jnp.sin(emb))

        def rotate_half(x):
            x1, x2 = (x[..., :x.shape[-1] // 2], x[..., x.shape[-1] // 2:])
            return jnp.concatenate([-x2, x1], axis=-1)
        key = jax.random.key(seed)
        ks = jax.random.split(key, 6)
        B, S, D = (2, 512, 512)
        return {'hidden_states': jax.random.normal(ks[0], (B, S, D), jnp.float32), 'q_a_w': jax.random.normal(ks[1], (384, D), jnp.float32) * 0.02, 'q_a_ln_w': jnp.ones((384,), jnp.float32), 'q_b_w': jax.random.normal(ks[2], (H * QHD, 384), jnp.float32) * 0.02, 'kv_a_w': jax.random.normal(ks[3], (128 + ROPE, D), jnp.float32) * 0.02, 'kv_a_ln_w': jnp.ones((128,), jnp.float32), 'kv_b_w': jax.random.normal(ks[4], (H * (NOPE + VD), 128), jnp.float32) * 0.02, 'o_w': jax.random.normal(ks[5], (D, H * VD), jnp.float32) * 0.02}
    _L1_attn_in = _L1_attn_setup()

    def _L1_ffn_setup():
        import jax, jax.numpy as jnp
        import numpy as np
        GROUP_SIZE = 64

        def ternary_quant(w_fp32, g=GROUP_SIZE):
            w = w_fp32.astype(jnp.bfloat16)
            w_g = w.reshape(-1, g)
            scale = jnp.clip(jnp.mean(jnp.abs(w_g), axis=-1, keepdims=True), 1e-08, None)
            q = jnp.clip(jnp.round(w_g / scale), -1, 1)
            w_hat = (q * scale).reshape(w.shape)
            return w + jax.lax.stop_gradient(w_hat - w)

        def rms_norm(x):
            eps = jnp.finfo(x.dtype).eps.astype(jnp.float32)
            xf = x.astype(jnp.float32)
            inv = jax.lax.rsqrt(jnp.mean(xf * xf, axis=-1, keepdims=True) + eps)
            return (xf * inv).astype(x.dtype)
        key = jax.random.key(seed)
        k1, k2, k3 = jax.random.split(key, 3)
        B, S, D = (2, 512, 512)
        H = 4 * D
        x = jax.random.normal(k1, (B, S, D), dtype=jnp.float32).astype(jnp.bfloat16)
        w_gate_up = jax.random.normal(k2, (2 * H, D), dtype=jnp.float32) * 0.02
        w_proj = jax.random.normal(k3, (D, H), dtype=jnp.float32) * 0.02
        return {'x': x, 'w_gate_up': w_gate_up, 'w_proj': w_proj}
    _L1_ffn_in = _L1_ffn_setup()
    _d = {'L0_attn_hidden_states': _L0_attn_in['hidden_states'], 'L0_attn_Wq': _L0_attn_in['Wq'], 'L0_attn_Wk': _L0_attn_in['Wk'], 'L0_attn_Wv': _L0_attn_in['Wv'], 'L0_attn_Wo': _L0_attn_in['Wo'], 'L0_ffn_w_gate': _L0_ffn_in['w_gate'], 'L0_ffn_w_up': _L0_ffn_in['w_up'], 'L0_ffn_w_down': _L0_ffn_in['w_down'], 'L1_attn_q_a_w': _L1_attn_in['q_a_w'], 'L1_attn_q_a_ln_w': _L1_attn_in['q_a_ln_w'], 'L1_attn_q_b_w': _L1_attn_in['q_b_w'], 'L1_attn_kv_a_w': _L1_attn_in['kv_a_w'], 'L1_attn_kv_a_ln_w': _L1_attn_in['kv_a_ln_w'], 'L1_attn_kv_b_w': _L1_attn_in['kv_b_w'], 'L1_attn_o_w': _L1_attn_in['o_w'], 'L1_ffn_w_gate_up': _L1_ffn_in['w_gate_up'], 'L1_ffn_w_proj': _L1_ffn_in['w_proj']}
    _x0 = _d['L0_attn_hidden_states']
    _d['L0_attn_hidden_states'] = jax.random.normal(jax.random.fold_in(jax.random.key(seed), 1), (2, 1024, 512), dtype=_x0.dtype)
    del _x0
    return _d

def reference(L0_attn_hidden_states, L0_attn_Wq, L0_attn_Wk, L0_attn_Wv, L0_attn_Wo, L0_ffn_w_gate, L0_ffn_w_up, L0_ffn_w_down, L1_attn_q_a_w, L1_attn_q_a_ln_w, L1_attn_q_b_w, L1_attn_kv_a_w, L1_attn_kv_a_ln_w, L1_attn_kv_b_w, L1_attn_o_w, L1_ffn_w_gate_up, L1_ffn_w_proj):

    def _L0_attn_ref(hidden_states, Wq, Wk, Wv, Wo):
        import jax, jax.numpy as jnp
        import numpy as np
        import math
        H = 512
        NH = 16
        HD = H // NH
        THETA = 10000.0

        def rotate_half(x):
            x1, x2 = (x[..., :HD // 2], x[..., HD // 2:])
            return jnp.concatenate((-x2, x1), axis=-1)

        def rope_tables(seq_len, dtype):
            inv_freq = 1.0 / THETA ** (np.arange(0, HD, 2, dtype=np.float32) / HD)
            t = np.arange(seq_len, dtype=np.float32)
            freqs = np.einsum('i,j->ij', t, inv_freq)
            emb = np.concatenate((freqs, freqs), axis=-1)
            return (jnp.asarray(np.cos(emb), dtype), jnp.asarray(np.sin(emb), dtype))
        B, S, _ = hidden_states.shape

        def proj(W):
            y = jnp.einsum('bsh,oh->bso', hidden_states, W)
            return y.reshape(B, S, NH, HD).transpose(0, 2, 1, 3)
        q, k, v = (proj(Wq), proj(Wk), proj(Wv))
        cos, sin = rope_tables(S, hidden_states.dtype)
        cos, sin = (cos[None, None], sin[None, None])
        q = q * cos + rotate_half(q) * sin
        k = k * cos + rotate_half(k) * sin
        scores = jnp.einsum('bhqd,bhkd->bhqk', q, k) / math.sqrt(HD)
        causal = jnp.triu(jnp.ones((S, S), bool), k=1)
        scores = jnp.where(causal, -jnp.inf, scores)
        attn = jax.nn.softmax(scores, axis=-1)
        out = jnp.einsum('bhqk,bhkd->bhqd', attn, v)
        out = out.transpose(0, 2, 1, 3).reshape(B, S, H)
        return jnp.einsum('bsh,oh->bso', out, Wo)

    def _L0_ffn_ref(x, w_gate, w_up, w_down):
        import jax, jax.numpy as jnp
        import numpy as np
        DIM_IN = 512
        DIM_HIDDEN = 2048
        gate = jnp.einsum('bsd,hd->bsh', x, w_gate)
        up = jnp.einsum('bsd,hd->bsh', x, w_up)
        gated = jax.nn.silu(gate) * up
        return jnp.einsum('bsh,dh->bsd', gated, w_down)

    def _L1_attn_ref(hidden_states, q_a_w, q_a_ln_w, q_b_w, kv_a_w, kv_a_ln_w, kv_b_w, o_w):
        import jax, jax.numpy as jnp
        import numpy as np
        EPS = 1e-06
        H, NOPE, ROPE, VD = (16, 128, 64, 128)
        QHD = NOPE + ROPE
        SCALE = QHD ** (-0.5)
        THETA = 10000.0

        def rmsnorm(x, w):
            x32 = x.astype(jnp.float32)
            var = jnp.mean(x32 * x32, axis=-1, keepdims=True)
            return (w * (x32 * jax.lax.rsqrt(var + EPS))).astype(x.dtype)

        def rope_cos_sin(seq_len):
            inv_freq = 1.0 / THETA ** (jnp.arange(0, ROPE, 2, dtype=jnp.float32) / ROPE)
            t = jnp.arange(seq_len, dtype=jnp.float32)
            freqs = jnp.outer(t, inv_freq)
            emb = jnp.concatenate([freqs, freqs], -1)
            return (jnp.cos(emb), jnp.sin(emb))

        def rotate_half(x):
            x1, x2 = (x[..., :x.shape[-1] // 2], x[..., x.shape[-1] // 2:])
            return jnp.concatenate([-x2, x1], axis=-1)
        B, S, D = hidden_states.shape
        q_a = hidden_states @ q_a_w.T
        q = rmsnorm(q_a, q_a_ln_w) @ q_b_w.T
        q = q.reshape(B, S, H, QHD).transpose(0, 2, 1, 3)
        q_nope, q_pe = (q[..., :NOPE], q[..., NOPE:])
        ckv_full = hidden_states @ kv_a_w.T
        ckv, k_pe_raw = (ckv_full[..., :128], ckv_full[..., 128:])
        kv = rmsnorm(ckv, kv_a_ln_w) @ kv_b_w.T
        kv = kv.reshape(B, S, H, NOPE + VD).transpose(0, 2, 1, 3)
        k_nope, v = (kv[..., :NOPE], kv[..., NOPE:])
        k_pe = k_pe_raw.reshape(B, 1, S, ROPE)
        cos, sin = rope_cos_sin(S)
        cos, sin = (cos[None, None], sin[None, None])
        q_pe = q_pe * cos + rotate_half(q_pe) * sin
        k_pe = k_pe * cos + rotate_half(k_pe) * sin
        query = jnp.concatenate([q_nope, q_pe], -1)
        key_s = jnp.concatenate([k_nope, jnp.broadcast_to(k_pe, (B, H, S, ROPE))], -1)
        scores = jnp.einsum('bhqd,bhkd->bhqk', query, key_s) * SCALE
        causal = jnp.tril(jnp.ones((S, S), bool))
        scores = jnp.where(causal[None, None], scores, -jnp.inf)
        probs = jax.nn.softmax(scores.astype(jnp.float32), axis=-1).astype(query.dtype)
        attn = jnp.einsum('bhqk,bhkd->bhqd', probs, v)
        attn = attn.transpose(0, 2, 1, 3).reshape(B, S, H * VD)
        return attn @ o_w.T

    def _L1_ffn_ref(x, w_gate_up, w_proj):
        import jax, jax.numpy as jnp
        import numpy as np
        GROUP_SIZE = 64

        def ternary_quant(w_fp32, g=GROUP_SIZE):
            w = w_fp32.astype(jnp.bfloat16)
            w_g = w.reshape(-1, g)
            scale = jnp.clip(jnp.mean(jnp.abs(w_g), axis=-1, keepdims=True), 1e-08, None)
            q = jnp.clip(jnp.round(w_g / scale), -1, 1)
            w_hat = (q * scale).reshape(w.shape)
            return w + jax.lax.stop_gradient(w_hat - w)

        def rms_norm(x):
            eps = jnp.finfo(x.dtype).eps.astype(jnp.float32)
            xf = x.astype(jnp.float32)
            inv = jax.lax.rsqrt(jnp.mean(xf * xf, axis=-1, keepdims=True) + eps)
            return (xf * inv).astype(x.dtype)
        wq_gu = ternary_quant(w_gate_up)
        gu = jnp.einsum('bsd,hd->bsh', x, wq_gu)
        gate, up = jnp.split(gu, 2, axis=-1)
        h = jax.nn.silu(gate) * up
        hn = rms_norm(h)
        wq_p = ternary_quant(w_proj)
        return jnp.einsum('bsh,dh->bsd', hn, wq_p)
    x = L0_attn_hidden_states
    x = x + _layernorm(_L0_attn_ref(_layernorm(x, axis=-1), L0_attn_Wq, L0_attn_Wk, L0_attn_Wv, L0_attn_Wo), axis=-1)
    x = x + _layernorm(_L0_ffn_ref(_layernorm(x, axis=-1), L0_ffn_w_gate, L0_ffn_w_up, L0_ffn_w_down), axis=-1)
    x = x + _layernorm(_L1_attn_ref(_layernorm(x, axis=-1), L1_attn_q_a_w, L1_attn_q_a_ln_w, L1_attn_q_b_w, L1_attn_kv_a_w, L1_attn_kv_a_ln_w, L1_attn_kv_b_w, L1_attn_o_w), axis=-1)
    x = x + _layernorm(_L1_ffn_ref(_layernorm(x, axis=-1), L1_ffn_w_gate_up, L1_ffn_w_proj), axis=-1)
    return x

_drawn_inputs = setup_inputs


def setup_inputs(seed=0):
    import zlib

    import numpy as np

    out = dict(_drawn_inputs(seed))
    spreads = {'L1_attn_q_a_ln_w': (1.0, 0.2), 'L1_attn_kv_a_ln_w': (1.0, 0.2)}
    factors = {}
    for name, (base, spread) in spreads.items():
        noise = np.random.default_rng([zlib.crc32(name.encode()), seed]).standard_normal(out[name].shape)
        drawn = base * np.exp(spread * noise) if base else spread * noise
        out[name] = jnp.asarray(drawn.astype(out[name].dtype))
    for name, factor in factors.items():
        out[name] = (out[name] * factor).astype(out[name].dtype)
    return out
```

```python
from contextlib import ExitStack

import numpy as np

import concourse.bass as bass
from concourse import mybir

F32 = mybir.dt.float32
F32R = mybir.dt.float32r
BF16 = mybir.dt.bfloat16
ACT = mybir.ActivationFunctionType
ALU = mybir.AluOpType
AX = mybir.AxisListType

P = 128
D = 512
KT = D // P
B, S = 2, 1024
TB = S // P
NT = B * TB
SPAN = 512
QT = SPAN // P
EPS_LN = 1e-5
MASKED = -1e30

NH = 16
HD0 = D // NH
HALF0 = HD0 // 2
HID = 4 * D
HG = 256
NG = HID // HG
NOPE, ROPE, VD, LAT, QL = 128, 64, 128, 128, 384
QHD = NOPE + ROPE
HALF1 = ROPE // 2
EPS_RMS = 1e-6
SCALE0, SCALE1 = float(HD0) ** -0.5, float(QHD) ** -0.5
EPS_F32 = float(np.finfo(np.float32).eps)
GROUP = 64
THREE = [(0, 0), (0, 1), (1, 0)]


def wait(eng, sem, value):
    if isinstance(value, int) and value <= 0:
        return
    eng.wait_ge(sem, value)


class Mem:

    def __init__(self, nc, ctx, tag, sems):
        self.nc, self.ctx, self.tag, self.sems = nc, ctx, tag, sems

    def sb(self, name, shape, dt=F32):
        return self.ctx.enter_context(self.nc.sbuf_tensor(f"{self.tag}_{name}", shape, dt))

    def ps(self, name, shape, dt=F32):
        return self.ctx.enter_context(self.nc.psum_tensor(f"{self.tag}_{name}", shape, dt))

    def sem(self, name):
        handle = self.nc.alloc_semaphore(name=f"{self.tag}_{name}")
        self.sems.append(handle)
        return handle


def f32(ap):
    return ap.bitcast(F32)


def constants(nc, m, ident, ident_bf, mask_bf):
    mask = m.sb("mask", [P, P])
    zeroed, made = m.sem("zeroed"), m.sem("made")
    with nc.Block() as block:
        @block.gpsimd
        def _(pool):
            nc.gpsimd.memset(ident[:, :], 0.0).then_inc(zeroed, 1)
            nc.gpsimd.memset(mask[:, :], 0.0).then_inc(zeroed, 1)
            pool.wait_ge(zeroed, 2)
            nc.gpsimd.affine_select(out=ident[:, :], in_=ident[:, :], compare_op=ALU.not_equal, fill=1.0,
                                    base=0, pattern=[[-1, P]], channel_multiplier=1).then_inc(made, 1)
            nc.gpsimd.affine_select(out=mask[:, :], in_=mask[:, :], compare_op=ALU.is_ge, fill=MASKED,
                                    base=0, pattern=[[-1, P]], channel_multiplier=1).then_inc(made, 1)
            pool.wait_ge(made, 2)
            nc.gpsimd.tensor_copy(ident_bf[:, :], ident[:, :]).then_inc(made, 1)
            nc.gpsimd.tensor_copy(mask_bf[:, :], mask[:, :]).then_inc(made, 1)
            pool.wait_ge(made, 4)


def transpose_weights(nc, m, ident, jobs, loads):
    RING = 4
    bank = m.ps("bank", [P, RING, SPAN])
    loaded = [m.sem(f"loaded{i}") for i in range(len(loads))]
    turned, high_done, low_done = m.sem("turned"), m.sem("high_done"), m.sem("low_done")
    with nc.Block() as block:
        @block.sync
        def _(sp):
            for i, (dst, src) in enumerate(loads):
                sp.dma_start(dst, src).then_inc(loaded[i], 16)

        @block.tensor
        def _(pe):
            have = -1
            for n, (blocks, view, hi, lo, need) in enumerate(jobs):
                if need > have:
                    for i in range(have + 1, need + 1):
                        pe.wait_ge(loaded[i], 16)
                    have = need
                wait(pe, low_done, n - RING + 1)
                for src, off in blocks:
                    rows, cols = src.shape[0], src.shape[1]
                    last = pe.transpose(bank[0:cols, n % RING, off:off + rows], src, ident[0:rows, 0:rows])
                last.then_inc(turned, 1)

        @block.scalar
        def _(act):
            for n, (blocks, view, hi, lo, need) in enumerate(jobs):
                if lo is not None:
                    act.wait_ge(turned, n + 1)
                    nc.scalar.copy(hi, view(bank[:, n % RING])).then_inc(high_done, 1)

        @block.vector
        def _(dve):
            for n, (blocks, view, hi, lo, need) in enumerate(jobs):
                if lo is None:
                    dve.wait_ge(turned, n + 1)
                    nc.vector.tensor_copy(hi, view(bank[:, n % RING])).then_inc(low_done, 1)
                else:
                    dve.wait_ge(high_done, n + 1)
                    nc.vector.tensor_tensor(lo, view(bank[:, n % RING]), f32(hi),
                                            ALU.subtract).then_inc(low_done, 1)
            dve.wait_ge(low_done, len(jobs))


def whole(cols):
    return lambda bank: bank[:, 0:cols]


def square_jobs(raw, dst_hl, w, need):
    return [([(raw[:, o, k * P:(k + 1) * P], o * P) for o in range(KT)], whole(D),
             dst_hl[:, 0, w, k, :], dst_hl[:, 1, w, k, :], need) for k in range(KT)]


def norm_transposed(nc, m, ident, src, tiles, xT_hl):
    x = m.sb("x", [P, tiles, D])
    xn = m.sb("xn", [P, 2, D])
    stats = m.sb("stats", [P, tiles, 6])
    mv = m.sb("mv", [P, tiles, 2])
    std = m.sb("std", [P, tiles])
    rstd = m.sb("rstd", [P, tiles])
    eps = m.sb("eps", [P, 1])
    bank = m.ps("bank", [P, 2, SPAN])
    groups = tiles // QT
    loaded = [m.sem(f"loaded{g}") for g in range(groups)]
    stats_done, mv_done, std_done, rstd_done = (m.sem(x) for x in ("stats_done", "mv_done", "std_done", "rstd_done"))
    normed, turned, high_done, low_done, eps_set = (
        m.sem(x) for x in ("normed", "turned", "high_done", "low_done", "eps_set"))
    with nc.Block() as block:
        @block.sync
        def _(sp):
            for g in range(groups):
                rows = src[g * SPAN:(g + 1) * SPAN, :].rearrange("(t p) d -> p t d", p=P)
                sp.dma_start(x[:, g * QT:(g + 1) * QT, :], rows).then_inc(loaded[g], 16)

        @block.vector
        def _(dve):
            def statistics(g):
                dve.wait_ge(loaded[g], 16)
                for t in range(g * QT, (g + 1) * QT):
                    nc.vector.bn_stats(stats[:, t, :], x[:, t, :]).then_inc(stats_done, 1)
                for t in range(g * QT, (g + 1) * QT):
                    dve.wait_ge(stats_done, t + 1)
                    nc.vector.bn_aggr(mv[:, t, :], stats[:, t, :]).then_inc(mv_done, 1)

            nc.vector.memset(eps[:, :], EPS_LN).then_inc(eps_set, 1)
            statistics(0)
            for g in range(groups):
                if g + 1 < groups:
                    statistics(g + 1)
                a, b = g * QT, (g + 1) * QT
                dve.wait_ge(std_done, g + 1)
                nc.vector.reciprocal(rstd[:, a:b], std[:, a:b]).then_inc(rstd_done, 1)
                dve.wait_ge(rstd_done, g + 1)
                for t in range(a, b + 1):
                    if t < b:
                        wait(dve, turned, t - 1)
                        nc.vector.tensor_scalar(xn[:, t % 2, :], x[:, t, :], mv[:, t, 0:1], rstd[:, t:t + 1],
                                                ALU.subtract, ALU.mult).then_inc(normed, 1)
                    if t > a:
                        u = t - 1
                        dve.wait_ge(high_done, u + 1)
                        low = xT_hl[:, 1, :, u * P:(u + 1) * P]
                        nc.vector.tensor_tensor(low, bank[:, u % 2, :].rearrange("p (k t) -> p k t", k=KT),
                                                f32(xT_hl[:, 0, :, u * P:(u + 1) * P]),
                                                ALU.subtract).then_inc(low_done, 1)
            dve.wait_ge(low_done, tiles)

        @block.scalar
        def _(act):
            act.wait_ge(eps_set, 1)

            def root(g):
                act.wait_ge(mv_done, (g + 1) * QT)
                a, b = g * QT, (g + 1) * QT
                nc.scalar.activation(std[:, a:b], mv[:, a:b, 1], ACT.Sqrt, bias=eps[:, 0:1]).then_inc(std_done, 1)

            root(0)
            for g in range(groups):
                if g + 1 < groups:
                    root(g + 1)
                for t in range(g * QT, (g + 1) * QT):
                    act.wait_ge(turned, t + 1)
                    nc.scalar.copy(xT_hl[:, 0, :, t * P:(t + 1) * P],
                                   bank[:, t % 2, :].rearrange("p (k t) -> p k t", k=KT)).then_inc(high_done, 1)

        @block.tensor
        def _(pe):
            for t in range(tiles):
                pe.wait_ge(normed, t + 1)
                wait(pe, low_done, t - 1)
                for k in range(KT):
                    last = pe.transpose(bank[:, t % 2, k * P:(k + 1) * P], xn[:, t % 2, k * P:(k + 1) * P],
                                        ident[:, :])
                last.then_inc(turned, 1)


def residual(nc, m, tiles, src, dst, y_of, attn=None):
    RING = 4
    x = m.sb("x", [P, RING, D])
    stats = m.sb("stats", [P, RING, 6])
    mv = m.sb("mv", [P, RING, 2])
    std = m.sb("std", [P, RING])
    rstd = m.sb("rstd", [P, RING])
    z = m.sb("z", [P, RING, D])
    eps = m.sb("eps", [P, 1])
    loaded = [m.sem(f"loaded{i}") for i in range(RING)]
    stored = [m.sem(f"stored{i}") for i in range(RING)]
    names = ("stats_done", "mv_done", "std_done", "rstd_done", "z_done", "sum_done", "eps_set", "o_high", "o_low", "y_full")
    stats_done, mv_done, std_done, rstd_done, z_done, sum_done, eps_set, o_high, o_low, y_full = (m.sem(n) for n in names)
    if attn:
        oT, WoT_hl = attn
        ot_hl = m.sb("ot_hl", [P, 2, 2, KT, P], F32R)
        ybank = m.ps("ybank", [P, RING, SPAN])
        y_of = lambda t: ybank[:, t % RING, :]
    with nc.Block() as block:
        @block.sync
        def _(sp):
            for t in range(tiles + 1):
                if t < tiles:
                    wait(sp, sum_done, t - RING + 1)
                    sp.dma_start(x[:, t % RING, :], src[t * P:(t + 1) * P, :]).then_inc(loaded[t % RING], 16)
                if t:
                    u = t - 1
                    sp.wait_ge(sum_done, u + 1)
                    sp.dma_start(dst[u * P:(u + 1) * P, :], z[:, u % RING, :]).then_inc(stored[u % RING], 16)
            for i in range(RING):
                sp.wait_ge(stored[i], 16 * (tiles // RING))

        if attn:
            @block.tensor
            def _(pe):
                for t in range(tiles):
                    pe.wait_ge(o_low, t + 1)
                    wait(pe, z_done, t - RING + 1)
                    steps = [(g, a, b) for g in range(KT) for a, b in THREE]
                    for n, (g, a, b) in enumerate(steps):
                        last = pe.matmul(ybank[:, t % RING, :], ot_hl[:, t % 2, a, g, :], WoT_hl[:, b, g, :],
                                         start=(n == 0), stop=(n == len(steps) - 1))
                    last.then_inc(y_full, 1)

        @block.scalar
        def _(act):
            act.wait_ge(eps_set, 1)
            for t in range(tiles + 1):
                if attn and t < tiles:
                    wait(act, y_full, t - 1)
                    nc.scalar.copy(ot_hl[:, t % 2, 0], oT(t)).then_inc(o_high, 1)
                if t:
                    u = t - 1
                    act.wait_ge(mv_done, u + 1)
                    nc.scalar.activation(std[:, u % RING:u % RING + 1], mv[:, u % RING, 1:2], ACT.Sqrt,
                                         bias=eps[:, 0:1]).then_inc(std_done, 1)

        @block.vector
        def _(dve):
            nc.vector.memset(eps[:, :], EPS_LN).then_inc(eps_set, 1)

            def low(t):
                if attn and t < tiles:
                    dve.wait_ge(o_high, t + 1)
                    nc.vector.tensor_tensor(ot_hl[:, t % 2, 1], oT(t), f32(ot_hl[:, t % 2, 0]),
                                            ALU.subtract).then_inc(o_low, 1)

            low(0)
            for t in range(tiles + 1):
                low(t + 1)
                if t < tiles:
                    r = t % RING
                    if attn:
                        dve.wait_ge(y_full, t + 1)
                    nc.vector.bn_stats(stats[:, r, :], y_of(t)).then_inc(stats_done, 1)
                    dve.wait_ge(stats_done, t + 1)
                    nc.vector.bn_aggr(mv[:, r, :], stats[:, r, :]).then_inc(mv_done, 1)
                if t:
                    u = t - 1
                    r = u % RING
                    dve.wait_ge(std_done, u + 1)
                    nc.vector.reciprocal(rstd[:, r:r + 1], std[:, r:r + 1]).then_inc(rstd_done, 1)
                    dve.wait_ge(rstd_done, u + 1)
                    wait(dve, stored[r], 16 * (u // RING))
                    nc.vector.tensor_scalar(z[:, r, :], y_of(u), mv[:, r, 0:1], rstd[:, r:r + 1],
                                            ALU.subtract, ALU.mult).then_inc(z_done, 1)

        @block.gpsimd
        def _(pool):
            for t in range(tiles):
                r = t % RING
                pool.wait_ge(z_done, t + 1)
                pool.wait_ge(loaded[r], 16 * (t // RING + 1))
                nc.gpsimd.tensor_tensor(z[:, r, :], z[:, r, :], x[:, r, :], ALU.add).then_inc(sum_done, 1)


def qkv_layer0(nc, m, batch, xT_hl, W_hl, rope, q, k, v):
    bank = m.ps("bank", [P, 2, 3, SPAN])
    direct = m.sb("direct", [P, 2, 2, D])
    crossed = m.sb("crossed", [P, 2, 2, D])
    cos, sin = rope
    full = [m.sem(f"full_{n}") for n in "qkv"]
    read = [m.sem(f"read_{n}") for n in "qkv"]
    rotated = m.sem("rotated")
    with nc.Block() as block:
        @block.tensor
        def _(pe):
            for t in range(TB):
                for w in range(3):
                    wait(pe, read[w], t - 1)
                    steps = [(c, xa, wa) for c in range(KT) for xa, wa in THREE]
                    for n, (c, xa, wa) in enumerate(steps):
                        last = pe.matmul(bank[:, t % 2, w, :], xT_hl[:, xa, c, t * P:(t + 1) * P],
                                         W_hl[:, wa, w, c, :], start=(n == 0), stop=(n == len(steps) - 1))
                    last.then_inc(full[w], 1)

        @block.vector
        def _(dve):
            for t in range(TB):
                tt = t
                for w in range(2):
                    src = bank[:, t % 2, w, :].rearrange("p (h j d) -> p h j d", h=NH, j=2)
                    dve.wait_ge(full[w], t + 1)
                    wait(dve, rotated, 2 * (t - 1) + w - 1)
                    cb = cos[:, w, tt, None, :].to_broadcast([P, 2 * NH, HALF0])
                    nc.vector.tensor_tensor(direct[:, t % 2, w, :].rearrange("p (h d) -> p h d", d=HALF0),
                                            bank[:, t % 2, w, :].rearrange("p (h d) -> p h d", d=HALF0),
                                            cb, ALU.mult)
                    dst = crossed[:, t % 2, w, :].rearrange("p (h j d) -> p h j d", h=NH, j=2)
                    for j in range(2):
                        sb = sin[:, w, tt, j, None, :].to_broadcast([P, NH, HALF0])
                        last = nc.vector.tensor_tensor(dst[:, :, j, :], src[:, :, 1 - j, :], sb, ALU.mult)
                    last.then_inc(read[w], 1)

        @block.gpsimd
        def _(pool):
            for t in range(TB):
                b, tt = batch, t
                for w, out in enumerate((q, k)):
                    pool.wait_ge(read[w], t + 1)
                    view = lambda x: x[:, t % 2, w, :].rearrange("p (g d) -> p g d", g=KT)
                    nc.gpsimd.tensor_tensor(out[:, b * KT:(b + 1) * KT, tt, :], view(direct), view(crossed),
                                            ALU.add).then_inc(rotated, 1)

        @block.scalar
        def _(act):
            for t in range(TB):
                b, tt = batch, t
                act.wait_ge(full[2], t + 1)
                nc.scalar.copy(v[:, b * KT:(b + 1) * KT, tt, :],
                               bank[:, t % 2, 2, :].rearrange("p (g d) -> p g d", g=KT)).then_inc(read[2], 1)


KINDS = "STRPGVXOY"


def unit_events(u, last_unit, latent):
    h, s = divmod(u, 2)
    more = lambda head: last_unit is None or head <= last_unit // 2
    follows = last_unit is None or u < last_unit
    nh, ns = divmod(u + 1, 2)
    scores_at = [{0: 0, 1: 1, 2: 2, 3: 3}, {1: 0, 3: 1, 4: 2, 6: 3}][s]
    ev, later = [], []
    if s == 1:
        if more(h + 2):
            ev.append(("G", h + 2, 0, 0))
        if not latent and more(h + 1):
            ev.append(("V", h + 1, 0, 0))
    for kt in range(QT * (s + 1)):
        ev.append(("T", h, s, kt))
        ev += later
        later = []
        if follows and kt in scores_at:
            ev.append(("S", nh, ns, scores_at[kt]))
            later = [("R", nh, ns, scores_at[kt])]
        if kt:
            ev.append(("P", h, s, kt - 1))
        if latent and u > 0 and kt < QT:
            ev.append(("Y", (u - 1) // 2, (u - 1) % 2, kt))
        if s == 0 and more(h + 1):
            ev.append(("X", h + 1, 0, kt))
    ev.append(("P", h, s, QT * (s + 1) - 1))
    ev += later
    ev.append(("O", h, s, 0))
    return ev


def first_events(latent):
    ev = [("G", 0, 0, 0)] + ([] if latent else [("V", 0, 0, 0)])
    ev += [("X", 0, 0, m) for m in range(QT)] + [("G", 1, 0, 0)]
    for n in range(QT):
        ev += [("S", 0, 0, n)] + ([("R", 0, 0, n - 1)] if n else [])
    return ev + [("R", 0, 0, QT - 1)] + unit_events(0, None, latent)


def last_events(units, latent):
    ev = []
    for u in range(1, units):
        ev += unit_events(u, units - 1, latent)
    if latent:
        ev += [("Y", (units - 1) // 2, 1, tt) for tt in range(QT)]
    return ev


def numbered(events, before):
    seen = dict(before)
    for kind, h, s, n in events:
        yield kind, h, s, n, dict(seen)
        seen[kind] = seen[kind] + 1


def each_turn(eng, turns, units, latent, run):
    first, body = first_events(latent), [e for u in range(1, units + 1) for e in unit_events(u, None, latent)]
    count = lambda ev, k: sum(e[0] == k for e in ev)
    start = {k: count(first, k) for k in KINDS}
    per = {k: count(body, k) for k in KINDS}
    run(numbered(first, {k: 0 for k in KINDS}), 0)
    with eng.Fori(0, turns - 1) as it:
        run(numbered(body, {k: start[k] + it * per[k] for k in KINDS}), it)
    done = turns - 1
    run(numbered(last_events(units, latent), {k: start[k] + done * per[k] for k in KINDS}), done)


def attention(nc, m, ident, ident_bf, mask, latent, src, out):
    HB = 2 if latent else 4
    units = 2 * HB
    turns = NH // HB if latent else B * NH // HB
    QW = 2 * ROPE if latent else 3 * HD0
    VW = LAT if latent else 2 * HD0
    RPT = 3
    S_AHEAD, T_AHEAD = 2, 2

    scores = m.ps("scores", [P, S_AHEAD, 2 * SPAN])
    turned = m.ps("turned", [P, T_AHEAD, SPAN])
    obank = m.ps("obank", [P, SPAN])
    xbank = m.ps("xbank", [P, SPAN])
    probs = [m.sb(f"probs{s}", [P, QT * QT * s + QT * (QT + 1) // 2, P]) for s in range(2)]
    pT_hl = m.sb("pT_hl", [P, RPT, 2, SPAN], F32R)
    row = m.sb("row", [P, 3, 4 * QT])
    q_stage = m.sb("q_stage", [P, TB, QW], F32R)
    q_stack = m.sb("q_stack", [P, 2, S], F32R)
    ones = m.sb("ones", [P, 1])
    if latent:
        qa_hl = m.sb("qa_hl", [P, 2, 2, S], F32R)
        oT_hl = m.sb("oT_hl", [P, 2, 2, SPAN], F32R)
        wabs = m.sb("wabs", [P, 2, 2, 3, LAT], F32R)
        wov = m.sb("wov", [P, 2, 2, D], F32R)
        wabs_loaded = [m.sem(f"wabs_loaded{i}") for i in range(2)]
        wov_loaded = [m.sem(f"wov_loaded{i}") for i in range(2)]
    else:
        q, k, v = src
        k_stage = m.sb("k_stage", [P, TB, QW], F32R)
        k_stack = m.sb("k_stack", [P, 2, S], F32R)
        v_stage = m.sb("v_stage", [P, 2, TB, VW], F32R)
        o_low_rows = m.sb("o_low_rows", [HD0, SPAN])

    scores_full = m.sem("scores_full")
    max_done = m.sem("max_done")
    exp_done = m.sem("exp_done")
    inverse_done = m.sem("inverse_done")
    probs_done = m.sem("probs_done")
    turned_full = m.sem("turned_full")
    turned_high = m.sem("turned_high")
    turned_low = m.sem("turned_low")
    values_done = m.sem("values_done")
    o_high = m.sem("o_high")
    o_read = m.sem("o_read")
    x_full = m.sem("x_full")
    x_high = m.sem("x_high")
    x_read = m.sem("x_read")
    y_full = m.sem("y_full")
    y_read = m.sem("y_read")
    copied = m.sem("copied")
    staged = m.sem("staged")
    q_staged = m.sem("q_staged")
    v_staged = m.sem("v_staged")
    zeroed = m.sem("zeroed")
    ones_set = m.sem("ones_set")
    passed = m.sem("passed")

    def tile_of(s, n):
        first = sum(QT * s + i + 1 for i in range(n))
        return first, QT * s + n + 1

    def ring(n, s):
        return (n + QT * s) % RPT

    head_of = lambda it, h: it * HB + h

    block = m.ctx.enter_context(nc.Block())

    if latent:
        @block.sync
        def _(sp):
            def load(h, par, ready=None):
                if ready is not None:
                    sp.wait_ge(x_full, 4 * (h - 1))
                sp.dma_start(f32(wabs[:, par]), src["wabs_dram"][bass.ds(h, 1)].rearrange("o p a k c -> p (o a) k c")
                             ).then_inc(wabs_loaded[par], 16)
                if ready is not None:
                    sp.wait_ge(y_full, 8 * (h - 1))
                sp.dma_start(f32(wov[:, par]), src["wov_dram"][bass.ds(h, 1)].rearrange("o p a c -> p (o a) c")
                             ).then_inc(wov_loaded[par], 16)
            load(0, 0)
            load(1, 1)
            with sp.Fori(1, NH // 2) as i:
                for par in range(2):
                    load(2 * i + par, par, ready=True)

    @block.tensor
    def _(pe):
        pe.sem_inc(values_done, RPT)

        def run(events, it):
            for kind, h, s, n, seen in events:
                hp = h % 2
                if kind == "X":
                    pe.wait_ge(x_read, seen["X"] + 1)
                    if latent:
                        pe.wait_ge(y_read, seen["Y"] + 1)
                    if latent and n < 2:
                        if n == 0:
                            pe.wait_ge(wabs_loaded[hp], 16 * (it * (HB // 2) + h // 2 + 1))
                        steps = [(j, a, b) for j in range(3) for a, b in THREE]
                        for i, (j, a, b) in enumerate(steps):
                            last = pe.matmul(xbank[:, :], wabs[:, hp, a, j, :],
                                             src["qT_hl"][:, b, j, n * SPAN:(n + 1) * SPAN],
                                             start=(i == 0), stop=(i == len(steps) - 1))
                    else:
                        if n == (2 if latent else 0):
                            pe.wait_ge(staged, head_of(it, h) + 1)
                            if not latent:
                                pe.wait_ge(q_staged, head_of(it, h) + 1)
                        stage = q_stage if latent or n % 2 == 0 else k_stage
                        for i in range(QT):
                            t = (n % 2 if latent else n // 2) * QT + i
                            last = pe.transpose(xbank[0:QW, i * P:(i + 1) * P], f32(stage[:, t, :]), ident[:, :])
                    last.then_inc(x_full, 1)
                elif kind == "S":
                    pe.wait_ge(x_read, 4 * (head_of(it, h) + 1) + 1)
                    pe.wait_ge(exp_done, seen["S"] + 1)
                    t = QT * s + n
                    buf = n % S_AHEAD
                    for c in range(0, (t + 1) * P, SPAN):
                        cols = slice(c, min(c + SPAN, (t + 1) * P))
                        rows = slice(t * P, (t + 1) * P)
                        if latent:
                            steps = [(qa_hl[:, hp, a, rows], src["kT_hl"][:, b, cols]) for a, b in THREE]
                            steps += [(q_stack[:, hp, rows], src["kpe"][:, part, cols]) for part in range(2)]
                        else:
                            steps = [(q_stack[0:QW, hp, rows], k_stack[0:QW, hp, cols])]
                        diagonal = cols.stop == (t + 1) * P
                        for i, (lhs, rhs) in enumerate(steps):
                            last = pe.matmul(scores[:, buf, cols], lhs, rhs, start=(i == 0),
                                             stop=(not diagonal and i == len(steps) - 1))
                        if diagonal:
                            last = pe.matmul(scores[:, buf, t * P:(t + 1) * P], ident_bf[:, :], mask[:, :],
                                             start=False, stop=True)
                    last.then_inc(scores_full, 1)
                elif kind == "T":
                    if n == 0:
                        if latent:
                            pe.wait_ge(exp_done, seen["O"] * QT + QT + S_AHEAD)
                        else:
                            pe.wait_ge(probs_done, seen["O"] * QT + QT)
                    pe.wait_ge(turned_low, seen["T"] + 1)
                    for i in range(max(0, n - QT * s), QT):
                        first, _ = tile_of(s, i)
                        last = pe.transpose(turned[:, n % T_AHEAD, i * P:(i + 1) * P],
                                            probs[s][:, first + n, :], ident[:, :])
                    last.then_inc(turned_full, 1)
                elif kind == "P":
                    if n == 0:
                        pe.wait_ge(o_read, seen["O"] + 1)
                        if not latent:
                            pe.wait_ge(v_staged, head_of(it, h) + 1)
                    pe.wait_ge(turned_low, seen["P"] + 1 + T_AHEAD)
                    c = max(0, n - QT * s) * P
                    r = ring(n, s)
                    if latent:
                        steps = [(src["v_hl"][:, a, n, :], pT_hl[:, r, b, c:SPAN]) for a, b in THREE]
                    else:
                        steps = [(v_stage[:, hp, n, :], pT_hl[:, r, b, c:SPAN]) for b in range(2)]
                    for i, (lhs, rhs) in enumerate(steps):
                        last = pe.matmul(obank[0:VW, c:SPAN], lhs, rhs, start=(n == 0 and i == 0),
                                         stop=(n == QT * (s + 1) - 1 and i == len(steps) - 1))
                    last.then_inc(values_done, 1)
                elif kind == "Y":
                    pe.wait_ge(o_read, seen["O"] + 1)
                    pe.wait_ge(x_read, seen["X"] + 1)
                    pe.wait_ge(y_read, seen["Y"] + 1)
                    if s == 0 and n == 0:
                        pe.wait_ge(wov_loaded[hp], 16 * (it * (HB // 2) + h // 2 + 1))
                    for i, (a, b) in enumerate(THREE):
                        last = pe.matmul(xbank[:, :], oT_hl[:, s, a, n * P:(n + 1) * P], wov[:, hp, b, :],
                                         start=(i == 0), stop=(i == 2))
                    last.then_inc(y_full, 1)

        each_turn(pe, turns, units, latent, run)

    @block.scalar
    def _(act):
        act.sem_inc(exp_done, S_AHEAD)
        if not latent:
            act.sem_inc(x_read, 1)

        def run(events, it):
            for kind, h, s, n, seen in events:
                hp = h % 2
                if kind == "S":
                    first, wide = tile_of(s, n)
                    slot = (hp * 2 + s) * QT + n
                    act.wait_ge(max_done, seen["S"] + 1)
                    nc.scalar.activation(probs[s][:, first:first + wide, :].rearrange("p k c -> p (k c)"),
                                         scores[:, n % S_AHEAD, 0:wide * P], ACT.Exp, bias=row[:, 0, slot:slot + 1],
                                         accum_out=row[:, 1, slot:slot + 1]).then_inc(exp_done, 1)
                elif kind == "T":
                    c = max(0, n - QT * s) * P
                    act.wait_ge(turned_full, seen["T"] + 1)
                    act.wait_ge(values_done, seen["T"] + 1)
                    nc.scalar.copy(pT_hl[:, ring(n, s), 0, c:SPAN],
                                   turned[:, n % T_AHEAD, c:SPAN]).then_inc(turned_high, 1)
                elif kind == "X" and not latent and n % 2 == 0:
                    act.wait_ge(x_full, seen["X"] + 1)
                    nc.scalar.copy(q_stack[0:QW, hp, n // 2 * SPAN:(n // 2 + 1) * SPAN],
                                   xbank[0:QW, :]).then_inc(x_read, 1)
                elif kind == "X" and latent and n < 3:
                    act.wait_ge(x_full, seen["X"] + 1)
                    if n < 2:
                        nc.scalar.copy(qa_hl[:, hp, 0, n * SPAN:(n + 1) * SPAN], xbank[:, :]).then_inc(x_high, 1)
                    else:
                        nc.scalar.copy(q_stack[:, hp, 0:SPAN], xbank[:, :]).then_inc(x_read, 1)
                elif kind == "O":
                    act.wait_ge(values_done, seen["P"] + RPT)
                    if latent:
                        wait(act, y_full, seen["Y"])
                        nc.scalar.copy(oT_hl[:, s, 0, :], obank[:, :]).then_inc(o_high, 1)
                    else:
                        act.wait_ge(o_read, seen["O"] + 1)
                        nc.scalar.copy(o_low_rows[:, :], obank[HD0:2 * HD0, :]).then_inc(o_high, 1)

        each_turn(act, turns, units, latent, run)

    @block.vector
    def _(dve):
        dve.sem_inc(turned_low, T_AHEAD)
        dve.sem_inc(o_read, 1)
        if latent:
            dve.sem_inc(x_read, 1)
            dve.sem_inc(y_read, 1)
            nc.vector.memset(out[:, :, :], 0.0).then_inc(zeroed, 1)
            dve.wait_ge(zeroed, 1)

        def run(events, it):
            for kind, h, s, n, seen in events:
                hp = h % 2
                if kind == "S":
                    _, wide = tile_of(s, n)
                    slot = (hp * 2 + s) * QT + n
                    dve.wait_ge(scores_full, seen["S"] + 1)
                    nc.vector.tensor_reduce(row[:, 0, slot:slot + 1], scores[:, n % S_AHEAD, 0:wide * P],
                                            AX.X, ALU.max, negate=True).then_inc(max_done, 1)
                elif kind == "R":
                    slot = (hp * 2 + s) * QT + n
                    dve.wait_ge(exp_done, seen["R"] + 1 + S_AHEAD)
                    nc.vector.reciprocal(row[:, 2, slot:slot + 1], row[:, 1, slot:slot + 1]).then_inc(inverse_done, 1)
                elif kind == "T":
                    c = max(0, n - QT * s) * P
                    r = ring(n, s)
                    dve.wait_ge(turned_high, seen["T"] + 1)
                    nc.vector.tensor_tensor(pT_hl[:, r, 1, c:SPAN], turned[:, n % T_AHEAD, c:SPAN],
                                            f32(pT_hl[:, r, 0, c:SPAN]), ALU.subtract).then_inc(turned_low, 1)
                elif kind == "X" and not latent and n % 2:
                    dve.wait_ge(x_full, seen["X"] + 1)
                    nc.vector.tensor_copy(k_stack[0:QW, hp, n // 2 * SPAN:(n // 2 + 1) * SPAN],
                                          xbank[0:QW, :]).then_inc(x_read, 1)
                elif kind == "X" and latent and n != 2:
                    if n < 2:
                        cols = slice(n * SPAN, (n + 1) * SPAN)
                        dve.wait_ge(x_high, 2 * head_of(it, h) + n + 1)
                        nc.vector.tensor_tensor(qa_hl[:, hp, 1, cols], xbank[:, :], f32(qa_hl[:, hp, 0, cols]),
                                                ALU.subtract).then_inc(x_read, 1)
                    else:
                        dve.wait_ge(x_full, seen["X"] + 1)
                        nc.vector.tensor_copy(q_stack[:, hp, SPAN:S], xbank[:, :]).then_inc(x_read, 1)
                elif kind == "Y":
                    dve.wait_ge(y_full, seen["Y"] + 1)
                    t = QT * s + n
                    slot = (hp * 2 + s) * QT + n
                    dve.wait_ge(inverse_done, seen["Y"] + 1)
                    nc.vector.scalar_tensor_tensor(out=out[:, t, :], in0=xbank[:, :], scalar=row[:, 2, slot:slot + 1],
                                                   in1=out[:, t, :], op0=ALU.mult, op1=ALU.add).then_inc(y_read, 1)
                elif kind == "O":
                    dve.wait_ge(o_high, seen["O"] + 1)
                    if latent:
                        nc.vector.tensor_tensor(oT_hl[:, s, 1, :], obank[:, :], f32(oT_hl[:, s, 0, :]),
                                                ALU.subtract).then_inc(o_read, 1)
                    else:
                        j = h % HB
                        g = it + h // HB
                        dst = out[j * HD0:(j + 1) * HD0, bass.ds(g, 1), s * SPAN:(s + 1) * SPAN]
                        nc.vector.tensor_tensor(dst.rearrange("p o t -> p (o t)"), obank[0:HD0, :], o_low_rows[:, :],
                                                ALU.add).then_inc(o_read, 1)

        each_turn(dve, turns, units, latent, run)
        if latent:
            dve.wait_ge(y_read, 4 * 2 * NH + 1)
        else:
            dve.wait_ge(o_read, 2 * B * NH + 1)

    @block.gpsimd
    def _(pool):
        nc.gpsimd.memset(ones[:, :], 1.0).then_inc(ones_set, 1)
        pool.wait_ge(ones_set, 1)

        def pool_wait(sem, value):
            wait(pool, sem, value)
            pool.sem_inc(passed, 1)

        def split(dst, x, repeat, low_at, count):
            w = x.shape[-1]
            blocks = {1: [0], 2: [0, 1], 3: [0, 2]}[repeat]
            for i in blocks:
                nc.gpsimd.tensor_tensor(dst[:, :, i * w:(i + 1) * w], x, ones[:, :, None].to_broadcast([P, TB, w]),
                                        ALU.mult).then_inc(copied, 1)
            pool_wait(copied, count + len(blocks))
            return nc.gpsimd.tensor_tensor(dst[:, :, low_at * w:(low_at + 1) * w], x, f32(dst[:, :, 0:w]), ALU.subtract)

        def run(events, it):
            for kind, h, s, n, seen in events:
                hp = h % 2
                if kind == "G":
                    pool_wait(x_full, 4 * head_of(it, h))
                    if latent:
                        x = src["qpe"][:, :, bass.ds(head_of(it, h) * ROPE, ROPE)]
                        split(q_stage[:, :, :], x, 1, 1, seen["G"]).then_inc(staged, 1)
                    else:
                        j, g = h % HB, it + h // HB
                        cols = slice(j * HD0, (j + 1) * HD0)
                        count = seen["G"] * 4 + seen["V"]
                        x = q[:, bass.ds(g, 1), :, cols].rearrange("p o t c -> p (o t) c")
                        split(q_stage[:, :, :], x, 3, 1, count).then_inc(q_staged, 1)
                        x = k[:, bass.ds(g, 1), :, cols].rearrange("p o t c -> p (o t) c")
                        split(k_stage[:, :, :], x, 2, 2, count + 2).then_inc(staged, 1)
                elif kind == "V":
                    pool_wait(values_done, 12 * (head_of(it, h) - 1) + RPT)
                    j, g = h % HB, it + h // HB
                    x = v[:, bass.ds(g, 1), :, j * HD0:(j + 1) * HD0].rearrange("p o t c -> p (o t) c")
                    split(v_stage[:, hp], x, 1, 1, seen["G"] * 4 + seen["V"]).then_inc(v_staged, 1)
                elif kind == "R" and not latent:
                    first, wide = tile_of(s, n)
                    slot = (hp * 2 + s) * QT + n
                    pool_wait(inverse_done, seen["R"] + 1)
                    rows = probs[s][:, first:first + wide, :].rearrange("p k c -> p (k c)")
                    nc.gpsimd.tensor_scalar(rows, rows, row[:, 2, slot:slot + 1], 1.0, ALU.mult, ALU.mult
                                            ).then_inc(probs_done, 1)

        each_turn(pool, turns, units, latent, run)


HT = HG // P
SPANS = NT // QT
WBANKS = 3 * HT


def group_events(half, turn_next, quantise_after):
    ev = []
    banks = iter([("W", half, i, 0) for i in range(WBANKS)] if turn_next else [])
    for sp in range(SPANS):
        for ht in range(HT):
            ev.append(("H", half, sp, ht))
            if sp >= 1:
                ev += [e for e in [next(banks, None)] if e]
            if quantise_after and sp < 3:
                ev.append(("AL"[ht], half, sp, 0))
        if sp >= 1:
            ev += [("D", half, sp - 1, t) for t in range(QT)]
    return ev + [("D", half, SPANS - 1, t) for t in range(QT)]


def each_group(eng, ternary, run):
    kinds = "HDWAL"
    quantised = lambda half: [(k, half, i, 0) for i in range(3) for k in "AL"] if ternary else []
    first = quantised(0) + [("W", 1, i, 0) for i in range(WBANKS)] + quantised(1)
    body = group_events(0, True, ternary) + group_events(1, True, ternary)
    tail = group_events(0, True, False) + group_events(1, False, False)
    start = {k: sum(e[0] == k for e in first) for k in kinds}
    per = {k: sum(e[0] == k for e in body) for k in kinds}
    run(numbered(first, {k: 0 for k in kinds}), None)
    with eng.Fori(0, NG // 2 - 1) as it:
        run(numbered(body, {k: start[k] + it * per[k] for k in kinds}), it)
    done = NG // 2 - 1
    run(numbered(tail, {k: start[k] + done * per[k] for k in kinds}), done)


def feed_forward(nc, m, ident, xT_hl, acc, gate, up, down, ternary=None):
    PARTS = 1 if ternary is not None else 2
    pairs = [(0, 0), (1, 0)] if ternary is not None else [(0, 0), (1, 0), (0, 1)]
    WC = KT * HG
    raw = m.sb("raw", [P, 2, 3, WC])
    wT = m.sb("wT", [P, 2, PARTS, 3, WC], F32R)
    silu = m.sb("silu", [P, HT, SPAN])
    hid = m.sb("hid", [P, HT, SPAN])
    h_hl = m.sb("h_hl", [P, 2, HT, 2, SPAN], F32R)
    gbank = m.ps("gbank", [P, HT, SPAN])
    ubank = m.ps("ubank", [P, HT, SPAN])
    ybank = m.ps("ybank", [P, 2, SPAN])
    if ternary is None:
        wbank, turned_src, turn_ident = m.ps("wbank", [P, 2, SPAN]), raw, ident
    else:
        ident_bf, squares = ternary
        NGR = WC // GROUP
        wbank = m.ps("wbank", [P, 2, 2 * SPAN], BF16)
        quant = m.sb("quant", [P, 2, 3, WC], BF16)
        wb = m.sb("wb", [P, WC], BF16)
        ratio = m.sb("ratio", [P, WC], BF16)
        lower = m.sb("lower", [P, WC], BF16)
        level = m.sb("level", [P, WC], BF16)
        diff = m.sb("diff", [P, WC], BF16)
        total = m.sb("total", [P, NGR])
        mean = m.sb("mean", [P, NGR], BF16)
        scale = m.sb("scale", [P, NGR], BF16)
        inverse = m.sb("inverse", [P, NGR])
        sq = m.sb("sq", [P, SPAN])
        turned_src, turn_ident = quant, ident_bf
    loaded = [m.sem(f"loaded{i}") for i in range(2)]
    zeroed = m.sem("zeroed")
    w_full = m.sem("w_full")
    w_high = m.sem("w_high")
    w_read = m.sem("w_read")
    g_full, u_full = m.sem("g_full"), m.sem("u_full")
    silu_done = m.sem("silu_done")
    hid_done = m.sem("hid_done")
    h_high = m.sem("h_high")
    h_low = m.sem("h_low")
    y_full = m.sem("y_full")
    y_read = m.sem("y_read")
    squared, sq_added = m.sem("squared"), m.sem("sq_added")
    cast_done = m.sem("cast_done")
    q_step = m.sem("q_step")
    inverse_done = m.sem("inverse_done")
    ratio_done = m.sem("ratio_done")
    lower_done, level_done = m.sem("lower_done"), m.sem("level_done")
    l_step = m.sem("l_step")
    quant_done = m.sem("quant_done")

    def blocks(half, i):
        w, sub = divmod(i, HT)
        if w < 2:
            tile = turned_src[:, half, w, :].rearrange("p (h d) -> p h d", h=HT)
            return [tile[:, sub, c * P:(c + 1) * P] for c in range(KT)]
        tile = turned_src[:, half, 2, :].rearrange("p (o c) -> p o c", o=KT)
        return [tile[:, o, sub * P:(sub + 1) * P] for o in range(KT)]

    def turned_to(half, part, i):
        w, sub = divmod(i, HT)
        if w < 2:
            return wT[:, half, part, w, :].rearrange("p (c h) -> p c h", c=KT)[:, :, sub * P:(sub + 1) * P]
        return wT[:, half, part, 2, sub * D:(sub + 1) * D].rearrange("p (c h) -> p c h", c=KT)

    def bank_view(i):
        return wbank[:, i % 2, 0:SPAN].rearrange("p (c h) -> p c h", c=KT)

    block = m.ctx.enter_context(nc.Block())

    @block.sync
    def _(sp):
        def load(g, half, again):
            if again and ternary is None:
                sp.wait_ge(w_full, WBANKS * (g - 1))
            elif again:
                sp.wait_ge(cast_done, 3 * (g - 1))
            for w, src in ((0, gate), (1, up)):
                sp.dma_start(raw[:, half, w, :].rearrange("p (h d) -> p h d", h=HT),
                             src[bass.ds(g * HG, HG), :].rearrange("(h p) d -> p h d", p=P)
                             ).then_inc(loaded[half], 16)
            sp.dma_start(raw[:, half, 2, :].rearrange("p (o c) -> p o c", o=KT),
                         down[:, bass.ds(g * HG, HG)].rearrange("(o p) c -> p o c", p=P)
                         ).then_inc(loaded[half], 16)
        load(0, 0, False)
        load(1, 1, False)
        with sp.Fori(1, NG // 2) as i:
            for half in range(2):
                load(2 * i + half, half, True)

    def load_count(it, half):
        return 48 if it is None else 48 * (it + 1 + half)

    @block.tensor
    def _(pe):
        pe.sem_inc(y_full, 1)

        def run(events, it):
            for kind, half, a, b, seen in events:
                if kind == "W":
                    to = 1 - half
                    if a == 0 and ternary is None:
                        pe.wait_ge(loaded[to], load_count(it, half))
                    elif a == 0:
                        pe.wait_ge(quant_done, 4 if it is None else 3 * (2 * it + half + 2) + 1)
                    pe.wait_ge(w_read, seen["W"] + 1)
                    for c, blk in enumerate(blocks(to, a)):
                        last = pe.transpose(wbank[:, a % 2, c * P:(c + 1) * P], blk, turn_ident[:, :])
                    last.then_inc(w_full, 1)
                elif kind == "H":
                    if a == 0 and b == 0:
                        pe.wait_ge(w_read, seen["W"] + 2)
                    pe.wait_ge(hid_done, seen["H"] + 1)
                    for bank, w, full in ((gbank, 0, g_full), (ubank, 1, u_full)):
                        steps = [(c, xa, wa) for c in range(KT) for xa, wa in pairs]
                        for n, (c, xa, wa) in enumerate(steps):
                            last = pe.matmul(bank[:, b, :], wT[:, half, wa, w, c * HG + b * P:c * HG + (b + 1) * P],
                                             xT_hl[:, xa, c, a * SPAN:(a + 1) * SPAN], start=(n == 0),
                                             stop=(n == len(steps) - 1))
                        last.then_inc(full, 1)
                elif kind == "D":
                    if b == 0:
                        pe.wait_ge(h_low, seen["H"] + (HT if a == SPANS - 1 else 0))
                    pe.wait_ge(y_read, seen["D"] + 1)
                    steps = [(ht, ha, wa) for ht in range(HT) for ha, wa in pairs]
                    for n, (ht, ha, wa) in enumerate(steps):
                        last = pe.matmul(ybank[:, b % 2, :], h_hl[:, a % 2, ht, ha, b * P:(b + 1) * P],
                                         wT[:, half, wa, 2, ht * D:(ht + 1) * D],
                                         start=(n == 0), stop=(n == len(steps) - 1))
                    last.then_inc(y_full, 1)

        each_group(pe, ternary is not None, run)

    @block.scalar
    def _(act):
        if ternary is not None:
            act.sem_inc(w_read, 2)

        def run(events, it):
            for kind, half, a, b, seen in events:
                if kind == "W":
                    act.wait_ge(w_full, seen["W"] + 1)
                    nc.scalar.copy(turned_to(1 - half, 0, a), bank_view(a)
                                   ).then_inc(w_high if ternary is None else w_read, 1)
                elif kind == "H":
                    act.wait_ge(g_full, seen["H"] + 1)
                    nc.scalar.activation(silu[:, b, :], gbank[:, b, :], ACT.Silu).then_inc(silu_done, 1)
                    act.wait_ge(hid_done, seen["H"] + 1 + HT)
                    act.wait_ge(y_full, seen["D"] + 1)
                    nc.scalar.copy(h_hl[:, a % 2, b, 0, :], hid[:, b, :]).then_inc(h_high, 1)
                elif kind == "A":
                    act.wait_ge(loaded[half], 48 if it is None else 48 * (it + 2))
                    act.wait_ge(quant_done, seen["A"] + 1)
                    nc.scalar.copy(wb[:, :], raw[:, half, a, :]).then_inc(cast_done, 1)

        each_group(act, ternary is not None, run)

    @block.vector
    def _(dve):
        if ternary is None:
            dve.sem_inc(w_read, 2)
        dve.sem_inc(hid_done, HT)
        dve.sem_inc(y_read, 2)
        dve.wait_ge(zeroed, 1)

        def run(events, it):
            for kind, half, a, b, seen in events:
                if kind == "W" and ternary is None:
                    dve.wait_ge(w_high, seen["W"] + 1)
                    nc.vector.tensor_tensor(turned_to(1 - half, 1, a), bank_view(a), f32(turned_to(1 - half, 0, a)),
                                            ALU.subtract).then_inc(w_read, 1)
                elif kind == "H":
                    dve.wait_ge(silu_done, seen["H"] + 1)
                    dve.wait_ge(u_full, seen["H"] + 1)
                    dve.wait_ge(h_low, seen["H"] + 1)
                    nc.vector.tensor_tensor(hid[:, b, :], silu[:, b, :], ubank[:, b, :], ALU.mult
                                            ).then_inc(hid_done, 1)
                elif kind == "D":
                    dve.wait_ge(y_full, seen["D"] + 1 + 1)
                    y = acc[:, a * QT + b, :]
                    nc.vector.tensor_tensor(y, y, ybank[:, b % 2, :], ALU.add).then_inc(y_read, 1)
                elif kind == "A":
                    dve.wait_ge(cast_done, seen["A"] + 1)
                    nc.vector.tensor_reduce(total[:, :], wb[:, :].rearrange("p (n g) -> p n g", g=GROUP), AX.X,
                                            ALU.add, apply_absolute_value=True).then_inc(q_step, 1)
                    dve.wait_ge(q_step, 3 * seen["A"] + 1)
                    nc.vector.tensor_scalar(mean[:, :], total[:, :], 1.0 / GROUP, None, ALU.mult).then_inc(q_step, 1)
                    dve.wait_ge(q_step, 3 * seen["A"] + 2)
                    nc.vector.tensor_scalar(scale[:, :], mean[:, :], 1e-8, None, ALU.max).then_inc(q_step, 1)
                    dve.wait_ge(q_step, 3 * seen["A"] + 3)
                    nc.vector.reciprocal(inverse[:, :], scale[:, :]).then_inc(inverse_done, 1)
                elif kind == "L":
                    dve.wait_ge(ratio_done, seen["L"] + 1)
                    nc.vector.tensor_scalar(lower[:, :], ratio[:, :], -0.5, None, ALU.is_lt).then_inc(lower_done, 1)
                    dve.wait_ge(lower_done, seen["L"] + 1)
                    nc.vector.scalar_tensor_tensor(out=level[:, :], in0=ratio[:, :], scalar=0.5, in1=lower[:, :],
                                                   op0=ALU.is_gt, op1=ALU.subtract).then_inc(level_done, 1)

        each_group(dve, ternary is not None, run)
        dve.wait_ge(y_read, NG * NT + 2)

    @block.gpsimd
    def _(pool):
        pool.sem_inc(h_low, HT)
        if ternary is not None:
            pool.sem_inc(quant_done, 1)
            pool.sem_inc(sq_added, 1)
            nc.gpsimd.memset(squares[:, :], 0.0).then_inc(squared, 1)
            pool.wait_ge(squared, 1)
        nc.gpsimd.memset(acc[:, :, :], 0.0).then_inc(zeroed, 1)

        def run(events, it):
            for kind, half, a, b, seen in events:
                if kind == "H":
                    if ternary is not None:
                        pool.wait_ge(hid_done, seen["H"] + 1 + HT)
                        pool.wait_ge(sq_added, seen["H"] + 1)
                        nc.gpsimd.tensor_tensor(sq[:, :], hid[:, b, :], hid[:, b, :], ALU.mult).then_inc(squared, 1)
                        pool.wait_ge(squared, seen["H"] + 2)
                        tok = slice(a * SPAN, (a + 1) * SPAN)
                        nc.gpsimd.tensor_tensor(squares[:, tok], squares[:, tok], sq[:, :], ALU.add
                                                ).then_inc(sq_added, 1)
                    pool.wait_ge(h_high, seen["H"] + 1)
                    nc.gpsimd.tensor_tensor(h_hl[:, a % 2, b, 1, :], hid[:, b, :], f32(h_hl[:, a % 2, b, 0, :]),
                                            ALU.subtract).then_inc(h_low, 1)
                elif kind == "A":
                    pool.wait_ge(inverse_done, seen["A"] + 1)
                    view = lambda x: x[:, :].rearrange("p (n g) -> p n g", g=GROUP)
                    nc.gpsimd.tensor_tensor(view(ratio), view(wb), inverse[:, :, None].to_broadcast([P, NGR, GROUP]),
                                            ALU.mult).then_inc(ratio_done, 1)
                elif kind == "L":
                    pool.wait_ge(level_done, seen["L"] + 1)
                    view = lambda x: x[:, :].rearrange("p (n g) -> p n g", g=GROUP)
                    nc.gpsimd.tensor_tensor(view(ratio), view(level), scale[:, :, None].to_broadcast([P, NGR, GROUP]),
                                            ALU.mult).then_inc(l_step, 1)
                    pool.wait_ge(l_step, 2 * seen["L"] + 1)
                    nc.gpsimd.tensor_tensor(diff[:, :], ratio[:, :], wb[:, :], ALU.subtract).then_inc(l_step, 1)
                    pool.wait_ge(l_step, 2 * seen["L"] + 2)
                    if it is not None:
                        pool.wait_ge(w_full, WBANKS * (2 * it + half + 1))
                    nc.gpsimd.tensor_tensor(quant[:, half, a, :], wb[:, :], diff[:, :], ALU.add
                                            ).then_inc(quant_done, 1)

        each_group(pool, ternary is not None, run)


def scale_rows(nc, m, squares, acc):
    ones = m.sb("ones", [P, 1])
    eps = m.sb("eps", [P, 1])
    root = m.sb("root", [P, NT])
    inv = m.sb("inv", [P, NT])
    bank = m.ps("bank", [P, NT])
    ready, summed, rooted, inverted, scaled = (m.sem(x) for x in ("ready", "summed", "rooted", "inverted", "scaled"))
    with nc.Block() as block:
        @block.vector
        def _(dve):
            nc.vector.memset(ones[:, :], 1.0).then_inc(ready, 1)
            nc.vector.memset(eps[:, :], EPS_F32).then_inc(ready, 1)
            dve.wait_ge(rooted, 1)
            nc.vector.reciprocal(inv[:, :], root[:, :]).then_inc(inverted, 1)
            dve.wait_ge(inverted, 1)
            for t in range(NT):
                nc.vector.tensor_scalar(acc[:, t, :], acc[:, t, :], inv[:, t:t + 1], None, ALU.mult).then_inc(scaled, 1)
            dve.wait_ge(scaled, NT)

        @block.tensor
        def _(pe):
            pe.wait_ge(ready, 2)
            for t in range(NT):
                last = pe.matmul(bank[:, t:t + 1], squares[:, t * P:(t + 1) * P], ones[:, :], start=True, stop=True)
            last.then_inc(summed, 1)

        @block.scalar
        def _(act):
            act.wait_ge(ready, 2)
            act.wait_ge(summed, 1)
            nc.scalar.activation(root[:, :], bank[:, :], ACT.Sqrt, bias=eps[:, 0:1], scale=1.0 / HID).then_inc(rooted, 1)


def absorbed_weights(nc, m, q_nope, k_b, v_b, owT, wabs_dram, wov_dram):
    wabs = m.sb("wabs", [P, 2, 2, 3, LAT], F32R)
    wov = m.sb("wov", [P, 2, 2, D], F32R)
    abank = m.ps("abank", [P, 2, SPAN])
    vbank = m.ps("vbank", [P, 2, SPAN])
    full, high, low = m.sem("full"), m.sem("high"), m.sem("low")
    stored = [m.sem(f"stored{i}") for i in range(2)]
    with nc.Block() as block:
        @block.tensor
        def _(pe):
            for h in range(NH):
                wait(pe, low, 2 * (h - 1))
                for j in range(3):
                    last = pe.matmul(abank[:, h % 2, j * P:(j + 1) * P], q_nope[:, h, j * P:(j + 1) * P],
                                     k_b[:, h, :], start=True, stop=True)
                last.then_inc(full, 1)
                pe.matmul(vbank[:, h % 2, :], v_b[:, h, :], owT[:, h, :], start=True, stop=True).then_inc(full, 1)

        def pieces(h):
            par = h % 2
            yield 2 * h, SCALE1, abank[:, par, 0:3 * P].rearrange("p (j c) -> p j c", j=3), wabs[:, par, 0], wabs[:, par, 1]
            yield 2 * h + 1, 1.0, vbank[:, par, :], wov[:, par, 0], wov[:, par, 1]

        @block.scalar
        def _(act):
            for h in range(NH):
                wait(act, stored[h % 2], 32 * (h // 2))
                for n, scale, src, hi, lo in pieces(h):
                    act.wait_ge(full, n + 1)
                    nc.scalar.activation(hi, src, ACT.Copy, scale=scale).then_inc(high, 1)

        @block.vector
        def _(dve):
            for h in range(NH):
                for n, scale, src, hi, lo in pieces(h):
                    dve.wait_ge(high, n + 1)
                    nc.vector.scalar_tensor_tensor(out=lo, in0=src, scalar=scale, in1=f32(hi), op0=ALU.mult,
                                                   op1=ALU.subtract).then_inc(low, 1)

        @block.sync
        def _(sp):
            for h in range(NH):
                par = h % 2
                sp.wait_ge(low, 2 * h + 2)
                sp.dma_start(wabs_dram[h], f32(wabs[:, par])).then_inc(stored[par], 16)
                sp.dma_start(wov_dram[h], f32(wov[:, par])).then_inc(stored[par], 16)
            for par in range(2):
                sp.wait_ge(stored[par], 32 * NH // 2)


def store_all(nc, m, pairs):
    stored = m.sem("stored")
    with nc.Block() as block:
        @block.sync
        def _(sp):
            for dst, src in pairs:
                sp.dma_start(dst, src).then_inc(stored, 16)
            sp.wait_ge(stored, 16 * len(pairs))


def latent_operands(nc, m, ident, xT_hl, weights, norms, rope, out):
    WA = QL + LAT + ROPE
    HW = WA // 2
    waT = m.sb("waT", [P, 2, KT, WA], F32R)
    wpT = m.sb("wpT", [P, 2, 3, NH * ROPE], F32R)
    norm_w = m.sb("norm_w", [P, QL + LAT])
    down = m.sb("down", [P, 2, WA])
    squares = m.sb("squares", [P, QL])
    sums = m.sb("sums", [P, 2, 2])
    root = m.sb("root", [P, 2, 2])
    inv = m.sb("inv", [P, 2, 2])
    eps = m.sb("eps", [P, 1])
    normed = m.sb("normed", [P, 2, QL + LAT])
    k_parts = m.sb("k_parts", [P, 2, 3, ROPE])
    k_stage = m.sb("k_stage", [P, 2, 2, 2 * ROPE], F32R)
    direct = m.sb("direct", [P, NH * ROPE])
    crossed = m.sb("crossed", [P, NH * ROPE])
    dbank = m.ps("dbank", [P, 2, 2, SPAN])
    tbank = m.ps("tbank", [P, SPAN])
    kbank = m.ps("kbank", [P, 2 * P])
    pbank = m.ps("pbank", [P, 2, SPAN])
    cos, sin = rope
    names = ("w_loaded", "eps_set", "d_full", "d_read", "sq_done", "root_done", "inv_done", "norm_done", "k_mul",
             "k_sum", "k_high", "k_staged", "v_high", "v_low", "t_full", "t_high", "t_low", "k_full", "k_read",
             "p_full", "p_read", "p_sum")
    (w_loaded, eps_set, d_full, d_read, sq_done, root_done, inv_done, norm_done, k_mul, k_sum, k_high, k_staged,
     v_high, v_low, t_full, t_high, t_low, k_full, k_read, p_full, p_read, p_sum) = (m.sem(n) for n in names)
    qT_hl, kT_hl, kpe, v_hl, qpe = (out[n] for n in ("qT_hl", "kT_hl", "kpe", "v_hl", "qpe"))
    with nc.Block() as block:
        @block.sync
        def _(sp):
            sp.dma_start(f32(waT[:, :, :, :]), weights[0]).then_inc(w_loaded, 16)
            sp.dma_start(f32(wpT[:, :, :, :]), weights[1]).then_inc(w_loaded, 16)
            for dst, src in ((norm_w[:, 0:QL], norms[0]), (norm_w[:, QL:QL + LAT], norms[1])):
                sp.dma_start(dst, src.partition_broadcast(P)).then_inc(w_loaded, 16)

        @block.tensor
        def _(pe):
            pe.wait_ge(w_loaded, 64)
            for i in range(TB + 2):
                if i < TB:
                    t = i
                    wait(pe, d_read, t - 1)
                    for half in range(2):
                        steps = [(c, a, b) for c in range(KT) for a, b in THREE]
                        for n, (c, a, b) in enumerate(steps):
                            last = pe.matmul(dbank[:, t % 2, half, 0:HW], xT_hl[:, a, c, t * P:(t + 1) * P],
                                             waT[:, b, c, half * HW:(half + 1) * HW],
                                             start=(n == 0), stop=(n == len(steps) - 1))
                    last.then_inc(d_full, 1)
                if 0 <= i - 1 < TB:
                    t = i - 1
                    pe.wait_ge(norm_done, 2 * t + 2)
                    wait(pe, t_low, 2 * t)
                    for c in range(4):
                        last = pe.transpose(tbank[:, c * P:(c + 1) * P], normed[:, t % 2, c * P:(c + 1) * P], ident[:, :])
                    last.then_inc(t_full, 1)
                    pe.wait_ge(k_staged, t + 1)
                    wait(pe, k_read, t)
                    for part in range(2):
                        last = pe.transpose(kbank[:, part * P:(part + 1) * P], f32(k_stage[:, t % 2, part, :]), ident[:, :])
                    last.then_inc(k_full, 1)
                if i >= 2:
                    t = i - 2
                    pe.wait_ge(t_low, 2 * t + 2)
                    wait(pe, p_read, t)
                    for half in range(2):
                        steps = [(j, a, b) for j in range(3) for a, b in THREE]
                        for n, (j, a, b) in enumerate(steps):
                            last = pe.matmul(pbank[:, half, :], qT_hl[:, a, j, t * P:(t + 1) * P],
                                             wpT[:, b, j, half * SPAN:(half + 1) * SPAN],
                                             start=(n == 0), stop=(n == len(steps) - 1))
                    last.then_inc(p_full, 1)

        @block.scalar
        def _(act):
            act.wait_ge(eps_set, 1)
            for i in range(TB + 1):
                if i < TB:
                    t = i
                    act.wait_ge(d_full, t + 1)
                    wait(act, k_sum, t - 1)
                    wait(act, norm_done, 2 * (t - 1))
                    nc.scalar.copy(down[:, t % 2, :].rearrange("p (h c) -> p h c", h=2),
                                   dbank[:, t % 2, :, 0:HW]).then_inc(d_read, 1)
                    act.wait_ge(d_read, t + 1)
                    for n, (a, b) in enumerate(((0, QL), (QL, QL + LAT))):
                        wait(act, sq_done, 2 * t + n)
                        nc.scalar.activation(squares[:, 0:b - a], down[:, t % 2, a:b], ACT.Square,
                                             accum_out=sums[:, t % 2, n:n + 1]).then_inc(sq_done, 1)
                    act.wait_ge(sq_done, 2 * t + 2)
                    for n, size in enumerate((QL, LAT)):
                        nc.scalar.activation(root[:, t % 2, n:n + 1], sums[:, t % 2, n:n + 1], ACT.Sqrt,
                                             bias=eps[:, 0:1], scale=1.0 / size).then_inc(root_done, 1)
                if i >= 1:
                    t = i - 1
                    tok = slice(t * P, (t + 1) * P)
                    act.wait_ge(t_full, t + 1)
                    nc.scalar.copy(qT_hl[:, 0, :, tok], tbank[:, 0:QL].rearrange("p (j t) -> p j t", j=3)).then_inc(t_high, 1)
                    nc.scalar.copy(kT_hl[:, 0, tok], tbank[:, QL:QL + P]).then_inc(t_high, 1)
                    act.wait_ge(k_full, t + 1)
                    nc.scalar.copy(kpe[:, :, tok], kbank[:, :].rearrange("p (a t) -> p a t", a=2)).then_inc(k_read, 1)

        @block.vector
        def _(dve):
            nc.vector.memset(eps[:, :], EPS_RMS).then_inc(eps_set, 1)
            dve.wait_ge(w_loaded, 64)
            for i in range(TB + 2):
                if i < TB:
                    t = i
                    par = t % 2
                    dve.wait_ge(d_read, t + 1)
                    wait(dve, k_staged, t - 1)
                    key = down[:, par, QL + LAT:WA].rearrange("p (j d) -> p j d", j=2)
                    nc.vector.tensor_tensor(k_parts[:, par, 0, :].rearrange("p (j d) -> p j d", j=2), key,
                                            cos[:, 1, t, None, :].to_broadcast([P, 2, HALF1]), ALU.mult).then_inc(k_mul, 1)
                    for j in range(2):
                        nc.vector.tensor_tensor(k_parts[:, par, 1, j * HALF1:(j + 1) * HALF1], key[:, 1 - j, :],
                                                sin[:, 1, t, j, :], ALU.mult).then_inc(k_mul, 1)
                    dve.wait_ge(root_done, 2 * t + 2)
                    nc.vector.reciprocal(inv[:, par, :], root[:, par, :]).then_inc(inv_done, 1)
                    dve.wait_ge(inv_done, t + 1)
                    wait(dve, t_full, t - 1)
                    wait(dve, v_low, t - 1)
                    for n, (a, b) in enumerate(((0, QL), (QL, QL + LAT))):
                        nc.vector.scalar_tensor_tensor(out=normed[:, par, a:b], in0=down[:, par, a:b],
                                                       scalar=inv[:, par, n:n + 1], in1=norm_w[:, a:b],
                                                       op0=ALU.mult, op1=ALU.mult).then_inc(norm_done, 1)
                if 0 <= i - 1 < TB:
                    t = i - 1
                    tok = slice(t * P, (t + 1) * P)
                    dve.wait_ge(t_high, 2 * t + 2)
                    nc.vector.tensor_tensor(qT_hl[:, 1, :, tok], tbank[:, 0:QL].rearrange("p (j t) -> p j t", j=3),
                                            f32(qT_hl[:, 0, :, tok]), ALU.subtract).then_inc(t_low, 1)
                    nc.vector.tensor_tensor(kT_hl[:, 1, tok], tbank[:, QL:QL + P], f32(kT_hl[:, 0, tok]),
                                            ALU.subtract).then_inc(t_low, 1)
                if i >= 2:
                    t = i - 2
                    dve.wait_ge(p_full, t + 1)
                    wait(dve, p_sum, t)
                    src = pbank[:, :, :].rearrange("p a (h j d) -> p (a h) j d", j=2, d=HALF1)
                    flat = pbank[:, :, :].rearrange("p a (h d) -> p (a h) d", d=HALF1)
                    nc.vector.tensor_tensor(direct[:, :].rearrange("p (h d) -> p h d", d=HALF1), flat,
                                            cos[:, 0, t, None, :].to_broadcast([P, 2 * NH, HALF1]), ALU.mult)
                    dst = crossed[:, :].rearrange("p (h j d) -> p h j d", j=2, d=HALF1)
                    for j in range(2):
                        last = nc.vector.tensor_tensor(dst[:, :, j, :], src[:, :, 1 - j, :],
                                                       sin[:, 0, t, j, None, :].to_broadcast([P, NH, HALF1]), ALU.mult)
                    last.then_inc(p_read, 1)
            dve.wait_ge(t_low, 2 * TB)

        @block.gpsimd
        def _(pool):
            for i in range(TB + 2):
                if i < TB:
                    t = i
                    par = t % 2
                    pool.wait_ge(k_mul, 3 * t + 3)
                    nc.gpsimd.tensor_tensor(k_parts[:, par, 2, :], k_parts[:, par, 0, :], k_parts[:, par, 1, :],
                                            ALU.add).then_inc(k_sum, 1)
                    pool.wait_ge(k_sum, t + 1)
                    wait(pool, k_full, t - 1)
                    for n in range(2):
                        nc.gpsimd.tensor_copy(k_stage[:, par, 0, n * ROPE:(n + 1) * ROPE], k_parts[:, par, 2, :]
                                              ).then_inc(k_high, 1)
                    pool.wait_ge(k_high, 3 * t + 2)
                    nc.gpsimd.tensor_tensor(k_stage[:, par, 1, 0:ROPE], k_parts[:, par, 2, :],
                                            f32(k_stage[:, par, 0, 0:ROPE]), ALU.subtract).then_inc(k_high, 1)
                    pool.wait_ge(k_high, 3 * t + 3)
                    nc.gpsimd.tensor_tensor(k_stage[:, par, 1, ROPE:2 * ROPE], k_parts[:, par, 2, :],
                                            f32(k_stage[:, par, 0, 0:ROPE]), ALU.subtract).then_inc(k_staged, 1)
                    pool.wait_ge(norm_done, 2 * t + 2)
                    nc.gpsimd.tensor_copy(v_hl[:, 0, t, :], normed[:, par, QL:QL + LAT]).then_inc(v_high, 1)
                    pool.wait_ge(v_high, t + 1)
                    nc.gpsimd.tensor_tensor(v_hl[:, 1, t, :], normed[:, par, QL:QL + LAT], f32(v_hl[:, 0, t, :]),
                                            ALU.subtract).then_inc(v_low, 1)
                if i >= 2:
                    t = i - 2
                    pool.wait_ge(p_read, t + 1)
                    nc.gpsimd.tensor_tensor(qpe[:, t, :], direct[:, :], crossed[:, :], ALU.add
                                            ).then_inc(p_sum, 1)


def load_tables(nc, m, pairs):
    loaded = m.sem("loaded")
    with nc.Block() as block:
        @block.sync
        def _(sp):
            for dst, src in pairs:
                sp.dma_start(dst, src).then_inc(loaded, 16)
            sp.wait_ge(loaded, 16 * len(pairs))


def two_layers(nc, a, out, stop=99):
    from contextlib import contextmanager

    sems = []

    @contextmanager
    def phase(tag):
        with ExitStack() as ctx:
            yield Mem(nc, ctx, tag, sems)

    def clear_semaphores():
        nc.clear_and_free_semaphores(sems)
        sems.clear()
        nc.all_engine_barrier()

    def dram(name, shape, dt=F32):
        return nc.dram_tensor(name, shape, dt, kind="Internal").ap()

    rows = lambda x: x.rearrange("b s d -> (b s) d")
    x0, y_out = rows(a["L0_attn_hidden_states"]), rows(out)
    x1, x2, x3 = (dram(f"x{i}", [NT * P, D]) for i in (1, 2, 3))
    wabs_dram = dram("wabs_dram", [NH, P, 2, 3, LAT])
    wov_dram = dram("wov_dram", [NH, P, 2, D])
    waT_dram = dram("waT_dram", [P, 2, KT, QL + LAT + ROPE])
    wpT_dram = dram("wpT_dram", [P, 2, 3, NH * ROPE])

    with phase("all") as top:
        ident, mask = top.sb("ident", [P, P]), top.sb("mask", [P, P], BF16)
        ident_bf = top.sb("ident_bf", [P, P], BF16)
        with phase("const") as m:
            constants(nc, m, ident, ident_bf, mask)

        view = lambda n: a[n].rearrange("(o p) i -> p o i", p=P)
        with phase("l0") as keep:
            q, k, v = (keep.sb(n, [P, B * KT, TB, P]) for n in "qkv")
            with phase("l0w") as w:
                Wqkv = w.sb("Wqkv", [P, 2, 3, KT, D], F32R)
                with phase("l0wt") as m:
                    raw = m.sb("raw", [P, 3, KT, D])
                    names = ("L0_attn_Wq", "L0_attn_Wk", "L0_attn_Wv")
                    transpose_weights(nc, m, ident, [j for i in range(3) for j in square_jobs(raw[:, i], Wqkv, i, i)],
                                      [(raw[:, i], view(n)) for i, n in enumerate(names)])
                for b in range(B):
                    with phase(f"l0x{b}") as x:
                        xT = x.sb("xT", [P, 2, KT, S], F32R)
                        with phase(f"l0n{b}") as m:
                            norm_transposed(nc, m, ident, x0[b * S:(b + 1) * S], TB, xT)
                        with phase(f"l0p{b}") as m:
                            cos, sin = m.sb("cos", [P, 2, TB, HALF0]), m.sb("sin", [P, 2, TB, 2, HALF0])
                            with phase(f"l0t{b}") as n:
                                load_tables(nc, n, [(cos[:, i], a[f"cos_{w}0"]) for i, w in enumerate("qk")]
                                            + [(sin[:, i], a[f"sin_{w}0"]) for i, w in enumerate("qk")])
                            qkv_layer0(nc, m, b, xT, Wqkv, (cos, sin), q, k, v)
            oT = keep.sb("oT", [P, B * KT, S])
            with phase("l0a") as m:
                attention(nc, m, ident, ident_bf, mask, False, (q, k, v), oT)
            WoT = keep.sb("WoT", [P, 2, 1, KT, D], F32R)
            with phase("l0ot") as m:
                raw = m.sb("raw", [P, KT, D])
                transpose_weights(nc, m, ident, square_jobs(raw, WoT, 0, 0), [(raw[:, :, :], view("L0_attn_Wo"))])
            with phase("l0o") as m:
                tile_oT = lambda t: oT[:, t // TB * KT:(t // TB + 1) * KT, t % TB * P:(t % TB + 1) * P]
                residual(nc, m, NT, x0, x1, None, attn=(tile_oT, WoT[:, :, 0]))
        clear_semaphores()
        if stop == 1:
            return

        with phase("f0") as keep:
            acc = keep.sb("acc", [P, NT, D])
            with phase("f0x") as x:
                xT = x.sb("xT", [P, 2, KT, NT * P], F32R)
                with phase("f0n") as m:
                    norm_transposed(nc, m, ident, x1, NT, xT)
                with phase("f0f") as m:
                    feed_forward(nc, m, ident, xT, acc, a["L0_ffn_w_gate"], a["L0_ffn_w_up"], a["L0_ffn_w_down"])
            with phase("f0r") as m:
                residual(nc, m, NT, x1, x2, lambda t: acc[:, t, :])
        clear_semaphores()
        if stop == 2:
            return

        with phase("w1") as w:
            q_nope = w.sb("q_nope", [P, NH, QL])
            k_b, v_b = w.sb("k_b", [P, NH, LAT]), w.sb("v_b", [P, NH, LAT])
            owT = w.sb("owT", [P, NH, D])
            waT = w.sb("waT", [P, 2, KT, QL + LAT + ROPE], F32R)
            wpT = w.sb("wpT", [P, 2, 3, NH * ROPE], F32R)
            with phase("w1t") as m:
                qa = m.sb("qa", [P, 3, D])
                kva = m.sb("kva", [P, 2, D])
                qp = m.sb("qp", [P, NH // 2, QL])
                ow = m.sb("ow", [P, KT, NH * VD // 2])
                q_b = a["L1_attn_q_b_w"].rearrange("(h r) j -> r h j", r=QHD)
                kv_b = a["L1_attn_kv_b_w"].rearrange("(h t d) c -> t d h c", t=2, d=NOPE)
                o_w = a["L1_attn_o_w"].rearrange("(o p) v -> p o v", p=P)
                pe_rows = q_b[NOPE:QHD].rearrange("r (n e) j -> e r n j", e=2)
                loads = [(qa[:, :, :], a["L1_attn_q_a_w"].rearrange("(o p) i -> p o i", p=P)),
                         (kva[:, 0, :], a["L1_attn_kv_a_w"][0:P]),
                         (kva[0:ROPE, 1, :], a["L1_attn_kv_a_w"][P:P + ROPE]),
                         (qp[0:ROPE], pe_rows[0]), (qp[ROPE:P], pe_rows[1]),
                         (q_nope[:, :, :], q_b[0:NOPE]), (k_b[:, :, :], kv_b[0]), (v_b[:, :, :], kv_b[1]),
                         (ow[:, :, :], o_w[:, :, 0:NH * VD // 2])]
                jobs = [([(qa[:, i, c * P:(c + 1) * P], i * P) for i in range(3)] + [(kva[:, 0, c * P:(c + 1) * P], 3 * P)],
                         whole(SPAN), waT[:, 0, c, 0:SPAN], waT[:, 1, c, 0:SPAN], 1) for c in range(KT)]
                jobs.append(([(kva[0:ROPE, 1, c * P:(c + 1) * P], c * ROPE) for c in range(KT)],
                             lambda bank: bank[:, 0:KT * ROPE].rearrange("p (c r) -> p c r", c=KT),
                             waT[:, 0, :, SPAN:SPAN + ROPE], waT[:, 1, :, SPAN:SPAN + ROPE], 2))
                jobs += [([(qp[:, 4 * g + i, j * P:(j + 1) * P], i * P) for i in range(4)], whole(SPAN),
                          wpT[:, 0, j, g * SPAN:(g + 1) * SPAN], wpT[:, 1, j, g * SPAN:(g + 1) * SPAN], 4)
                         for j in range(3) for g in range(2)]
                jobs += [([(ow[:, o, h * P:(h + 1) * P], o * P) for o in range(KT)], whole(SPAN), owT[:, h, :], None, 8)
                         for h in range(NH // 2)]
                transpose_weights(nc, m, ident, jobs, loads)
            with phase("w1u") as m:
                ow = m.sb("ow", [P, KT, NH * VD // 2])
                transpose_weights(nc, m, ident,
                                  [([(ow[:, o, h * P:(h + 1) * P], o * P) for o in range(KT)], whole(SPAN),
                                    owT[:, NH // 2 + h, :], None, 0) for h in range(NH // 2)],
                                  [(ow[:, :, :], o_w[:, :, NH * VD // 2:])])
            with phase("w1s") as m:
                store_all(nc, m, [(waT_dram, f32(waT[:, :, :, :])), (wpT_dram, f32(wpT[:, :, :, :]))])
            with phase("w1a") as m:
                absorbed_weights(nc, m, q_nope, k_b, v_b, owT, wabs_dram, wov_dram)
        clear_semaphores()
        for b in range(B):
            with phase(f"l1_{b}") as keep:
                acc = keep.sb("acc", [P, TB, D])
                with phase(f"l1k{b}") as mid:
                    ops = {"qT_hl": mid.sb("qT_hl", [P, 2, 3, S], F32R), "kT_hl": mid.sb("kT_hl", [P, 2, S], F32R),
                           "kpe": mid.sb("kpe", [P, 2, S], F32R), "v_hl": mid.sb("v_hl", [P, 2, TB, LAT], F32R),
                           "qpe": mid.sb("qpe", [P, TB, NH * ROPE]), "wabs_dram": wabs_dram, "wov_dram": wov_dram}
                    with phase(f"l1x{b}") as x:
                        xT = x.sb("xT", [P, 2, KT, S], F32R)
                        with phase(f"l1n{b}") as m:
                            norm_transposed(nc, m, ident, x2[b * S:(b + 1) * S], TB, xT)
                        with phase(f"l1p{b}") as m:
                            cos, sin = m.sb("cos", [P, 2, TB, HALF1]), m.sb("sin", [P, 2, TB, 2, HALF1])
                            with phase(f"l1t{b}") as n:
                                load_tables(nc, n, [(cos[:, i], a[f"cos_{w}1"]) for i, w in enumerate("qk")]
                                            + [(sin[:, i], a[f"sin_{w}1"]) for i, w in enumerate("qk")])
                            latent_operands(nc, m, ident, xT, (waT_dram, wpT_dram),
                                            (a["L1_attn_q_a_ln_w"], a["L1_attn_kv_a_ln_w"]), (cos, sin), ops)
                    with phase(f"l1a{b}") as m:
                        attention(nc, m, ident, ident_bf, mask, True, ops, acc)
                with phase(f"l1r{b}") as m:
                    residual(nc, m, TB, x2[b * S:(b + 1) * S], x3[b * S:(b + 1) * S], lambda t: acc[:, t, :])
            clear_semaphores()
        if stop == 3:
            return

        with phase("f1") as keep:
            acc = keep.sb("acc", [P, NT, D])
            with phase("f1x") as x:
                squares = x.sb("squares", [P, NT * P])
                xT = x.sb("xT", [P, 2, KT, NT * P], F32R)
                with phase("f1n") as m:
                    norm_transposed(nc, m, ident, x3, NT, xT)
                with phase("f1f") as m:
                    w = a["L1_ffn_w_gate_up"]
                    feed_forward(nc, m, ident, xT, acc, w[0:HID], w[HID:2 * HID], a["L1_ffn_w_proj"],
                                 (ident_bf, squares))
                with phase("f1s") as m:
                    scale_rows(nc, m, squares, acc)
            with phase("f1r") as m:
                residual(nc, m, NT, x3, y_out, lambda t: acc[:, t, :])
        clear_semaphores()


_INS = ['L0_attn_hidden_states', 'L0_attn_Wq', 'L0_attn_Wk', 'L0_attn_Wv', 'L0_attn_Wo', 'L0_ffn_w_gate',
        'L0_ffn_w_up', 'L0_ffn_w_down', 'L1_attn_q_a_w', 'L1_attn_q_a_ln_w', 'L1_attn_q_b_w', 'L1_attn_kv_a_w',
        'L1_attn_kv_a_ln_w', 'L1_attn_kv_b_w', 'L1_attn_o_w', 'L1_ffn_w_gate_up', 'L1_ffn_w_proj']


def rotary_tables(width, scale):
    freq = (1.0 / 10000.0 ** (np.arange(0, width, 2, dtype=np.float32) / width)).astype(np.float32)
    angle = np.outer(np.arange(S, dtype=np.float32), freq).astype(np.float32)
    tiles = lambda x: x.astype(np.float32).reshape(TB, P, width // 2).transpose(1, 0, 2)
    cos, sin = tiles(np.cos(angle) * np.float32(scale)), tiles(np.sin(angle) * np.float32(scale))
    return np.ascontiguousarray(cos), np.ascontiguousarray(np.stack([-sin, sin], axis=2))


def kernel(**inputs):
    import concourse.bacc as _bacc
    from concourse.bass_utils import run_bass_kernel_spmd as _run

    nc = _bacc.Bacc("TRN2", target_bir_lowering=False, num_devices=1)
    host = {n: np.ascontiguousarray(inputs[n]) for n in _INS}
    for i, (width, scale) in enumerate(((HD0, SCALE0), (ROPE, SCALE1))):
        host[f"cos_k{i}"], host[f"sin_k{i}"] = rotary_tables(width, 1.0)
        host[f"cos_q{i}"], host[f"sin_q{i}"] = rotary_tables(width, scale)
    aps = {n: nc.dram_tensor(f"in_{n}", x.shape, mybir.dt.from_np(x.dtype), kind="ExternalInput").ap()
           for n, x in host.items()}
    out = nc.dram_tensor("out_0", (B, S, D), F32, kind="ExternalOutput").ap()
    two_layers(nc, aps, out)
    r = _run(nc, [{f"in_{n}": x for n, x in host.items()}], core_ids=[0])
    return r.results[0]["out_0"]
```

```python
from contextlib import ExitStack

import numpy as np

import concourse.bass as bass
from concourse import mybir

F32 = mybir.dt.float32
F32R = mybir.dt.float32r
BF16 = mybir.dt.bfloat16
ACT = mybir.ActivationFunctionType
ALU = mybir.AluOpType
AX = mybir.AxisListType

P = 128
D = 512
KT = D // P
B, S = 2, 1024
TB = S // P
NT = B * TB
SPAN = 512
QT = SPAN // P
EPS_LN = 1e-5
MASKED = -1e30

NH = 16
HD0 = D // NH
HALF0 = HD0 // 2
HID = 4 * D
HG = 256
NG = HID // HG
NOPE, ROPE, VD, LAT, QL = 128, 64, 128, 128, 384
QHD = NOPE + ROPE
HALF1 = ROPE // 2
EPS_RMS = 1e-6
SCALE0, SCALE1 = float(HD0) ** -0.5, float(QHD) ** -0.5
EPS_F32 = float(np.finfo(np.float32).eps)
GROUP = 64
THREE = [(0, 0), (0, 1), (1, 0)]


def wait(eng, sem, value):
    if isinstance(value, int) and value <= 0:
        return
    eng.wait_ge(sem, value)


class Mem:

    def __init__(self, nc, ctx, tag, sems):
        self.nc, self.ctx, self.tag, self.sems = nc, ctx, tag, sems

    def sb(self, name, shape, dt=F32):
        return self.ctx.enter_context(self.nc.sbuf_tensor(f"{self.tag}_{name}", shape, dt))

    def ps(self, name, shape, dt=F32):
        return self.ctx.enter_context(self.nc.psum_tensor(f"{self.tag}_{name}", shape, dt))

    def sem(self, name):
        handle = self.nc.alloc_semaphore(name=f"{self.tag}_{name}")
        self.sems.append(handle)
        return handle


def f32(ap):
    return ap.bitcast(F32)


def constants(nc, m, ident, ident_bf, mask_bf):
    mask = m.sb("mask", [P, P])
    zeroed, made = m.sem("zeroed"), m.sem("made")
    with nc.Block() as block:
        @block.gpsimd
        def _(pool):
            nc.gpsimd.memset(ident[:, :], 0.0).then_inc(zeroed, 1)
            nc.gpsimd.memset(mask[:, :], 0.0).then_inc(zeroed, 1)
            pool.wait_ge(zeroed, 2)
            nc.gpsimd.affine_select(out=ident[:, :], in_=ident[:, :], compare_op=ALU.not_equal, fill=1.0,
                                    base=0, pattern=[[-1, P]], channel_multiplier=1).then_inc(made, 1)
            nc.gpsimd.affine_select(out=mask[:, :], in_=mask[:, :], compare_op=ALU.is_ge, fill=MASKED,
                                    base=0, pattern=[[-1, P]], channel_multiplier=1).then_inc(made, 1)
            pool.wait_ge(made, 2)
            nc.gpsimd.tensor_copy(ident_bf[:, :], ident[:, :]).then_inc(made, 1)
            nc.gpsimd.tensor_copy(mask_bf[:, :], mask[:, :]).then_inc(made, 1)
            pool.wait_ge(made, 4)


def transpose_weights(nc, m, ident, jobs, loads):
    RING = 4
    bank = m.ps("bank", [P, RING, SPAN])
    loaded = [m.sem(f"loaded{i}") for i in range(len(loads))]
    turned, high_done, low_done = m.sem("turned"), m.sem("high_done"), m.sem("low_done")
    with nc.Block() as block:
        @block.sync
        def _(sp):
            for i, (dst, src) in enumerate(loads):
                sp.dma_start(dst, src).then_inc(loaded[i], 16)

        @block.tensor
        def _(pe):
            have = -1
            for n, (blocks, view, hi, lo, need) in enumerate(jobs):
                if need > have:
                    for i in range(have + 1, need + 1):
                        pe.wait_ge(loaded[i], 16)
                    have = need
                wait(pe, low_done, n - RING + 1)
                for src, off in blocks:
                    rows, cols = src.shape[0], src.shape[1]
                    last = pe.transpose(bank[0:cols, n % RING, off:off + rows], src, ident[0:rows, 0:rows])
                last.then_inc(turned, 1)

        @block.scalar
        def _(act):
            for n, (blocks, view, hi, lo, need) in enumerate(jobs):
                if lo is not None:
                    act.wait_ge(turned, n + 1)
                    nc.scalar.copy(hi, view(bank[:, n % RING])).then_inc(high_done, 1)

        @block.vector
        def _(dve):
            for n, (blocks, view, hi, lo, need) in enumerate(jobs):
                if lo is None:
                    dve.wait_ge(turned, n + 1)
                    nc.vector.tensor_copy(hi, view(bank[:, n % RING])).then_inc(low_done, 1)
                else:
                    dve.wait_ge(high_done, n + 1)
                    nc.vector.tensor_tensor(lo, view(bank[:, n % RING]), f32(hi),
                                            ALU.subtract).then_inc(low_done, 1)
            dve.wait_ge(low_done, len(jobs))


def whole(cols):
    return lambda bank: bank[:, 0:cols]


def square_jobs(raw, dst_hl, w, need):
    return [([(raw[:, o, k * P:(k + 1) * P], o * P) for o in range(KT)], whole(D),
             dst_hl[:, 0, w, k, :], dst_hl[:, 1, w, k, :], need) for k in range(KT)]


def norm_transposed(nc, m, ident, src, tiles, xT_hl, loads=()):
    x = m.sb("x", [P, tiles, D])
    xn = m.sb("xn", [P, 2, D])
    stats = m.sb("stats", [P, tiles, 6])
    mv = m.sb("mv", [P, tiles, 2])
    std = m.sb("std", [P, tiles])
    rstd = m.sb("rstd", [P, tiles])
    eps = m.sb("eps", [P, 1])
    bank = m.ps("bank", [P, 2, SPAN])
    groups = tiles // QT
    loaded = [m.sem(f"loaded{g}") for g in range(groups)]
    next_loaded = m.sem("next_loaded")
    stats_done, mv_done, std_done, rstd_done = (m.sem(x) for x in ("stats_done", "mv_done", "std_done", "rstd_done"))
    normed, turned, high_done, low_done, eps_set = (
        m.sem(x) for x in ("normed", "turned", "high_done", "low_done", "eps_set"))
    with nc.Block() as block:
        @block.sync
        def _(sp):
            for g in range(groups):
                rows = src[g * SPAN:(g + 1) * SPAN, :].rearrange("(t p) d -> p t d", p=P)
                sp.dma_start(x[:, g * QT:(g + 1) * QT, :], rows).then_inc(loaded[g], 16)
            for dst, extra in loads:
                sp.dma_start(dst, extra).then_inc(next_loaded, 16)
            wait(sp, next_loaded, 16 * len(loads))

        @block.vector
        def _(dve):
            def statistics(g):
                dve.wait_ge(loaded[g], 16)
                for t in range(g * QT, (g + 1) * QT):
                    nc.vector.bn_stats(stats[:, t, :], x[:, t, :]).then_inc(stats_done, 1)
                for t in range(g * QT, (g + 1) * QT):
                    dve.wait_ge(stats_done, t + 1)
                    nc.vector.bn_aggr(mv[:, t, :], stats[:, t, :]).then_inc(mv_done, 1)

            nc.vector.memset(eps[:, :], EPS_LN).then_inc(eps_set, 1)
            statistics(0)
            for g in range(groups):
                if g + 1 < groups:
                    statistics(g + 1)
                a, b = g * QT, (g + 1) * QT
                dve.wait_ge(std_done, g + 1)
                nc.vector.reciprocal(rstd[:, a:b], std[:, a:b]).then_inc(rstd_done, 1)
                dve.wait_ge(rstd_done, g + 1)
                for t in range(a, b + 1):
                    if t < b:
                        wait(dve, turned, t - 1)
                        nc.vector.tensor_scalar(xn[:, t % 2, :], x[:, t, :], mv[:, t, 0:1], rstd[:, t:t + 1],
                                                ALU.subtract, ALU.mult).then_inc(normed, 1)
                    if t > a:
                        u = t - 1
                        dve.wait_ge(high_done, u + 1)
                        low = xT_hl[:, 1, :, u * P:(u + 1) * P]
                        nc.vector.tensor_tensor(low, bank[:, u % 2, :].rearrange("p (k t) -> p k t", k=KT),
                                                f32(xT_hl[:, 0, :, u * P:(u + 1) * P]),
                                                ALU.subtract).then_inc(low_done, 1)
            dve.wait_ge(low_done, tiles)

        @block.scalar
        def _(act):
            act.wait_ge(eps_set, 1)

            def root(g):
                act.wait_ge(mv_done, (g + 1) * QT)
                a, b = g * QT, (g + 1) * QT
                nc.scalar.activation(std[:, a:b], mv[:, a:b, 1], ACT.Sqrt, bias=eps[:, 0:1]).then_inc(std_done, 1)

            root(0)
            for g in range(groups):
                if g + 1 < groups:
                    root(g + 1)
                for t in range(g * QT, (g + 1) * QT):
                    act.wait_ge(turned, t + 1)
                    nc.scalar.copy(xT_hl[:, 0, :, t * P:(t + 1) * P],
                                   bank[:, t % 2, :].rearrange("p (k t) -> p k t", k=KT)).then_inc(high_done, 1)

        @block.tensor
        def _(pe):
            for t in range(tiles):
                pe.wait_ge(normed, t + 1)
                wait(pe, low_done, t - 1)
                for k in range(KT):
                    last = pe.transpose(bank[:, t % 2, k * P:(k + 1) * P], xn[:, t % 2, k * P:(k + 1) * P],
                                        ident[:, :])
                last.then_inc(turned, 1)


def residual(nc, m, tiles, src, dst, y_of, attn=None):
    RING = 4
    x = m.sb("x", [P, RING, D])
    stats = m.sb("stats", [P, RING, 6])
    mv = m.sb("mv", [P, RING, 2])
    std = m.sb("std", [P, RING])
    rstd = m.sb("rstd", [P, RING])
    z = m.sb("z", [P, RING, D])
    eps = m.sb("eps", [P, 1])
    loaded = [m.sem(f"loaded{i}") for i in range(RING)]
    stored = [m.sem(f"stored{i}") for i in range(RING)]
    names = ("stats_done", "mv_done", "std_done", "rstd_done", "z_done", "sum_done", "eps_set", "o_high", "o_low", "y_full")
    stats_done, mv_done, std_done, rstd_done, z_done, sum_done, eps_set, o_high, o_low, y_full = (m.sem(n) for n in names)
    if attn:
        oT, WoT_hl = attn
        ot_hl = m.sb("ot_hl", [P, 2, 2, KT, P], F32R)
        ybank = m.ps("ybank", [P, RING, SPAN])
        y_of = lambda t: ybank[:, t % RING, :]
    with nc.Block() as block:
        @block.sync
        def _(sp):
            for t in range(tiles + 1):
                if t < tiles:
                    wait(sp, sum_done, t - RING + 1)
                    sp.dma_start(x[:, t % RING, :], src[t * P:(t + 1) * P, :]).then_inc(loaded[t % RING], 16)
                if t:
                    u = t - 1
                    sp.wait_ge(sum_done, u + 1)
                    sp.dma_start(dst[u * P:(u + 1) * P, :], z[:, u % RING, :]).then_inc(stored[u % RING], 16)
            for i in range(RING):
                sp.wait_ge(stored[i], 16 * (tiles // RING))

        if attn:
            @block.tensor
            def _(pe):
                for t in range(tiles):
                    pe.wait_ge(o_low, t + 1)
                    wait(pe, z_done, t - RING + 1)
                    steps = [(g, a, b) for g in range(KT) for a, b in THREE]
                    for n, (g, a, b) in enumerate(steps):
                        last = pe.matmul(ybank[:, t % RING, :], ot_hl[:, t % 2, a, g, :], WoT_hl[:, b, g, :],
                                         start=(n == 0), stop=(n == len(steps) - 1))
                    last.then_inc(y_full, 1)

        @block.scalar
        def _(act):
            act.wait_ge(eps_set, 1)
            for t in range(tiles + 1):
                if attn and t < tiles:
                    wait(act, y_full, t - 1)
                    nc.scalar.copy(ot_hl[:, t % 2, 0], oT(t)).then_inc(o_high, 1)
                if t:
                    u = t - 1
                    act.wait_ge(mv_done, u + 1)
                    nc.scalar.activation(std[:, u % RING:u % RING + 1], mv[:, u % RING, 1:2], ACT.Sqrt,
                                         bias=eps[:, 0:1]).then_inc(std_done, 1)

        @block.vector
        def _(dve):
            nc.vector.memset(eps[:, :], EPS_LN).then_inc(eps_set, 1)

            def low(t):
                if attn and t < tiles:
                    dve.wait_ge(o_high, t + 1)
                    nc.vector.tensor_tensor(ot_hl[:, t % 2, 1], oT(t), f32(ot_hl[:, t % 2, 0]),
                                            ALU.subtract).then_inc(o_low, 1)

            low(0)
            for t in range(tiles + 1):
                low(t + 1)
                if t < tiles:
                    r = t % RING
                    if attn:
                        dve.wait_ge(y_full, t + 1)
                    nc.vector.bn_stats(stats[:, r, :], y_of(t)).then_inc(stats_done, 1)
                    dve.wait_ge(stats_done, t + 1)
                    nc.vector.bn_aggr(mv[:, r, :], stats[:, r, :]).then_inc(mv_done, 1)
                if t:
                    u = t - 1
                    r = u % RING
                    dve.wait_ge(std_done, u + 1)
                    nc.vector.reciprocal(rstd[:, r:r + 1], std[:, r:r + 1]).then_inc(rstd_done, 1)
                    dve.wait_ge(rstd_done, u + 1)
                    wait(dve, stored[r], 16 * (u // RING))
                    nc.vector.tensor_scalar(z[:, r, :], y_of(u), mv[:, r, 0:1], rstd[:, r:r + 1],
                                            ALU.subtract, ALU.mult).then_inc(z_done, 1)

        @block.gpsimd
        def _(pool):
            for t in range(tiles):
                r = t % RING
                pool.wait_ge(z_done, t + 1)
                pool.wait_ge(loaded[r], 16 * (t // RING + 1))
                nc.gpsimd.tensor_tensor(z[:, r, :], z[:, r, :], x[:, r, :], ALU.add).then_inc(sum_done, 1)


def qkv_layer0(nc, m, batch, xT_hl, W_hl, rope, q, k, v):
    bank = m.ps("bank", [P, 2, 3, SPAN])
    direct = m.sb("direct", [P, 2, 2, D])
    crossed = m.sb("crossed", [P, 2, 2, D])
    cos, sin = rope
    full = [m.sem(f"full_{n}") for n in "qkv"]
    read = [m.sem(f"read_{n}") for n in "qkv"]
    rotated = m.sem("rotated")
    with nc.Block() as block:
        @block.tensor
        def _(pe):
            for t in range(TB):
                for w in range(3):
                    wait(pe, read[w], t - 1)
                    steps = [(c, xa, wa) for c in range(KT) for xa, wa in THREE]
                    for n, (c, xa, wa) in enumerate(steps):
                        last = pe.matmul(bank[:, t % 2, w, :], xT_hl[:, xa, c, t * P:(t + 1) * P],
                                         W_hl[:, wa, w, c, :], start=(n == 0), stop=(n == len(steps) - 1))
                    last.then_inc(full[w], 1)

        @block.vector
        def _(dve):
            for t in range(TB):
                tt = t
                for w in range(2):
                    src = bank[:, t % 2, w, :].rearrange("p (h j d) -> p h j d", h=NH, j=2)
                    dve.wait_ge(full[w], t + 1)
                    wait(dve, rotated, 2 * (t - 1) + w - 1)
                    cb = cos[:, w, tt, None, :].to_broadcast([P, 2 * NH, HALF0])
                    nc.vector.tensor_tensor(direct[:, t % 2, w, :].rearrange("p (h d) -> p h d", d=HALF0),
                                            bank[:, t % 2, w, :].rearrange("p (h d) -> p h d", d=HALF0),
                                            cb, ALU.mult)
                    dst = crossed[:, t % 2, w, :].rearrange("p (h j d) -> p h j d", h=NH, j=2)
                    for j in range(2):
                        sb = sin[:, w, tt, j, None, :].to_broadcast([P, NH, HALF0])
                        last = nc.vector.tensor_tensor(dst[:, :, j, :], src[:, :, 1 - j, :], sb, ALU.mult)
                    last.then_inc(read[w], 1)

        @block.gpsimd
        def _(pool):
            for t in range(TB):
                b, tt = batch, t
                for w, out in enumerate((q, k)):
                    pool.wait_ge(read[w], t + 1)
                    view = lambda x: x[:, t % 2, w, :].rearrange("p (g d) -> p g d", g=KT)
                    nc.gpsimd.tensor_tensor(out[:, b * KT:(b + 1) * KT, tt, :], view(direct), view(crossed),
                                            ALU.add).then_inc(rotated, 1)

        @block.scalar
        def _(act):
            for t in range(TB):
                b, tt = batch, t
                act.wait_ge(full[2], t + 1)
                nc.scalar.copy(v[:, b * KT:(b + 1) * KT, tt, :],
                               bank[:, t % 2, 2, :].rearrange("p (g d) -> p g d", g=KT)).then_inc(read[2], 1)


KINDS0 = "XCMENDZLPOIQGV"
GROUP_HEADS = 4
STEPS = 3 * QT
AHEAD = 2
RING0 = 4
MAX_PARTS = [(t, c) for t in range(TB) for c in range(0, (t + 1) * P, SPAN)]
M_AT = [0, 2, 2, 1, 1, 2, 2, 1, 1, 0, 0, 0]


def step_of(k):
    s, kt = (0, k) if k < QT else (1, k - QT)
    return s, kt, max(0, kt - QT * s) * P, kt >= QT * s


def head_events(h, last_head=None):
    more = lambda head: last_head is None or head <= last_head
    parts = iter(range(len(MAX_PARTS)))
    for k in range(STEPS):
        if k == 0 and more(h + 1):
            yield "C", h + 1, 3
        if k in (10, 11) and more(h + 2):
            yield from [("C", h + 2, 0), ("C", h + 2, 1)] if k == 10 else [("C", h + 2, 2)]
        if k in (7, 11) and more(h + 1):
            yield "D", h + 1, k // 11
        j = k + AHEAD
        if more(h + j // STEPS):
            yield "Z", h + j // STEPS, j % STEPS
        j -= 1
        if more(h + j // STEPS):
            yield "L", h + j // STEPS, j % STEPS
        if k in (1, 4) and more(h + 2):
            yield "G", h + 2, k // 4
        if k == 7 and more(h + 1):
            yield "V", h + 1, 0
        if more(h + 1):
            for _ in range(M_AT[k]):
                yield "M", h + 1, next(parts)
            if k in (4, 9):
                yield "E", h + 1, k // 9
            if k in (6, 10):
                yield "N", h + 1, k // 10
        if more(h + 2):
            yield from {9: [("X", h + 2, 0), ("X", h + 2, 1)], 10: [("X", h + 2, 2)], 11: [("X", h + 2, 3)]}.get(k, [])
        if k == 1 and h > 0:
            yield "O", h - 1, 1
        if k in (2, 7) and h >= GROUP_HEADS:
            yield "I", h, 2 * (h % GROUP_HEADS) + k // 7
        if k == STEPS - 1 and h >= GROUP_HEADS and h % 2:
            yield "Q", h, h % GROUP_HEADS // 2
        if k == QT + 1:
            yield "O", h, 0
        yield "P", h, k
    if last_head == h:
        yield "O", h, 1
        for n in range(8):
            yield "I", h + 1, n
            if n % 4 == 3:
                yield "Q", h + 1, n // 4


def opening_events():
    yield from [("G", 0, 0), ("G", 0, 1), ("V", 0, 0)]
    for n in range(4):
        yield from [("X", 0, n), ("C", 0, n)]
    yield from [("G", 1, 0), ("G", 1, 1)]
    for n in range(len(MAX_PARTS)):
        yield "M", 0, n
        if n == QT - 1:
            yield from [("E", 0, 0), ("N", 0, 0), ("D", 0, 0), ("Z", 0, 0)]
    yield from [("E", 0, 1), ("Z", 0, 1), ("L", 0, 0), ("N", 0, 1), ("D", 0, 1)]
    for n in range(2, AHEAD):
        yield from [("Z", 0, n), ("L", 0, n - 1)]
    for n in range(3):
        yield from [("X", 1, n), ("C", 1, n)]
    yield "X", 1, 3


def counted(events, before):
    seen = dict(before)
    for kind, h, n in events:
        yield kind, h, n, dict(seen)
        seen[kind] = seen[kind] + 1
        if kind in "XN":
            seen[n % 2] = seen[n % 2] + 1
        if (kind, n) == ("N", 0):
            seen["first maxima"] = seen[0]


def each_head(eng, turns, per_turn, run):
    G = GROUP_HEADS
    first = list(opening_events()) + [e for h in range(G) for e in head_events(h)]
    body = [e for h in range(G, G + per_turn) for e in head_events(h)]
    last = [e for h in range(G, per_turn) for e in head_events(h, last_head=per_turn - 1)]
    keys = list(KINDS0) + [0, 1]
    count = lambda ev, k: sum(e[0] in "XN" and e[2] % 2 == k if isinstance(k, int) else e[0] == k for e in ev)
    start = {k: count(first, k) for k in keys}
    per = {k: count(body, k) for k in keys}
    run(counted(first, {k: 0 for k in keys}), 0)
    with eng.Fori(0, turns - 1) as it:
        run(counted(body, {k: start[k] + it * per[k] for k in keys}), it)
    run(counted(last, {k: start[k] + (turns - 1) * per[k] for k in keys}), turns - 1)


def attention_layer0(nc, m, ident, ident_bf, mask, q, k, v, out):
    HB = 2 * GROUP_HEADS
    turns = B * NH // HB
    QW = 3 * HD0
    KW = QW + 2
    VW = 3 * HD0

    mbank = m.ps("mbank", [P, 2, SPAN])
    sbank = m.ps("sbank", [P, 2, SPAN])
    obank = m.ps("obank", [P, 2, SPAN])
    xbank = m.ps("xbank", [P, 2, SPAN])
    probs = m.sb("probs", [P, RING0, SPAN])
    probs_hl = m.sb("probs_hl", [P, RING0, 2, SPAN], F32R)
    negmax = m.sb("negmax", [P, 2, len(MAX_PARTS)])
    negmax_span = m.sb("negmax_span", [P, QT])
    negmax_hl = m.sb("negmax_hl", [P, 2, 2, QT, 2], F32R)
    q_stage, k_stage = (m.sb(n, [P, TB, QW], F32R) for n in ("q_stage", "k_stage"))
    v_stage = m.sb("v_stage", [P, 2, TB, VW], F32R)
    q_stack, k_stack = (m.sb(n, [P, 2, S], F32R) for n in ("q_stack", "k_stack"))
    o_low_rows = m.sb("o_low_rows", [HD0, 2, SPAN])
    sum_rows = m.sb("sum_rows", [P, 2, 2, SPAN])
    ones = m.sb("ones", [P, 1])
    ident_r = m.sb("ident_r", [P, P], F32R)

    bank_full = [m.sem(f"bank_full{i}") for i in range(2)]
    bank_free = [m.sem(f"bank_free{i}") for i in range(2)]
    max_full = m.sem("max_full")
    max_done = m.sem("max_done")
    max_step = m.sem("max_step")
    max_split = m.sem("max_split")
    scores_full = m.sem("scores_full")
    exp_done = m.sem("exp_done")
    low_done = [m.sem("low_by_dve"), m.sem("low_by_pool")]
    values_done = m.sem("values_done")
    o_high = m.sem("o_high")
    o_read = m.sem("o_read")
    inverse_done = m.sem("inverse_done")
    o_done = m.sem("o_done")
    copied = m.sem("copied")
    qk_staged = m.sem("qk_staged")
    v_staged = m.sem("v_staged")
    ones_set = m.sem("ones_set")
    rows_set = m.sem("rows_set")
    passed = m.sem("passed")

    by_pool = lambda k: k % 3 == 1
    head_of = lambda it, h: it * HB + h

    group_of = lambda it, h: it * (HB // GROUP_HEADS) + h // GROUP_HEADS

    def lows_before(it, h, k):
        pool = by_pool(k)
        mine = [j for j in range(STEPS) if by_pool(j) == pool]
        return int(pool), head_of(it, h) * len(mine) + sum(j <= k for j in mine)

    block = m.ctx.enter_context(nc.Block())

    @block.tensor
    def _(pe):
        pe.sem_inc(values_done, RING0)
        pe.wait_ge(rows_set, 4)

        def run(events, it):
            for kind, h, n, seen in events:
                hp = h % 2
                if kind == "X":
                    pe.wait_ge(bank_free[n % 2], seen[n % 2] + 1)
                    if n == 0:
                        pe.wait_ge(qk_staged, head_of(it, h) * 2 + 2)
                    for i in range(QT):
                        last = pe.transpose(xbank[0:QW, n % 2, i * P:(i + 1) * P],
                                            f32((k_stage if n % 2 else q_stage)[:, n // 2 * QT + i, :]), ident[:, :])
                    last.then_inc(bank_full[n % 2], 1)
                elif kind == "M":
                    t, c = MAX_PARTS[n]
                    end = min(c + SPAN, (t + 1) * P)
                    if n == 0:
                        for slot in range(2):
                            pe.wait_ge(bank_free[slot], seen[slot] + 1)
                    pe.wait_ge(max_done, seen["M"] + 1)
                    diagonal = end == (t + 1) * P
                    last = pe.matmul(mbank[:, n % 2, 0:end - c], q_stack[0:QW, hp, t * P:(t + 1) * P],
                                     k_stack[0:QW, hp, c:end], start=True, stop=not diagonal)
                    if diagonal:
                        last = pe.matmul(mbank[:, n % 2, end - c - P:end - c], ident_bf[:, :], mask[:, :],
                                         start=False, stop=True)
                    last.then_inc(max_full, 1)
                elif kind == "N":
                    pe.wait_ge(max_split, seen["N"] + 1)
                    pe.wait_ge(bank_free[n], seen[n] + 1)
                    for i in range(QT):
                        last = pe.matmul(xbank[0:2, n, i * P:(i + 1) * P], negmax_hl[:, hp, n, i, :], ident_r[:, :],
                                         start=True, stop=True)
                    last.then_inc(bank_full[n], 1)
                elif kind == "Z":
                    s, kt, c, diagonal = step_of(n)
                    if kt == 0:
                        pe.wait_ge(bank_free[s], (seen[1] if s else seen["first maxima"]) + 1)
                    pe.wait_ge(exp_done, seen["Z"] + 1)
                    last = pe.matmul(sbank[:, n % 2, c:SPAN], k_stack[0:KW, hp, kt * P:(kt + 1) * P],
                                     q_stack[0:KW, hp, s * SPAN + c:(s + 1) * SPAN], start=True, stop=not diagonal)
                    if diagonal:
                        last = pe.matmul(sbank[:, n % 2, c:c + P], mask[:, :], ident_bf[:, :], start=False, stop=True)
                    last.then_inc(scores_full, 1)
                elif kind == "P":
                    s, kt, c, _ = step_of(n)
                    if kt == 0:
                        pe.wait_ge(o_read, seen["O"] + 1)
                        pe.wait_ge(v_staged, head_of(it, h) + 1)
                    maker, count = lows_before(it, h, n)
                    pe.wait_ge(low_done[maker], count)
                    for b in range(2):
                        last = pe.matmul(obank[0:VW, s, c:SPAN], v_stage[:, hp, kt, :], probs_hl[:, n % RING0, b, c:SPAN],
                                         start=(kt == 0 and b == 0), stop=(kt == QT * (s + 1) - 1 and b == 1))
                    last.then_inc(values_done, 1)

        each_head(pe, turns, HB, run)

    @block.scalar
    def _(act):
        nc.scalar.copy(ident_r[:, :], ident[:, :]).then_inc(rows_set, 1)
        act.sem_inc(exp_done, 2)
        act.sem_inc(bank_free[0], 1)
        act.sem_inc(bank_free[1], 1)

        def run(events, it):
            for kind, h, n, seen in events:
                hp = h % 2
                if kind == "Z":
                    s, kt, c, _ = step_of(n)
                    r = n % RING0
                    act.wait_ge(scores_full, seen["Z"] + 1)
                    act.wait_ge(values_done, seen["Z"] + 1)
                    nc.scalar.activation(probs[:, r, c:SPAN], sbank[:, n % 2, c:SPAN], ACT.Exp)
                    nc.scalar.activation(probs_hl[:, r, 0, c:SPAN], sbank[:, n % 2, c:SPAN], ACT.Exp
                                         ).then_inc(exp_done, 1)
                elif kind == "C" and n % 2 == 0:
                    act.wait_ge(bank_full[0], seen[0])
                    nc.scalar.copy(q_stack[0:QW, hp, n // 2 * SPAN:(n // 2 + 1) * SPAN], xbank[0:QW, 0, :]
                                   ).then_inc(bank_free[0], 1)
                elif kind == "D":
                    act.wait_ge(bank_full[n], seen[n])
                    nc.scalar.copy(q_stack[QW:KW, hp, n * SPAN:(n + 1) * SPAN], xbank[0:2, n, :]
                                   ).then_inc(bank_free[n], 1)
                elif kind == "O":
                    act.wait_ge(values_done, seen["P"] + RING0 - (0 if isinstance(seen["P"], int) and seen["P"] == STEPS * B * NH else 1))
                    act.wait_ge(o_read, seen["O"])
                    j, group = h % GROUP_HEADS, h // GROUP_HEADS % 2
                    if j == 0:
                        act.wait_ge(o_done, seen["Q"] + 1)
                    nc.scalar.copy(o_low_rows[:, n, :], obank[HD0:2 * HD0, n, :])
                    nc.scalar.copy(sum_rows[j * HD0:(j + 1) * HD0, group, n, :], obank[2 * HD0:3 * HD0, n, :]
                                   ).then_inc(o_high, 1)

        each_head(act, turns, HB, run)

    @block.vector
    def _(dve):
        dve.wait_ge(ones_set, 1)
        for par in range(2):
            nc.vector.tensor_copy(k_stack[QW:KW, par, :], ones[QW:KW, :].to_broadcast([2, S])).then_inc(rows_set, 1)
        nc.vector.tensor_copy(v_stage[:, :, :, 2 * HD0:VW].rearrange("p a t c -> p (a t) c"),
                              ones[:, :, None].to_broadcast([P, 2 * TB, HD0])).then_inc(rows_set, 1)
        dve.sem_inc(max_done, 2)
        dve.sem_inc(o_read, 1)

        def run(events, it):
            for kind, h, n, seen in events:
                hp = h % 2
                if kind == "M":
                    t, c = MAX_PARTS[n]
                    dve.wait_ge(max_full, seen["M"] + 1)
                    nc.vector.tensor_reduce(negmax[:, hp, n:n + 1], mbank[:, n % 2, 0:min(SPAN, (t + 1) * P - c)],
                                            AX.X, ALU.max, negate=True).then_inc(max_done, 1)
                elif kind == "E":
                    step = head_of(it, h) * 3 + n
                    dve.wait_ge(max_done, seen["M"] + 2)
                    if n == 0:
                        span = negmax[:, hp, 0:QT]
                    else:
                        span = negmax_span[:, :]
                        halves = negmax[:, hp, QT:3 * QT].rearrange("p (i two) -> p i two", two=2)
                        nc.vector.tensor_tensor(span, halves[:, :, 0], halves[:, :, 1], ALU.min).then_inc(max_step, 1)
                        dve.wait_ge(max_step, step + 1)
                    nc.vector.tensor_copy(negmax_hl[:, hp, n, :, 0], span).then_inc(max_step, 1)
                    dve.wait_ge(max_step, step + 1 + n)
                    nc.vector.tensor_tensor(negmax_hl[:, hp, n, :, 1], span, f32(negmax_hl[:, hp, n, :, 0]),
                                            ALU.subtract).then_inc(max_split, 1)
                elif kind == "L" and not by_pool(n):
                    _, _, c, _ = step_of(n)
                    r = n % RING0
                    dve.wait_ge(exp_done, seen["L"] + 3)
                    nc.vector.tensor_tensor(probs_hl[:, r, 1, c:SPAN], probs[:, r, c:SPAN],
                                            f32(probs_hl[:, r, 0, c:SPAN]), ALU.subtract).then_inc(low_done[0], 1)
                elif kind == "C" and n % 2:
                    dve.wait_ge(bank_full[1], seen[1])
                    nc.vector.tensor_copy(k_stack[0:QW, hp, n // 2 * SPAN:(n // 2 + 1) * SPAN], xbank[0:QW, 1, :]
                                          ).then_inc(bank_free[1], 1)
                elif kind == "O":
                    dve.wait_ge(o_high, seen["O"] + 1)
                    j = h % GROUP_HEADS
                    dst = out[j * HD0:(j + 1) * HD0, bass.ds(group_of(it, h), 1), n * SPAN:(n + 1) * SPAN]
                    nc.vector.tensor_tensor(dst.rearrange("p o t -> p (o t)"), obank[0:HD0, n, :], o_low_rows[:, n, :],
                                            ALU.add).then_inc(o_read, 1)
                elif kind == "I":
                    dve.wait_ge(o_high, seen["O"])
                    part = sum_rows[:, (h // GROUP_HEADS - 1) % 2].rearrange("p s t -> p (s t)")[:, n * P:(n + 1) * P]
                    nc.vector.reciprocal(part, part).then_inc(inverse_done, 1)

        each_head(dve, turns, HB, run)

    @block.gpsimd
    def _(pool):
        nc.gpsimd.memset(ones[:, :], 1.0).then_inc(ones_set, 1)
        pool.wait_ge(ones_set, 1)
        pool.sem_inc(o_done, 1)

        def pool_wait(sem, value):
            wait(pool, sem, value)
            pool.sem_inc(passed, 1)

        def split(dst, x, high_at, low_at, count):
            w = x.shape[-1]
            for i in high_at:
                nc.gpsimd.tensor_tensor(dst[:, :, i * w:(i + 1) * w], x, ones[:, :, None].to_broadcast([P, TB, w]),
                                        ALU.mult).then_inc(copied, 1)
            pool_wait(copied, count + len(high_at))
            return nc.gpsimd.tensor_tensor(dst[:, :, low_at * w:(low_at + 1) * w], x, f32(dst[:, :, 0:w]), ALU.subtract)

        def run(events, it):
            for kind, h, n, seen in events:
                hp = h % 2
                j, g = h % GROUP_HEADS, group_of(it, h)
                rows_of = lambda x: x[:, bass.ds(g, 1), :, j * HD0:(j + 1) * HD0].rearrange("p o t c -> p (o t) c")
                if kind == "G":
                    for slot in range(2):
                        pool_wait(bank_full[slot], seen[slot])
                    count = seen["G"] * 2 + seen["V"]
                    if n == 0:
                        last = split(q_stage[:, :, :], rows_of(q), (0, 2), 1, count)
                    else:
                        last = split(k_stage[:, :, :], rows_of(k), (0, 1), 2, count)
                    last.then_inc(qk_staged, 1)
                elif kind == "V":
                    pool_wait(values_done, seen["P"] - 7 + RING0)
                    split(v_stage[:, hp], rows_of(v), (0,), 1, seen["G"] * 2 + seen["V"]).then_inc(v_staged, 1)
                elif kind == "L" and by_pool(n):
                    _, _, c, _ = step_of(n)
                    r = n % RING0
                    pool_wait(exp_done, seen["L"] + 3)
                    nc.gpsimd.tensor_tensor(probs_hl[:, r, 1, c:SPAN], probs[:, r, c:SPAN],
                                            f32(probs_hl[:, r, 0, c:SPAN]), ALU.subtract).then_inc(low_done[1], 1)
                elif kind == "Q":
                    pool_wait(inverse_done, seen["I"])
                    rows = out[:, bass.ds(group_of(it, h - GROUP_HEADS), 1), n * SPAN:(n + 1) * SPAN]
                    rows = rows.rearrange("p o t -> p (o t)")
                    nc.gpsimd.tensor_tensor(rows, rows, sum_rows[:, (h // GROUP_HEADS - 1) % 2, n, :],
                                            ALU.mult).then_inc(o_done, 1)

        each_head(pool, turns, HB, run)
        pool.wait_ge(o_done, 2 * B * NH // GROUP_HEADS + 1)


SCORES_AT = [[[0], [1, 2], [3], []], [[0, 1], [], [2], [], [3], [], [], []]]
OUTPUTS_AT = [[[], [], [0, 1], [2, 3]], [[0], [1], [2], [3], [], [], [], []]]


def unit_events(u, last_unit):
    h, s = divmod(u, 2)
    more = lambda head: last_unit is None or head <= last_unit // 2
    follows = last_unit is None or u < last_unit
    nh, ns = divmod(u + 1, 2)
    ev, later = [], []
    if s == 1 and more(h + 2):
        ev.append(("G", h + 2, 0, 0))
    for kt in range(QT * (s + 1)):
        ev.append(("T", h, s, kt))
        ev += later
        later = []
        if follows:
            ev += [("S", nh, ns, n) for n in SCORES_AT[s][kt]]
            later = [("R", nh, ns, n) for n in SCORES_AT[s][kt]]
        if kt:
            ev.append(("P", h, s, kt - 1))
        if u > 0:
            ev += [("Y", (u - 1) // 2, (u - 1) % 2, n) for n in OUTPUTS_AT[s][kt]]
        if s == 1 and kt >= QT and more(h + 2):
            ev.append(("X", h + 2, 0, kt - QT))
    ev.append(("P", h, s, QT * (s + 1) - 1))
    ev += later
    ev.append(("O", h, s, 0))
    return ev


def first_events():
    ev = []
    for h in range(2):
        ev += [("G", h, 0, 0)] + [("X", h, 0, n) for n in range(4)]
    for n in range(QT):
        ev += [("S", 0, 0, n)] + ([("R", 0, 0, n - 1)] if n else [])
    return ev + [("R", 0, 0, QT - 1)] + unit_events(0, None)


def last_events(units):
    ev = []
    for u in range(1, units):
        ev += unit_events(u, units - 1)
    return ev + [("Y", (units - 1) // 2, 1, tt) for tt in range(QT)]


WORK = 3


def numbered(events, before):
    seen, uses, sources = dict(before), 0, {}
    for kind, h, s, n in events:
        now = dict(seen)
        if kind in "TXY":
            slot = now["slot"] = uses % WORK
            uses += 1
            seen[slot] = seen[slot] + 1
            sources[kind, h, s, n] = slot, seen[slot]
        if kind == "P":
            now["source"] = sources["T", h, s, n]
        yield kind, h, s, n, now
        seen[kind] = seen[kind] + 1


def each_turn(eng, turns, units, run):
    first, body = first_events(), [e for u in range(1, units + 1) for e in unit_events(u, None)]
    kinds, slots = "STRPGXOY", range(WORK)

    def counts(ev):
        uses = sum(e[0] in "TXY" for e in ev)
        assert uses % WORK == 0
        return {**{k: sum(e[0] == k for e in ev) for k in kinds}, **{i: uses // WORK for i in slots}}

    start, per = counts(first), counts(body)
    run(numbered(first, {k: 0 for k in start}), 0)
    with eng.Fori(0, turns - 1) as it:
        run(numbered(body, {k: start[k] + it * per[k] for k in start}), it)
    done = turns - 1
    run(numbered(last_events(units), {k: start[k] + done * per[k] for k in start}), done)


def attention_layer1(nc, m, ident, ident_bf, mask, src, out):
    HB = 2
    units = 2 * HB
    turns = NH // HB
    RPT = 3
    S_AHEAD = 2

    scores = m.ps("scores", [P, S_AHEAD, 2 * SPAN])
    work = m.ps("work", [P, WORK, SPAN])
    obank = m.ps("obank", [P, SPAN])
    probs = [m.sb(f"probs{s}", [P, QT * QT * s + QT * (QT + 1) // 2, P]) for s in range(2)]
    pT_hl = m.sb("pT_hl", [P, RPT, 2, SPAN], F32R)
    row = m.sb("row", [P, 3, 4 * QT])
    q_stage = m.sb("q_stage", [P, TB, 2 * ROPE], F32R)
    q_stack = m.sb("q_stack", [P, 2, S], F32R)
    ones = m.sb("ones", [P, 1])
    qa_hl = m.sb("qa_hl", [P, 2, 2, S], F32R)
    oT_hl = m.sb("oT_hl", [P, 2, 2, SPAN], F32R)
    wabs = m.sb("wabs", [P, 2, 2, 3, LAT], F32R)
    wov = m.sb("wov", [P, 2, 2, D], F32R)

    work_full = [m.sem(f"work_full{i}") for i in range(WORK)]
    work_free = [m.sem(f"work_free{i}") for i in range(WORK)]
    scores_full = m.sem("scores_full")
    max_done = m.sem("max_done")
    exp_done = m.sem("exp_done")
    inverse_done = m.sem("inverse_done")
    turned_high = m.sem("turned_high")
    values_done = m.sem("values_done")
    o_high = m.sem("o_high")
    o_read = m.sem("o_read")
    x_high = m.sem("x_high")
    copied = m.sem("copied")
    staged = m.sem("staged")
    zeroed = m.sem("zeroed")
    ones_set = m.sem("ones_set")
    passed = m.sem("passed")
    wabs_loaded = [m.sem(f"wabs_loaded{i}") for i in range(2)]
    wov_loaded = [m.sem(f"wov_loaded{i}") for i in range(2)]

    def tile_of(s, n):
        first = sum(QT * s + i + 1 for i in range(n))
        return first, QT * s + n + 1

    def ring(n, s):
        return (n + QT * s) % RPT

    head_of = lambda it, h: it * HB + h

    block = m.ctx.enter_context(nc.Block())

    @block.sync
    def _(sp):
        def load(h, par, ready=None):
            if ready is not None:
                sp.wait_ge(x_high, 2 * (h - 1))
            sp.dma_start(f32(wabs[:, par]), src["wabs_dram"][bass.ds(h, 1)].rearrange("o p a k c -> p (o a) k c")
                         ).then_inc(wabs_loaded[par], 16)
            if ready is not None:
                sp.wait_ge(o_high, 2 * h - 1)
            sp.dma_start(f32(wov[:, par]), src["wov_dram"][bass.ds(h, 1)].rearrange("o p a c -> p (o a) c")
                         ).then_inc(wov_loaded[par], 16)
        load(0, 0)
        load(1, 1)
        with sp.Fori(1, NH // 2) as i:
            for par in range(2):
                load(2 * i + par, par, ready=True)

    @block.tensor
    def _(pe):
        pe.sem_inc(values_done, RPT)

        def run(events, it):
            for kind, h, s, n, seen in events:
                hp = h % 2
                if kind in "TXY":
                    slot = seen["slot"]
                    pe.wait_ge(work_free[slot], seen[slot] + 1)
                if kind == "X":
                    if n < 2:
                        if n == 0:
                            pe.wait_ge(wabs_loaded[hp], 16 * (it * (HB // 2) + h // 2 + 1))
                        steps = [(j, a, b) for j in range(3) for a, b in THREE]
                        for i, (j, a, b) in enumerate(steps):
                            last = pe.matmul(work[:, slot, :], wabs[:, hp, a, j, :],
                                             src["qT_hl"][:, b, j, n * SPAN:(n + 1) * SPAN],
                                             start=(i == 0), stop=(i == len(steps) - 1))
                    else:
                        if n == 2:
                            pe.wait_ge(staged, head_of(it, h) + 1)
                        for i in range(QT):
                            last = pe.transpose(work[:, slot, i * P:(i + 1) * P],
                                                f32(q_stage[:, n % 2 * QT + i, :]), ident[:, :])
                    last.then_inc(work_full[slot], 1)
                elif kind == "S":
                    if s == 0 and n == 0:
                        for i in range(WORK):
                            pe.wait_ge(work_free[i], seen[i])
                    pe.wait_ge(exp_done, seen["S"] + 1)
                    t = QT * s + n
                    buf = n % S_AHEAD
                    rows = slice(t * P, (t + 1) * P)
                    for c in range(0, (t + 1) * P, SPAN):
                        cols = slice(c, min(c + SPAN, (t + 1) * P))
                        steps = [(qa_hl[:, hp, a, rows], src["kT_hl"][:, b, cols]) for a, b in THREE]
                        steps += [(q_stack[:, hp, rows], src["kpe"][:, part, cols]) for part in range(2)]
                        diagonal = cols.stop == (t + 1) * P
                        for i, (lhs, rhs) in enumerate(steps):
                            last = pe.matmul(scores[:, buf, cols], lhs, rhs, start=(i == 0),
                                             stop=(not diagonal and i == len(steps) - 1))
                        if diagonal:
                            last = pe.matmul(scores[:, buf, t * P:(t + 1) * P], ident_bf[:, :], mask[:, :],
                                             start=False, stop=True)
                    last.then_inc(scores_full, 1)
                elif kind == "T":
                    if n == 0:
                        pe.wait_ge(exp_done, seen["O"] * QT + QT + S_AHEAD)
                    for i in range(max(0, n - QT * s), QT):
                        first, _ = tile_of(s, i)
                        last = pe.transpose(work[:, slot, i * P:(i + 1) * P], probs[s][:, first + n, :], ident[:, :])
                    last.then_inc(work_full[slot], 1)
                elif kind == "P":
                    if n == 0:
                        pe.wait_ge(o_read, seen["O"] + 1)
                    bank, uses = seen["source"]
                    pe.wait_ge(work_free[bank], uses + 1)
                    c = max(0, n - QT * s) * P
                    for i, (a, b) in enumerate(THREE):
                        last = pe.matmul(obank[:, c:SPAN], src["v_hl"][:, a, n, :], pT_hl[:, ring(n, s), b, c:SPAN],
                                         start=(n == 0 and i == 0), stop=(n == QT * (s + 1) - 1 and i == 2))
                    last.then_inc(values_done, 1)
                elif kind == "Y":
                    pe.wait_ge(o_read, seen["O"] + 1)
                    if s == 0 and n == 0:
                        pe.wait_ge(wov_loaded[hp], 16 * (it * (HB // 2) + h // 2 + 1))
                    for i, (a, b) in enumerate(THREE):
                        last = pe.matmul(work[:, slot, :], oT_hl[:, s, a, n * P:(n + 1) * P], wov[:, hp, b, :],
                                         start=(i == 0), stop=(i == 2))
                    last.then_inc(work_full[slot], 1)

        each_turn(pe, turns, units, run)

    @block.scalar
    def _(act):
        act.sem_inc(exp_done, S_AHEAD)

        def run(events, it):
            for kind, h, s, n, seen in events:
                hp, slot = h % 2, seen.get("slot")
                if kind == "S":
                    first, wide = tile_of(s, n)
                    row_slot = (hp * 2 + s) * QT + n
                    act.wait_ge(max_done, seen["S"] + 1)
                    nc.scalar.activation(probs[s][:, first:first + wide, :].rearrange("p k c -> p (k c)"),
                                         scores[:, n % S_AHEAD, 0:wide * P], ACT.Exp, bias=row[:, 0, row_slot:row_slot + 1],
                                         accum_out=row[:, 1, row_slot:row_slot + 1]).then_inc(exp_done, 1)
                elif kind == "T":
                    c = max(0, n - QT * s) * P
                    act.wait_ge(work_full[slot], seen[slot] + 1)
                    act.wait_ge(values_done, seen["T"] + 1)
                    nc.scalar.copy(pT_hl[:, ring(n, s), 0, c:SPAN], work[:, slot, c:SPAN]).then_inc(turned_high, 1)
                elif kind == "X" and n < 3:
                    act.wait_ge(work_full[slot], seen[slot] + 1)
                    if n < 2:
                        nc.scalar.copy(qa_hl[:, hp, 0, n * SPAN:(n + 1) * SPAN], work[:, slot, :]).then_inc(x_high, 1)
                    else:
                        nc.scalar.copy(q_stack[:, hp, 0:SPAN], work[:, slot, :]).then_inc(work_free[slot], 1)
                elif kind == "O":
                    act.wait_ge(values_done, seen["P"] + RPT)
                    for i in range(WORK):
                        act.wait_ge(work_full[i], seen[i])
                    nc.scalar.copy(oT_hl[:, s, 0, :], obank[:, :]).then_inc(o_high, 1)

        each_turn(act, turns, units, run)

    @block.vector
    def _(dve):
        for i in range(WORK):
            dve.sem_inc(work_free[i], 1)
        dve.sem_inc(o_read, 1)
        nc.vector.memset(out[:, :, :], 0.0).then_inc(zeroed, 1)
        dve.wait_ge(zeroed, 1)

        def run(events, it):
            for kind, h, s, n, seen in events:
                hp, slot = h % 2, seen.get("slot")
                row_slot = (hp * 2 + s) * QT + n
                if kind == "S":
                    _, wide = tile_of(s, n)
                    dve.wait_ge(scores_full, seen["S"] + 1)
                    nc.vector.tensor_reduce(row[:, 0, row_slot:row_slot + 1], scores[:, n % S_AHEAD, 0:wide * P],
                                            AX.X, ALU.max, negate=True).then_inc(max_done, 1)
                elif kind == "R":
                    dve.wait_ge(exp_done, seen["R"] + 1 + S_AHEAD)
                    nc.vector.reciprocal(row[:, 2, row_slot:row_slot + 1], row[:, 1, row_slot:row_slot + 1]
                                         ).then_inc(inverse_done, 1)
                elif kind == "T":
                    c = max(0, n - QT * s) * P
                    r = ring(n, s)
                    dve.wait_ge(turned_high, seen["T"] + 1)
                    nc.vector.tensor_tensor(pT_hl[:, r, 1, c:SPAN], work[:, slot, c:SPAN], f32(pT_hl[:, r, 0, c:SPAN]),
                                            ALU.subtract).then_inc(work_free[slot], 1)
                elif kind == "X" and n < 2:
                    cols = slice(n * SPAN, (n + 1) * SPAN)
                    dve.wait_ge(x_high, 2 * head_of(it, h) + n + 1)
                    nc.vector.tensor_tensor(qa_hl[:, hp, 1, cols], work[:, slot, :], f32(qa_hl[:, hp, 0, cols]),
                                            ALU.subtract).then_inc(work_free[slot], 1)
                elif kind == "X" and n == 3:
                    dve.wait_ge(work_full[slot], seen[slot] + 1)
                    nc.vector.tensor_copy(q_stack[:, hp, SPAN:S], work[:, slot, :]).then_inc(work_free[slot], 1)
                elif kind == "Y":
                    dve.wait_ge(work_full[slot], seen[slot] + 1)
                    dve.wait_ge(inverse_done, seen["Y"] + 1)
                    t = QT * s + n
                    nc.vector.scalar_tensor_tensor(out=out[:, t, :], in0=work[:, slot, :],
                                                   scalar=row[:, 2, row_slot:row_slot + 1], in1=out[:, t, :],
                                                   op0=ALU.mult, op1=ALU.add).then_inc(work_free[slot], 1)
                elif kind == "O":
                    dve.wait_ge(o_high, seen["O"] + 1)
                    nc.vector.tensor_tensor(oT_hl[:, s, 1, :], obank[:, :], f32(oT_hl[:, s, 0, :]),
                                            ALU.subtract).then_inc(o_read, 1)

        each_turn(dve, turns, units, run)
        for i in range(WORK):
            dve.wait_ge(work_free[i], 24 * NH // WORK + 1)

    @block.gpsimd
    def _(pool):
        nc.gpsimd.memset(ones[:, :], 1.0).then_inc(ones_set, 1)
        pool.wait_ge(ones_set, 1)

        def pool_wait(sem, value):
            wait(pool, sem, value)
            pool.sem_inc(passed, 1)

        def run(events, it):
            for kind, h, s, n, seen in events:
                if kind == "G":
                    for i in range(WORK):
                        pool_wait(work_full[i], seen[i])
                    x = src["qpe"][:, :, bass.ds(head_of(it, h) * ROPE, ROPE)]
                    nc.gpsimd.tensor_tensor(q_stage[:, :, 0:ROPE], x, ones[:, :, None].to_broadcast([P, TB, ROPE]),
                                            ALU.mult).then_inc(copied, 1)
                    pool_wait(copied, seen["G"] + 1)
                    nc.gpsimd.tensor_tensor(q_stage[:, :, ROPE:2 * ROPE], x, f32(q_stage[:, :, 0:ROPE]), ALU.subtract
                                            ).then_inc(staged, 1)

        each_turn(pool, turns, units, run)


HT = HG // P
SPANS = NT // QT
WBANKS = 3 * HT


def group_events(half, turn_next=True, quantise_after=False, first=False, last=False):
    ev = []
    banks = iter([("W", half, i, 0) for i in range(WBANKS)] if turn_next else [])
    for sp in range(SPANS):
        for ht in range(HT):
            ev.append(("H", half, sp, ht))
            if sp >= 1:
                ev += [e for e in [next(banks, None)] if e]
            if quantise_after and sp < 3:
                ev.append(("AL"[ht], half, sp, 0))
            before = (half, sp - 1) if sp else (1 - half, SPANS - 1)
            if sp or not first:
                ev += [("D", *before, t) for t in range(ht * QT // HT, (ht + 1) * QT // HT)]
            ev.append(("K", half, sp, ht))
    return ev + ([("D", half, SPANS - 1, t) for t in range(QT)] if last else [])


def each_group(eng, ternary, run):
    kinds = "HKDWAL"
    quantised = lambda half: [(k, half, i, 0) for i in range(3) for k in "AL"] if ternary else []
    opening = quantised(0) + [("W", 1, i, 0) for i in range(WBANKS)] + quantised(1)
    first = group_events(0, quantise_after=ternary, first=True) + group_events(1, quantise_after=ternary)
    body = group_events(0, quantise_after=ternary) + group_events(1, quantise_after=ternary)
    tail = group_events(0) + group_events(1, turn_next=False, last=True)
    count = lambda ev: {k: sum(e[0] == k for e in ev) for k in kinds}
    at = {k: 0 for k in kinds}
    for events, turn in ((opening, None), (first, 0)):
        run(numbered(events, at), turn)
        at = {k: at[k] + count(events)[k] for k in kinds}
    per = count(body)
    with eng.Fori(1, NG // 2 - 1) as it:
        run(numbered(body, {k: at[k] + (it - 1) * per[k] for k in kinds}), it)
    done = NG // 2 - 1
    run(numbered(tail, {k: at[k] + (done - 1) * per[k] for k in kinds}), done)


def feed_forward(nc, m, ident, xT_hl, acc, gate, up, down, ternary=None):
    PARTS = 1 if ternary is not None else 2
    pairs = [(0, 0), (1, 0)] if ternary is not None else [(0, 0), (1, 0), (0, 1)]
    WC = KT * HG
    raw = m.sb("raw", [P, 2, 3, WC])
    wT = m.sb("wT", [P, 2, PARTS, 3, WC], F32R)
    silu = m.sb("silu", [P, HT, SPAN])
    hid = m.sb("hid", [P, HT, SPAN])
    h_hl = m.sb("h_hl", [P, 2, HT, 2, SPAN], F32R)
    gbank = m.ps("gbank", [P, HT, SPAN])
    ubank = m.ps("ubank", [P, HT, SPAN])
    ybank = m.ps("ybank", [P, 2, SPAN])
    if ternary is None:
        wbank, turned_src, turn_ident = m.ps("wbank", [P, 2, SPAN]), raw, ident
    else:
        ident_bf, squares = ternary
        NGR = WC // GROUP
        wbank = m.ps("wbank", [P, 2, 2 * SPAN], BF16)
        quant = m.sb("quant", [P, 2, 3, WC], BF16)
        wb = m.sb("wb", [P, WC], BF16)
        ratio = m.sb("ratio", [P, WC], BF16)
        lower = m.sb("lower", [P, WC], BF16)
        level = m.sb("level", [P, WC], BF16)
        diff = m.sb("diff", [P, WC], BF16)
        total = m.sb("total", [P, NGR])
        mean = m.sb("mean", [P, NGR], BF16)
        scale = m.sb("scale", [P, NGR], BF16)
        inverse = m.sb("inverse", [P, NGR])
        sq = m.sb("sq", [P, SPAN])
        turned_src, turn_ident = quant, ident_bf
    loaded = [m.sem(f"loaded{i}") for i in range(2)]
    zeroed = m.sem("zeroed")
    w_full = m.sem("w_full")
    w_high = m.sem("w_high")
    w_read = m.sem("w_read")
    g_full, u_full = m.sem("g_full"), m.sem("u_full")
    silu_done = m.sem("silu_done")
    hid_done = m.sem("hid_done")
    h_high = m.sem("h_high")
    h_low = m.sem("h_low")
    y_full = m.sem("y_full")
    y_read = m.sem("y_read")
    squared, sq_added = m.sem("squared"), m.sem("sq_added")
    cast_done = m.sem("cast_done")
    q_step = m.sem("q_step")
    inverse_done = m.sem("inverse_done")
    ratio_done = m.sem("ratio_done")
    lower_done, level_done = m.sem("lower_done"), m.sem("level_done")
    l_step = m.sem("l_step")
    quant_done = m.sem("quant_done")

    def blocks(half, i):
        w, sub = divmod(i, HT)
        if w < 2:
            tile = turned_src[:, half, w, :].rearrange("p (h d) -> p h d", h=HT)
            return [tile[:, sub, c * P:(c + 1) * P] for c in range(KT)]
        tile = turned_src[:, half, 2, :].rearrange("p (o c) -> p o c", o=KT)
        return [tile[:, o, sub * P:(sub + 1) * P] for o in range(KT)]

    def turned_to(half, part, i):
        w, sub = divmod(i, HT)
        if w < 2:
            return wT[:, half, part, w, :].rearrange("p (c h) -> p c h", c=KT)[:, :, sub * P:(sub + 1) * P]
        return wT[:, half, part, 2, sub * D:(sub + 1) * D].rearrange("p (c h) -> p c h", c=KT)

    def bank_view(i):
        return wbank[:, i % 2, 0:SPAN].rearrange("p (c h) -> p c h", c=KT)

    block = m.ctx.enter_context(nc.Block())

    @block.sync
    def _(sp):
        def load(g, half, again):
            if again and ternary is None:
                sp.wait_ge(w_full, WBANKS * (g - 1))
            elif again:
                sp.wait_ge(cast_done, 3 * (g - 1))
            for w, src in ((0, gate), (1, up)):
                sp.dma_start(raw[:, half, w, :].rearrange("p (h d) -> p h d", h=HT),
                             src[bass.ds(g * HG, HG), :].rearrange("(h p) d -> p h d", p=P)
                             ).then_inc(loaded[half], 16)
            sp.dma_start(raw[:, half, 2, :].rearrange("p (o c) -> p o c", o=KT),
                         down[:, bass.ds(g * HG, HG)].rearrange("(o p) c -> p o c", p=P)
                         ).then_inc(loaded[half], 16)
        load(0, 0, False)
        load(1, 1, False)
        with sp.Fori(1, NG // 2) as i:
            for half in range(2):
                load(2 * i + half, half, True)

    def load_count(it, half):
        return 48 if it is None else 48 * (it + 1 + half)

    @block.tensor
    def _(pe):
        pe.sem_inc(y_full, 1)

        def run(events, it):
            for kind, half, a, b, seen in events:
                if kind == "W":
                    to = 1 - half
                    if a == 0 and ternary is None:
                        pe.wait_ge(loaded[to], load_count(it, half))
                    elif a == 0:
                        pe.wait_ge(quant_done, 4 if it is None else 3 * (2 * it + half + 2) + 1)
                    pe.wait_ge(w_read, seen["W"] + 1)
                    for c, blk in enumerate(blocks(to, a)):
                        last = pe.transpose(wbank[:, a % 2, c * P:(c + 1) * P], blk, turn_ident[:, :])
                    last.then_inc(w_full, 1)
                elif kind == "H":
                    if a == 0 and b == 0:
                        pe.wait_ge(w_read, seen["W"] + 2)
                    pe.wait_ge(hid_done, seen["H"] + 1)
                    for bank, w, full in ((gbank, 0, g_full), (ubank, 1, u_full)):
                        steps = [(c, xa, wa) for c in range(KT) for xa, wa in pairs]
                        for n, (c, xa, wa) in enumerate(steps):
                            last = pe.matmul(bank[:, b, :], wT[:, half, wa, w, c * HG + b * P:c * HG + (b + 1) * P],
                                             xT_hl[:, xa, c, a * SPAN:(a + 1) * SPAN], start=(n == 0),
                                             stop=(n == len(steps) - 1))
                        last.then_inc(full, 1)
                elif kind == "D":
                    if b == 0:
                        pe.wait_ge(h_low, seen["K"] + HT)
                    pe.wait_ge(y_read, seen["D"] + 1)
                    steps = [(ht, ha, wa) for ht in range(HT) for ha, wa in pairs]
                    for n, (ht, ha, wa) in enumerate(steps):
                        last = pe.matmul(ybank[:, b % 2, :], h_hl[:, a % 2, ht, ha, b * P:(b + 1) * P],
                                         wT[:, half, wa, 2, ht * D:(ht + 1) * D],
                                         start=(n == 0), stop=(n == len(steps) - 1))
                    last.then_inc(y_full, 1)

        each_group(pe, ternary is not None, run)

    @block.scalar
    def _(act):
        if ternary is not None:
            act.sem_inc(w_read, 2)

        def run(events, it):
            for kind, half, a, b, seen in events:
                if kind == "W":
                    act.wait_ge(w_full, seen["W"] + 1)
                    nc.scalar.copy(turned_to(1 - half, 0, a), bank_view(a)
                                   ).then_inc(w_high if ternary is None else w_read, 1)
                elif kind == "H":
                    act.wait_ge(g_full, seen["H"] + 1)
                    nc.scalar.activation(silu[:, b, :], gbank[:, b, :], ACT.Silu).then_inc(silu_done, 1)
                elif kind == "K":
                    act.wait_ge(hid_done, seen["K"] + 1 + HT)
                    if ternary is not None:
                        act.wait_ge(sq_added, seen["K"] + 1)
                        nc.scalar.activation(sq[:, :], hid[:, b, :], ACT.Square).then_inc(squared, 1)
                    wait(act, y_full, seen["D"] + 1 - (b + 1) * QT // HT)
                    nc.scalar.copy(h_hl[:, a % 2, b, 0, :], hid[:, b, :]).then_inc(h_high, 1)
                elif kind == "A":
                    act.wait_ge(loaded[half], 48 if it is None else 48 * (it + 2))
                    act.wait_ge(quant_done, seen["A"] + 1)
                    nc.scalar.copy(wb[:, :], raw[:, half, a, :]).then_inc(cast_done, 1)

        each_group(act, ternary is not None, run)

    @block.vector
    def _(dve):
        if ternary is None:
            dve.sem_inc(w_read, 2)
        else:
            dve.sem_inc(h_low, HT)
        dve.sem_inc(hid_done, HT)
        dve.sem_inc(y_read, 2)
        dve.wait_ge(zeroed, 1)

        def run(events, it):
            for kind, half, a, b, seen in events:
                if kind == "W" and ternary is None:
                    dve.wait_ge(w_high, seen["W"] + 1)
                    nc.vector.tensor_tensor(turned_to(1 - half, 1, a), bank_view(a), f32(turned_to(1 - half, 0, a)),
                                            ALU.subtract).then_inc(w_read, 1)
                elif kind == "H":
                    dve.wait_ge(silu_done, seen["H"] + 1)
                    dve.wait_ge(u_full, seen["H"] + 1)
                    dve.wait_ge(h_low, seen["H"] + 1)
                    nc.vector.tensor_tensor(hid[:, b, :], silu[:, b, :], ubank[:, b, :], ALU.mult
                                            ).then_inc(hid_done, 1)
                elif kind == "K" and ternary is not None:
                    dve.wait_ge(h_high, seen["K"] + 1)
                    nc.vector.tensor_tensor(h_hl[:, a % 2, b, 1, :], hid[:, b, :], f32(h_hl[:, a % 2, b, 0, :]),
                                            ALU.subtract).then_inc(h_low, 1)
                elif kind == "D":
                    dve.wait_ge(y_full, seen["D"] + 1 + 1)
                    y = acc[:, a * QT + b, :]
                    nc.vector.tensor_tensor(y, y, ybank[:, b % 2, :], ALU.add).then_inc(y_read, 1)
                elif kind == "A":
                    dve.wait_ge(cast_done, seen["A"] + 1)
                    nc.vector.tensor_reduce(total[:, :], wb[:, :].rearrange("p (n g) -> p n g", g=GROUP), AX.X,
                                            ALU.add, apply_absolute_value=True).then_inc(q_step, 1)
                    dve.wait_ge(q_step, 3 * seen["A"] + 1)
                    nc.vector.tensor_scalar(mean[:, :], total[:, :], 1.0 / GROUP, None, ALU.mult).then_inc(q_step, 1)
                    dve.wait_ge(q_step, 3 * seen["A"] + 2)
                    nc.vector.tensor_scalar(scale[:, :], mean[:, :], 1e-8, None, ALU.max).then_inc(q_step, 1)
                    dve.wait_ge(q_step, 3 * seen["A"] + 3)
                    nc.vector.reciprocal(inverse[:, :], scale[:, :]).then_inc(inverse_done, 1)
                elif kind == "L":
                    dve.wait_ge(ratio_done, seen["L"] + 1)
                    nc.vector.tensor_scalar(lower[:, :], ratio[:, :], -0.5, None, ALU.is_lt).then_inc(lower_done, 1)
                    dve.wait_ge(lower_done, seen["L"] + 1)
                    nc.vector.scalar_tensor_tensor(out=level[:, :], in0=ratio[:, :], scalar=0.5, in1=lower[:, :],
                                                   op0=ALU.is_gt, op1=ALU.subtract).then_inc(level_done, 1)

        each_group(dve, ternary is not None, run)
        dve.wait_ge(y_read, NG * NT + 2)

    @block.gpsimd
    def _(pool):
        if ternary is None:
            pool.sem_inc(h_low, HT)
        else:
            pool.sem_inc(quant_done, 1)
            pool.sem_inc(sq_added, 1)
            nc.gpsimd.memset(squares[:, :], 0.0).then_inc(squared, 1)
            pool.wait_ge(squared, 1)
        nc.gpsimd.memset(acc[:, :, :], 0.0).then_inc(zeroed, 1)

        def run(events, it):
            for kind, half, a, b, seen in events:
                if kind == "K" and ternary is not None:
                    pool.wait_ge(squared, seen["K"] + 2)
                    tok = slice(a * SPAN, (a + 1) * SPAN)
                    nc.gpsimd.tensor_tensor(squares[:, tok], squares[:, tok], sq[:, :], ALU.add).then_inc(sq_added, 1)
                elif kind == "K":
                    pool.wait_ge(h_high, seen["K"] + 1)
                    nc.gpsimd.tensor_tensor(h_hl[:, a % 2, b, 1, :], hid[:, b, :], f32(h_hl[:, a % 2, b, 0, :]),
                                            ALU.subtract).then_inc(h_low, 1)
                elif kind == "A":
                    pool.wait_ge(inverse_done, seen["A"] + 1)
                    view = lambda x: x[:, :].rearrange("p (n g) -> p n g", g=GROUP)
                    nc.gpsimd.tensor_tensor(view(ratio), view(wb), inverse[:, :, None].to_broadcast([P, NGR, GROUP]),
                                            ALU.mult).then_inc(ratio_done, 1)
                elif kind == "L":
                    pool.wait_ge(level_done, seen["L"] + 1)
                    view = lambda x: x[:, :].rearrange("p (n g) -> p n g", g=GROUP)
                    nc.gpsimd.tensor_tensor(view(ratio), view(level), scale[:, :, None].to_broadcast([P, NGR, GROUP]),
                                            ALU.mult).then_inc(l_step, 1)
                    pool.wait_ge(l_step, 2 * seen["L"] + 1)
                    nc.gpsimd.tensor_tensor(diff[:, :], ratio[:, :], wb[:, :], ALU.subtract).then_inc(l_step, 1)
                    pool.wait_ge(l_step, 2 * seen["L"] + 2)
                    if it is not None:
                        pool.wait_ge(w_full, WBANKS * (2 * it + half + 1))
                    nc.gpsimd.tensor_tensor(quant[:, half, a, :], wb[:, :], diff[:, :], ALU.add
                                            ).then_inc(quant_done, 1)

        each_group(pool, ternary is not None, run)


def scale_rows(nc, m, squares, acc):
    ones = m.sb("ones", [P, 1])
    eps = m.sb("eps", [P, 1])
    root = m.sb("root", [P, NT])
    inv = m.sb("inv", [P, NT])
    bank = m.ps("bank", [P, NT])
    ready, summed, rooted, inverted, scaled = (m.sem(x) for x in ("ready", "summed", "rooted", "inverted", "scaled"))
    with nc.Block() as block:
        @block.vector
        def _(dve):
            nc.vector.memset(ones[:, :], 1.0).then_inc(ready, 1)
            nc.vector.memset(eps[:, :], EPS_F32).then_inc(ready, 1)
            dve.wait_ge(rooted, 1)
            nc.vector.reciprocal(inv[:, :], root[:, :]).then_inc(inverted, 1)
            dve.wait_ge(inverted, 1)
            for t in range(NT):
                nc.vector.tensor_scalar(acc[:, t, :], acc[:, t, :], inv[:, t:t + 1], None, ALU.mult).then_inc(scaled, 1)
            dve.wait_ge(scaled, NT)

        @block.tensor
        def _(pe):
            pe.wait_ge(ready, 2)
            for t in range(NT):
                last = pe.matmul(bank[:, t:t + 1], squares[:, t * P:(t + 1) * P], ones[:, :], start=True, stop=True)
            last.then_inc(summed, 1)

        @block.scalar
        def _(act):
            act.wait_ge(ready, 2)
            act.wait_ge(summed, 1)
            nc.scalar.activation(root[:, :], bank[:, :], ACT.Sqrt, bias=eps[:, 0:1], scale=1.0 / HID).then_inc(rooted, 1)


def absorbed_weights(nc, m, q_nope, k_b, v_b, owT, wabs_dram, wov_dram, stores):
    wabs = m.sb("wabs", [P, 2, 2, 3, LAT], F32R)
    wov = m.sb("wov", [P, 2, 2, D], F32R)
    abank = m.ps("abank", [P, 2, SPAN])
    vbank = m.ps("vbank", [P, 2, SPAN])
    full, high, low = m.sem("full"), m.sem("high"), m.sem("low")
    stored = [m.sem(f"stored{i}") for i in range(2)]
    stores_done = m.sem("stores_done")
    with nc.Block() as block:
        @block.tensor
        def _(pe):
            for h in range(NH):
                wait(pe, low, 2 * (h - 1))
                for j in range(3):
                    last = pe.matmul(abank[:, h % 2, j * P:(j + 1) * P], q_nope[:, h, j * P:(j + 1) * P],
                                     k_b[:, h, :], start=True, stop=True)
                last.then_inc(full, 1)
                pe.matmul(vbank[:, h % 2, :], v_b[:, h, :], owT[:, h, :], start=True, stop=True).then_inc(full, 1)

        def pieces(h):
            par = h % 2
            yield 2 * h, SCALE1, abank[:, par, 0:3 * P].rearrange("p (j c) -> p j c", j=3), wabs[:, par, 0], wabs[:, par, 1]
            yield 2 * h + 1, 1.0, vbank[:, par, :], wov[:, par, 0], wov[:, par, 1]

        @block.scalar
        def _(act):
            for h in range(NH):
                wait(act, stored[h % 2], 32 * (h // 2))
                for n, scale, src, hi, lo in pieces(h):
                    act.wait_ge(full, n + 1)
                    nc.scalar.activation(hi, src, ACT.Copy, scale=scale).then_inc(high, 1)

        @block.vector
        def _(dve):
            for h in range(NH):
                for n, scale, src, hi, lo in pieces(h):
                    dve.wait_ge(high, n + 1)
                    nc.vector.scalar_tensor_tensor(out=lo, in0=src, scalar=scale, in1=f32(hi), op0=ALU.mult,
                                                   op1=ALU.subtract).then_inc(low, 1)

        @block.sync
        def _(sp):
            for dst, tile in stores:
                sp.dma_start(dst, tile).then_inc(stores_done, 16)
            for h in range(NH):
                par = h % 2
                sp.wait_ge(low, 2 * h + 2)
                sp.dma_start(wabs_dram[h], f32(wabs[:, par])).then_inc(stored[par], 16)
                sp.dma_start(wov_dram[h], f32(wov[:, par])).then_inc(stored[par], 16)
            for par in range(2):
                sp.wait_ge(stored[par], 32 * NH // 2)
            sp.wait_ge(stores_done, 16 * len(stores))


def latent_operands(nc, m, ident, xT_hl, waT, wpT, norm_w, rope, out):
    WA = QL + LAT + ROPE
    HW = WA // 2
    down = m.sb("down", [P, 2, WA])
    squares = m.sb("squares", [P, QL])
    sums = m.sb("sums", [P, 2, 2])
    root = m.sb("root", [P, 2, 2])
    inv = m.sb("inv", [P, 2, 2])
    eps = m.sb("eps", [P, 1])
    normed = m.sb("normed", [P, 2, QL + LAT])
    k_parts = m.sb("k_parts", [P, 2, 3, ROPE])
    k_stage = m.sb("k_stage", [P, 2, 2, 2 * ROPE], F32R)
    direct = m.sb("direct", [P, NH * ROPE])
    crossed = m.sb("crossed", [P, NH * ROPE])
    dbank = m.ps("dbank", [P, 2, 2, SPAN])
    tbank = m.ps("tbank", [P, SPAN])
    kbank = m.ps("kbank", [P, 2 * P])
    pbank = m.ps("pbank", [P, 2, SPAN])
    cos, sin = rope
    names = ("eps_set", "d_full", "d_read", "sq_done", "root_done", "inv_done", "norm_done", "k_mul",
             "k_sum", "k_high", "k_staged", "v_high", "v_low", "t_full", "t_high", "t_low", "k_full", "k_read",
             "p_full", "p_read", "p_sum")
    (eps_set, d_full, d_read, sq_done, root_done, inv_done, norm_done, k_mul, k_sum, k_high, k_staged,
     v_high, v_low, t_full, t_high, t_low, k_full, k_read, p_full, p_read, p_sum) = (m.sem(n) for n in names)
    qT_hl, kT_hl, kpe, v_hl, qpe = (out[n] for n in ("qT_hl", "kT_hl", "kpe", "v_hl", "qpe"))
    with nc.Block() as block:
        @block.tensor
        def _(pe):
            for i in range(TB + 2):
                if i < TB:
                    t = i
                    wait(pe, d_read, t - 1)
                    for half in range(2):
                        steps = [(c, a, b) for c in range(KT) for a, b in THREE]
                        for n, (c, a, b) in enumerate(steps):
                            last = pe.matmul(dbank[:, t % 2, half, 0:HW], xT_hl[:, a, c, t * P:(t + 1) * P],
                                             waT[:, b, c, half * HW:(half + 1) * HW],
                                             start=(n == 0), stop=(n == len(steps) - 1))
                    last.then_inc(d_full, 1)
                if 0 <= i - 1 < TB:
                    t = i - 1
                    pe.wait_ge(norm_done, 2 * t + 2)
                    wait(pe, t_low, 2 * t)
                    for c in range(4):
                        last = pe.transpose(tbank[:, c * P:(c + 1) * P], normed[:, t % 2, c * P:(c + 1) * P], ident[:, :])
                    last.then_inc(t_full, 1)
                    pe.wait_ge(k_staged, t + 1)
                    wait(pe, k_read, t)
                    for part in range(2):
                        last = pe.transpose(kbank[:, part * P:(part + 1) * P], f32(k_stage[:, t % 2, part, :]), ident[:, :])
                    last.then_inc(k_full, 1)
                if i >= 2:
                    t = i - 2
                    pe.wait_ge(t_low, 2 * t + 2)
                    wait(pe, p_read, t)
                    for half in range(2):
                        steps = [(j, a, b) for j in range(3) for a, b in THREE]
                        for n, (j, a, b) in enumerate(steps):
                            last = pe.matmul(pbank[:, half, :], qT_hl[:, a, j, t * P:(t + 1) * P],
                                             wpT[:, b, j, half * SPAN:(half + 1) * SPAN],
                                             start=(n == 0), stop=(n == len(steps) - 1))
                    last.then_inc(p_full, 1)

        @block.scalar
        def _(act):
            act.wait_ge(eps_set, 1)
            for i in range(TB + 1):
                if i < TB:
                    t = i
                    act.wait_ge(d_full, t + 1)
                    wait(act, k_sum, t - 1)
                    wait(act, norm_done, 2 * (t - 1))
                    nc.scalar.copy(down[:, t % 2, :].rearrange("p (h c) -> p h c", h=2),
                                   dbank[:, t % 2, :, 0:HW]).then_inc(d_read, 1)
                    act.wait_ge(d_read, t + 1)
                    for n, (a, b) in enumerate(((0, QL), (QL, QL + LAT))):
                        wait(act, sq_done, 2 * t + n)
                        nc.scalar.activation(squares[:, 0:b - a], down[:, t % 2, a:b], ACT.Square,
                                             accum_out=sums[:, t % 2, n:n + 1]).then_inc(sq_done, 1)
                    act.wait_ge(sq_done, 2 * t + 2)
                    for n, size in enumerate((QL, LAT)):
                        nc.scalar.activation(root[:, t % 2, n:n + 1], sums[:, t % 2, n:n + 1], ACT.Sqrt,
                                             bias=eps[:, 0:1], scale=1.0 / size).then_inc(root_done, 1)
                if i >= 1:
                    t = i - 1
                    tok = slice(t * P, (t + 1) * P)
                    act.wait_ge(t_full, t + 1)
                    nc.scalar.copy(qT_hl[:, 0, :, tok], tbank[:, 0:QL].rearrange("p (j t) -> p j t", j=3)).then_inc(t_high, 1)
                    nc.scalar.copy(kT_hl[:, 0, tok], tbank[:, QL:QL + P]).then_inc(t_high, 1)
                    act.wait_ge(k_full, t + 1)
                    nc.scalar.copy(kpe[:, :, tok], kbank[:, :].rearrange("p (a t) -> p a t", a=2)).then_inc(k_read, 1)

        @block.vector
        def _(dve):
            nc.vector.memset(eps[:, :], EPS_RMS).then_inc(eps_set, 1)
            for i in range(TB + 2):
                if i < TB:
                    t = i
                    par = t % 2
                    dve.wait_ge(d_read, t + 1)
                    wait(dve, k_staged, t - 1)
                    key = down[:, par, QL + LAT:WA].rearrange("p (j d) -> p j d", j=2)
                    nc.vector.tensor_tensor(k_parts[:, par, 0, :].rearrange("p (j d) -> p j d", j=2), key,
                                            cos[:, 1, t, None, :].to_broadcast([P, 2, HALF1]), ALU.mult).then_inc(k_mul, 1)
                    for j in range(2):
                        nc.vector.tensor_tensor(k_parts[:, par, 1, j * HALF1:(j + 1) * HALF1], key[:, 1 - j, :],
                                                sin[:, 1, t, j, :], ALU.mult).then_inc(k_mul, 1)
                    dve.wait_ge(root_done, 2 * t + 2)
                    nc.vector.reciprocal(inv[:, par, :], root[:, par, :]).then_inc(inv_done, 1)
                    dve.wait_ge(inv_done, t + 1)
                    wait(dve, t_full, t - 1)
                    wait(dve, v_low, t - 1)
                    for n, (a, b) in enumerate(((0, QL), (QL, QL + LAT))):
                        nc.vector.scalar_tensor_tensor(out=normed[:, par, a:b], in0=down[:, par, a:b],
                                                       scalar=inv[:, par, n:n + 1], in1=norm_w[:, a:b],
                                                       op0=ALU.mult, op1=ALU.mult).then_inc(norm_done, 1)
                if 0 <= i - 1 < TB:
                    t = i - 1
                    tok = slice(t * P, (t + 1) * P)
                    dve.wait_ge(t_high, 2 * t + 2)
                    nc.vector.tensor_tensor(qT_hl[:, 1, :, tok], tbank[:, 0:QL].rearrange("p (j t) -> p j t", j=3),
                                            f32(qT_hl[:, 0, :, tok]), ALU.subtract).then_inc(t_low, 1)
                    nc.vector.tensor_tensor(kT_hl[:, 1, tok], tbank[:, QL:QL + P], f32(kT_hl[:, 0, tok]),
                                            ALU.subtract).then_inc(t_low, 1)
                if i >= 2:
                    t = i - 2
                    dve.wait_ge(p_full, t + 1)
                    wait(dve, p_sum, t)
                    src = pbank[:, :, :].rearrange("p a (h j d) -> p (a h) j d", j=2, d=HALF1)
                    flat = pbank[:, :, :].rearrange("p a (h d) -> p (a h) d", d=HALF1)
                    nc.vector.tensor_tensor(direct[:, :].rearrange("p (h d) -> p h d", d=HALF1), flat,
                                            cos[:, 0, t, None, :].to_broadcast([P, 2 * NH, HALF1]), ALU.mult)
                    dst = crossed[:, :].rearrange("p (h j d) -> p h j d", j=2, d=HALF1)
                    for j in range(2):
                        last = nc.vector.tensor_tensor(dst[:, :, j, :], src[:, :, 1 - j, :],
                                                       sin[:, 0, t, j, None, :].to_broadcast([P, NH, HALF1]), ALU.mult)
                    last.then_inc(p_read, 1)
            dve.wait_ge(t_low, 2 * TB)

        @block.gpsimd
        def _(pool):
            for i in range(TB + 2):
                if i < TB:
                    t = i
                    par = t % 2
                    pool.wait_ge(k_mul, 3 * t + 3)
                    nc.gpsimd.tensor_tensor(k_parts[:, par, 2, :], k_parts[:, par, 0, :], k_parts[:, par, 1, :],
                                            ALU.add).then_inc(k_sum, 1)
                    pool.wait_ge(k_sum, t + 1)
                    wait(pool, k_full, t - 1)
                    for n in range(2):
                        nc.gpsimd.tensor_copy(k_stage[:, par, 0, n * ROPE:(n + 1) * ROPE], k_parts[:, par, 2, :]
                                              ).then_inc(k_high, 1)
                    pool.wait_ge(k_high, 3 * t + 2)
                    nc.gpsimd.tensor_tensor(k_stage[:, par, 1, 0:ROPE], k_parts[:, par, 2, :],
                                            f32(k_stage[:, par, 0, 0:ROPE]), ALU.subtract).then_inc(k_high, 1)
                    pool.wait_ge(k_high, 3 * t + 3)
                    nc.gpsimd.tensor_tensor(k_stage[:, par, 1, ROPE:2 * ROPE], k_parts[:, par, 2, :],
                                            f32(k_stage[:, par, 0, 0:ROPE]), ALU.subtract).then_inc(k_staged, 1)
                    pool.wait_ge(norm_done, 2 * t + 2)
                    nc.gpsimd.tensor_copy(v_hl[:, 0, t, :], normed[:, par, QL:QL + LAT]).then_inc(v_high, 1)
                    pool.wait_ge(v_high, t + 1)
                    nc.gpsimd.tensor_tensor(v_hl[:, 1, t, :], normed[:, par, QL:QL + LAT], f32(v_hl[:, 0, t, :]),
                                            ALU.subtract).then_inc(v_low, 1)
                if i >= 2:
                    t = i - 2
                    pool.wait_ge(p_read, t + 1)
                    nc.gpsimd.tensor_tensor(qpe[:, t, :], direct[:, :], crossed[:, :], ALU.add
                                            ).then_inc(p_sum, 1)


def two_layers(nc, a, out, stop=99):
    from contextlib import contextmanager

    sems = []

    @contextmanager
    def phase(tag):
        with ExitStack() as ctx:
            yield Mem(nc, ctx, tag, sems)

    def clear_semaphores():
        nc.clear_and_free_semaphores(sems)
        sems.clear()
        nc.all_engine_barrier()

    def dram(name, shape, dt=F32):
        return nc.dram_tensor(name, shape, dt, kind="Internal").ap()

    tables = lambda cos, sin, layer: [(dst[:, i], a[f"{name}_{w}{layer}"]) for dst, name in ((cos, "cos"), (sin, "sin"))
                                      for i, w in enumerate("qk")]
    rows = lambda x: x.rearrange("b s d -> (b s) d")
    x0, y_out = rows(a["L0_attn_hidden_states"]), rows(out)
    x1, x2, x3 = (dram(f"x{i}", [NT * P, D]) for i in (1, 2, 3))
    wabs_dram = dram("wabs_dram", [NH, P, 2, 3, LAT])
    wov_dram = dram("wov_dram", [NH, P, 2, D])
    waT_dram = dram("waT_dram", [P, 2, KT, QL + LAT + ROPE])
    wpT_dram = dram("wpT_dram", [P, 2, 3, NH * ROPE])

    with phase("all") as top:
        ident, mask = top.sb("ident", [P, P]), top.sb("mask", [P, P], BF16)
        ident_bf = top.sb("ident_bf", [P, P], BF16)
        with phase("const") as m:
            constants(nc, m, ident, ident_bf, mask)

        view = lambda n: a[n].rearrange("(o p) i -> p o i", p=P)
        with phase("l0") as keep:
            q, k, v = (keep.sb(n, [P, B * KT, TB, P]) for n in "qkv")
            with phase("l0w") as w:
                Wqkv = w.sb("Wqkv", [P, 2, 3, KT, D], F32R)
                with phase("l0wt") as m:
                    raw = m.sb("raw", [P, 3, KT, D])
                    names = ("L0_attn_Wq", "L0_attn_Wk", "L0_attn_Wv")
                    transpose_weights(nc, m, ident, [j for i in range(3) for j in square_jobs(raw[:, i], Wqkv, i, i)],
                                      [(raw[:, i], view(n)) for i, n in enumerate(names)])
                for b in range(B):
                    with phase(f"l0x{b}") as x:
                        xT = x.sb("xT", [P, 2, KT, S], F32R)
                        cos, sin = x.sb("cos", [P, 2, TB, HALF0]), x.sb("sin", [P, 2, TB, 2, HALF0])
                        with phase(f"l0n{b}") as m:
                            norm_transposed(nc, m, ident, x0[b * S:(b + 1) * S], TB, xT, tables(cos, sin, 0))
                        with phase(f"l0p{b}") as m:
                            qkv_layer0(nc, m, b, xT, Wqkv, (cos, sin), q, k, v)
            oT = keep.sb("oT", [P, B * KT, S])
            with phase("l0a") as m:
                attention_layer0(nc, m, ident, ident_bf, mask, q, k, v, oT)
            WoT = keep.sb("WoT", [P, 2, 1, KT, D], F32R)
            with phase("l0ot") as m:
                raw = m.sb("raw", [P, KT, D])
                transpose_weights(nc, m, ident, square_jobs(raw, WoT, 0, 0), [(raw[:, :, :], view("L0_attn_Wo"))])
            with phase("l0o") as m:
                tile_oT = lambda t: oT[:, t // TB * KT:(t // TB + 1) * KT, t % TB * P:(t % TB + 1) * P]
                residual(nc, m, NT, x0, x1, None, attn=(tile_oT, WoT[:, :, 0]))
        clear_semaphores()
        if stop == 1:
            return

        with phase("f0") as keep:
            acc = keep.sb("acc", [P, NT, D])
            with phase("f0x") as x:
                xT = x.sb("xT", [P, 2, KT, NT * P], F32R)
                with phase("f0n") as m:
                    norm_transposed(nc, m, ident, x1, NT, xT)
                with phase("f0f") as m:
                    feed_forward(nc, m, ident, xT, acc, a["L0_ffn_w_gate"], a["L0_ffn_w_up"], a["L0_ffn_w_down"])
            with phase("f0r") as m:
                residual(nc, m, NT, x1, x2, lambda t: acc[:, t, :])
        clear_semaphores()
        if stop == 2:
            return

        with phase("w1") as w:
            q_nope = w.sb("q_nope", [P, NH, QL])
            k_b, v_b = w.sb("k_b", [P, NH, LAT]), w.sb("v_b", [P, NH, LAT])
            owT = w.sb("owT", [P, NH, D])
            waT = w.sb("waT", [P, 2, KT, QL + LAT + ROPE], F32R)
            wpT = w.sb("wpT", [P, 2, 3, NH * ROPE], F32R)
            with phase("w1t") as m:
                qa = m.sb("qa", [P, 3, D])
                kva = m.sb("kva", [P, 2, D])
                qp = m.sb("qp", [P, NH // 2, QL])
                ow = m.sb("ow", [P, KT, NH * VD // 2])
                q_b = a["L1_attn_q_b_w"].rearrange("(h r) j -> r h j", r=QHD)
                kv_b = a["L1_attn_kv_b_w"].rearrange("(h t d) c -> t d h c", t=2, d=NOPE)
                o_w = a["L1_attn_o_w"].rearrange("(o p) v -> p o v", p=P)
                pe_rows = q_b[NOPE:QHD].rearrange("r (n e) j -> e r n j", e=2)
                loads = [(qa[:, :, :], a["L1_attn_q_a_w"].rearrange("(o p) i -> p o i", p=P)),
                         (kva[:, 0, :], a["L1_attn_kv_a_w"][0:P]),
                         (kva[0:ROPE, 1, :], a["L1_attn_kv_a_w"][P:P + ROPE]),
                         (qp[0:ROPE], pe_rows[0]), (qp[ROPE:P], pe_rows[1]),
                         (q_nope[:, :, :], q_b[0:NOPE]), (k_b[:, :, :], kv_b[0]), (v_b[:, :, :], kv_b[1]),
                         (ow[:, :, :], o_w[:, :, 0:NH * VD // 2])]
                jobs = [([(qa[:, i, c * P:(c + 1) * P], i * P) for i in range(3)] + [(kva[:, 0, c * P:(c + 1) * P], 3 * P)],
                         whole(SPAN), waT[:, 0, c, 0:SPAN], waT[:, 1, c, 0:SPAN], 1) for c in range(KT)]
                jobs.append(([(kva[0:ROPE, 1, c * P:(c + 1) * P], c * ROPE) for c in range(KT)],
                             lambda bank: bank[:, 0:KT * ROPE].rearrange("p (c r) -> p c r", c=KT),
                             waT[:, 0, :, SPAN:SPAN + ROPE], waT[:, 1, :, SPAN:SPAN + ROPE], 2))
                jobs += [([(qp[:, 4 * g + i, j * P:(j + 1) * P], i * P) for i in range(4)], whole(SPAN),
                          wpT[:, 0, j, g * SPAN:(g + 1) * SPAN], wpT[:, 1, j, g * SPAN:(g + 1) * SPAN], 4)
                         for j in range(3) for g in range(2)]
                jobs += [([(ow[:, o, h * P:(h + 1) * P], o * P) for o in range(KT)], whole(SPAN), owT[:, h, :], None, 8)
                         for h in range(NH // 2)]
                transpose_weights(nc, m, ident, jobs, loads)
            with phase("w1u") as m:
                ow = m.sb("ow", [P, KT, NH * VD // 2])
                transpose_weights(nc, m, ident,
                                  [([(ow[:, o, h * P:(h + 1) * P], o * P) for o in range(KT)], whole(SPAN),
                                    owT[:, NH // 2 + h, :], None, 0) for h in range(NH // 2)],
                                  [(ow[:, :, :], o_w[:, :, NH * VD // 2:])])
            with phase("w1a") as m:
                absorbed_weights(nc, m, q_nope, k_b, v_b, owT, wabs_dram, wov_dram,
                                 [(waT_dram, f32(waT[:, :, :, :])), (wpT_dram, f32(wpT[:, :, :, :]))])
        clear_semaphores()
        for b in range(B):
            with phase(f"l1_{b}") as keep:
                acc = keep.sb("acc", [P, TB, D])
                with phase(f"l1k{b}") as mid:
                    ops = {"qT_hl": mid.sb("qT_hl", [P, 2, 3, S], F32R), "kT_hl": mid.sb("kT_hl", [P, 2, S], F32R),
                           "kpe": mid.sb("kpe", [P, 2, S], F32R), "v_hl": mid.sb("v_hl", [P, 2, TB, LAT], F32R),
                           "qpe": mid.sb("qpe", [P, TB, NH * ROPE]), "wabs_dram": wabs_dram, "wov_dram": wov_dram}
                    with phase(f"l1x{b}") as x:
                        xT = x.sb("xT", [P, 2, KT, S], F32R)
                        cos, sin = x.sb("cos", [P, 2, TB, HALF1]), x.sb("sin", [P, 2, TB, 2, HALF1])
                        waT = x.sb("waT", [P, 2, KT, QL + LAT + ROPE], F32R)
                        wpT = x.sb("wpT", [P, 2, 3, NH * ROPE], F32R)
                        norm_w = x.sb("norm_w", [P, QL + LAT])
                        operands = [(f32(waT[:, :, :, :]), waT_dram), (f32(wpT[:, :, :, :]), wpT_dram),
                                    (norm_w[:, 0:QL], a["L1_attn_q_a_ln_w"].partition_broadcast(P)),
                                    (norm_w[:, QL:QL + LAT], a["L1_attn_kv_a_ln_w"].partition_broadcast(P))]
                        with phase(f"l1n{b}") as m:
                            norm_transposed(nc, m, ident, x2[b * S:(b + 1) * S], TB, xT,
                                            tables(cos, sin, 1) + operands)
                        with phase(f"l1p{b}") as m:
                            latent_operands(nc, m, ident, xT, waT, wpT, norm_w, (cos, sin), ops)
                    with phase(f"l1a{b}") as m:
                        attention_layer1(nc, m, ident, ident_bf, mask, ops, acc)
                with phase(f"l1r{b}") as m:
                    residual(nc, m, TB, x2[b * S:(b + 1) * S], x3[b * S:(b + 1) * S], lambda t: acc[:, t, :])
            clear_semaphores()
        if stop == 3:
            return

        with phase("f1") as keep:
            acc = keep.sb("acc", [P, NT, D])
            with phase("f1x") as x:
                squares = x.sb("squares", [P, NT * P])
                xT = x.sb("xT", [P, 2, KT, NT * P], F32R)
                with phase("f1n") as m:
                    norm_transposed(nc, m, ident, x3, NT, xT)
                with phase("f1f") as m:
                    w = a["L1_ffn_w_gate_up"]
                    feed_forward(nc, m, ident, xT, acc, w[0:HID], w[HID:2 * HID], a["L1_ffn_w_proj"],
                                 (ident_bf, squares))
                with phase("f1s") as m:
                    scale_rows(nc, m, squares, acc)
            with phase("f1r") as m:
                residual(nc, m, NT, x3, y_out, lambda t: acc[:, t, :])
        clear_semaphores()


_INS = ['L0_attn_hidden_states', 'L0_attn_Wq', 'L0_attn_Wk', 'L0_attn_Wv', 'L0_attn_Wo', 'L0_ffn_w_gate',
        'L0_ffn_w_up', 'L0_ffn_w_down', 'L1_attn_q_a_w', 'L1_attn_q_a_ln_w', 'L1_attn_q_b_w', 'L1_attn_kv_a_w',
        'L1_attn_kv_a_ln_w', 'L1_attn_kv_b_w', 'L1_attn_o_w', 'L1_ffn_w_gate_up', 'L1_ffn_w_proj']


def rotary_tables(width, scale):
    freq = (1.0 / 10000.0 ** (np.arange(0, width, 2, dtype=np.float32) / width)).astype(np.float32)
    angle = np.outer(np.arange(S, dtype=np.float32), freq).astype(np.float32)
    tiles = lambda x: x.astype(np.float32).reshape(TB, P, width // 2).transpose(1, 0, 2)
    cos, sin = tiles(np.cos(angle) * np.float32(scale)), tiles(np.sin(angle) * np.float32(scale))
    return np.ascontiguousarray(cos), np.ascontiguousarray(np.stack([-sin, sin], axis=2))


def kernel(**inputs):
    import concourse.bacc as _bacc
    from concourse.bass_utils import run_bass_kernel_spmd as _run

    nc = _bacc.Bacc("TRN2", target_bir_lowering=False, num_devices=1)
    host = {n: np.ascontiguousarray(inputs[n]) for n in _INS}
    for i, (width, scale) in enumerate(((HD0, SCALE0), (ROPE, SCALE1))):
        host[f"cos_k{i}"], host[f"sin_k{i}"] = rotary_tables(width, 1.0)
        host[f"cos_q{i}"], host[f"sin_q{i}"] = rotary_tables(width, scale)
    aps = {n: nc.dram_tensor(f"in_{n}", x.shape, mybir.dt.from_np(x.dtype), kind="ExternalInput").ap()
           for n, x in host.items()}
    out = nc.dram_tensor("out_0", (B, S, D), F32, kind="ExternalOutput").ap()
    two_layers(nc, aps, out)
    r = _run(nc, [{f"in_{n}": x for n, x in host.items()}], core_ids=[0])
    return r.results[0]["out_0"]
```

```python
from contextlib import ExitStack

import numpy as np

import concourse.bass as bass
from concourse import mybir

F32 = mybir.dt.float32
F32R = mybir.dt.float32r
BF16 = mybir.dt.bfloat16
ACT = mybir.ActivationFunctionType
ALU = mybir.AluOpType
AX = mybir.AxisListType

P = 128
D = 512
KT = D // P
B, S = 2, 1024
TB = S // P
NT = B * TB
SPAN = 512
QT = SPAN // P
EPS_LN = 1e-5
MASKED = -1e30

NH = 16
HD0 = D // NH
HALF0 = HD0 // 2
HID = 4 * D
HG = 256
NG = HID // HG
NOPE, ROPE, VD, LAT, QL = 128, 64, 128, 128, 384
QHD = NOPE + ROPE
HALF1 = ROPE // 2
EPS_RMS = 1e-6
SCALE0, SCALE1 = float(HD0) ** -0.5, float(QHD) ** -0.5
EPS_F32 = float(np.finfo(np.float32).eps)
GROUP = 64
THREE = [(0, 0), (0, 1), (1, 0)]


def wait(eng, sem, value):
    if isinstance(value, int) and value <= 0:
        return
    eng.wait_ge(sem, value)


class Mem:

    def __init__(self, nc, ctx, tag, sems):
        self.nc, self.ctx, self.tag, self.sems = nc, ctx, tag, sems

    def sb(self, name, shape, dt=F32, side="left"):
        return self.ctx.enter_context(self.nc.sbuf_tensor(f"{self.tag}_{name}", shape, dt, side=side))

    def ps(self, name, shape, dt=F32):
        return self.ctx.enter_context(self.nc.psum_tensor(f"{self.tag}_{name}", shape, dt))

    def sem(self, name):
        handle = self.nc.alloc_semaphore(name=f"{self.tag}_{name}")
        self.sems.append(handle)
        return handle


def f32(ap):
    return ap.bitcast(F32)


def constants(nc, m, ident, ident_bf, mask_bf):
    mask = m.sb("mask", [P, P])
    zeroed, made = m.sem("zeroed"), m.sem("made")
    with nc.Block() as block:
        @block.gpsimd
        def _(pool):
            nc.gpsimd.memset(ident[:, :], 0.0).then_inc(zeroed, 1)
            nc.gpsimd.memset(mask[:, :], 0.0).then_inc(zeroed, 1)
            pool.wait_ge(zeroed, 2)
            nc.gpsimd.affine_select(out=ident[:, :], in_=ident[:, :], compare_op=ALU.not_equal, fill=1.0,
                                    base=0, pattern=[[-1, P]], channel_multiplier=1).then_inc(made, 1)
            nc.gpsimd.affine_select(out=mask[:, :], in_=mask[:, :], compare_op=ALU.is_ge, fill=MASKED,
                                    base=0, pattern=[[-1, P]], channel_multiplier=1).then_inc(made, 1)
            pool.wait_ge(made, 2)
            nc.gpsimd.tensor_copy(ident_bf[:, :], ident[:, :]).then_inc(made, 1)
            nc.gpsimd.tensor_copy(mask_bf[:, :], mask[:, :]).then_inc(made, 1)
            pool.wait_ge(made, 4)


def transpose_weights(nc, m, ident, jobs, loads, stores=()):
    RING = 4
    bank = m.ps("bank", [P, RING, SPAN])
    loaded = [m.sem(f"loaded{i}") for i in range(len(loads))]
    turned, high_done, low_done, stored = (m.sem(n) for n in ("turned", "high_done", "low_done", "stored"))
    with nc.Block() as block:
        @block.sync
        def _(sp):
            for i, (dst, src) in enumerate(loads):
                sp.dma_start(dst, src).then_inc(loaded[i], 16)
            for dst, tile in stores:
                sp.dma_start(dst, tile).then_inc(stored, 16)
            wait(sp, stored, 16 * len(stores))

        @block.tensor
        def _(pe):
            have = -1
            for n, (blocks, view, hi, lo, need) in enumerate(jobs):
                if need > have:
                    for i in range(have + 1, need + 1):
                        pe.wait_ge(loaded[i], 16)
                    have = need
                wait(pe, low_done, n - RING + 1)
                for src, off in blocks:
                    rows, cols = src.shape[0], src.shape[1]
                    last = pe.transpose(bank[0:cols, n % RING, off:off + rows], src, ident[0:rows, 0:rows])
                last.then_inc(turned, 1)

        @block.scalar
        def _(act):
            for n, (blocks, view, hi, lo, need) in enumerate(jobs):
                if lo is not None:
                    act.wait_ge(turned, n + 1)
                    nc.scalar.copy(hi, view(bank[:, n % RING])).then_inc(high_done, 1)

        @block.vector
        def _(dve):
            for n, (blocks, view, hi, lo, need) in enumerate(jobs):
                if lo is None:
                    dve.wait_ge(turned, n + 1)
                    nc.vector.tensor_copy(hi, view(bank[:, n % RING])).then_inc(low_done, 1)
                else:
                    dve.wait_ge(high_done, n + 1)
                    nc.vector.tensor_tensor(lo, view(bank[:, n % RING]), f32(hi),
                                            ALU.subtract).then_inc(low_done, 1)
            dve.wait_ge(low_done, len(jobs))


def whole(cols):
    return lambda bank: bank[:, 0:cols]


def square_jobs(raw, dst_hl, w, need):
    return [([(raw[:, o, k * P:(k + 1) * P], o * P) for o in range(KT)], whole(D),
             dst_hl[:, 0, w, k, :], dst_hl[:, 1, w, k, :], need) for k in range(KT)]


def norm_transposed(nc, m, ident, src, tiles, xT_hl, loads=()):
    x = m.sb("x", [P, tiles, D])
    RING, LAG = 4, 2
    xn = m.sb("xn", [P, RING, D])
    stats = m.sb("stats", [P, tiles, 6])
    mv = m.sb("mv", [P, tiles, 2])
    std = m.sb("std", [P, tiles])
    rstd = m.sb("rstd", [P, tiles])
    eps = m.sb("eps", [P, 1])
    bank = m.ps("bank", [P, RING, SPAN])
    groups = tiles // QT
    loaded = [m.sem(f"loaded{g}") for g in range(groups)]
    next_loaded = m.sem("next_loaded")
    stats_done, mv_done, std_done, rstd_done = (m.sem(x) for x in ("stats_done", "mv_done", "std_done", "rstd_done"))
    normed, turned, high_done, low_done, eps_set = (
        m.sem(x) for x in ("normed", "turned", "high_done", "low_done", "eps_set"))
    with nc.Block() as block:
        @block.sync
        def _(sp):
            for g in range(groups):
                rows = src[g * SPAN:(g + 1) * SPAN, :].rearrange("(t p) d -> p t d", p=P)
                sp.dma_start(x[:, g * QT:(g + 1) * QT, :], rows).then_inc(loaded[g], 16)
            for dst, extra in loads:
                sp.dma_start(dst, extra).then_inc(next_loaded, 16)
            wait(sp, next_loaded, 16 * len(loads))

        @block.vector
        def _(dve):
            def statistics(g):
                dve.wait_ge(loaded[g], 16)
                for t in range(g * QT, (g + 1) * QT):
                    nc.vector.bn_stats(stats[:, t, :], x[:, t, :]).then_inc(stats_done, 1)
                for t in range(g * QT, (g + 1) * QT):
                    dve.wait_ge(stats_done, t + 1)
                    nc.vector.bn_aggr(mv[:, t, :], stats[:, t, :]).then_inc(mv_done, 1)

            nc.vector.memset(eps[:, :], EPS_LN).then_inc(eps_set, 1)
            statistics(0)
            for g in range(groups):
                if g + 1 < groups:
                    statistics(g + 1)
                a, b = g * QT, (g + 1) * QT
                dve.wait_ge(std_done, g + 1)
                nc.vector.reciprocal(rstd[:, a:b], std[:, a:b]).then_inc(rstd_done, 1)
                dve.wait_ge(rstd_done, g + 1)
                for t in range(a, b + (LAG if b == tiles else 0)):
                    if t < tiles:
                        wait(dve, turned, t - RING + 1)
                        nc.vector.tensor_scalar(xn[:, t % RING, :], x[:, t, :], mv[:, t, 0:1], rstd[:, t:t + 1],
                                                ALU.subtract, ALU.mult).then_inc(normed, 1)
                    if t >= LAG:
                        u = t - LAG
                        dve.wait_ge(high_done, u + 1)
                        low = xT_hl[:, 1, :, u * P:(u + 1) * P]
                        nc.vector.tensor_tensor(low, bank[:, u % RING, :].rearrange("p (k t) -> p k t", k=KT),
                                                f32(xT_hl[:, 0, :, u * P:(u + 1) * P]),
                                                ALU.subtract).then_inc(low_done, 1)
            dve.wait_ge(low_done, tiles)

        @block.scalar
        def _(act):
            act.wait_ge(eps_set, 1)

            def root(g):
                act.wait_ge(mv_done, (g + 1) * QT)
                a, b = g * QT, (g + 1) * QT
                nc.scalar.activation(std[:, a:b], mv[:, a:b, 1], ACT.Sqrt, bias=eps[:, 0:1]).then_inc(std_done, 1)

            root(0)
            for g in range(groups):
                if g + 1 < groups:
                    root(g + 1)
                for t in range(g * QT, (g + 1) * QT):
                    act.wait_ge(turned, t + 1)
                    nc.scalar.copy(xT_hl[:, 0, :, t * P:(t + 1) * P],
                                   bank[:, t % RING, :].rearrange("p (k t) -> p k t", k=KT)).then_inc(high_done, 1)

        @block.tensor
        def _(pe):
            for t in range(tiles):
                pe.wait_ge(normed, t + 1)
                wait(pe, low_done, t - RING + 1)
                for k in range(KT):
                    last = pe.transpose(bank[:, t % RING, k * P:(k + 1) * P], xn[:, t % RING, k * P:(k + 1) * P],
                                        ident[:, :])
                last.then_inc(turned, 1)


def residual(nc, m, tiles, src, dst, y_of):
    RING, LAG = 4, 2
    x = m.sb("x", [P, 2 * QT, D])
    stats = m.sb("stats", [P, RING, 6])
    mv = m.sb("mv", [P, RING, 2])
    std = m.sb("std", [P, RING])
    rstd = m.sb("rstd", [P, RING])
    z = m.sb("z", [P, RING, D])
    eps = m.sb("eps", [P, 1])
    loaded = [m.sem(f"loaded{i}") for i in range(2)]
    stored = [m.sem(f"stored{i}") for i in range(RING)]
    names = ("stats_done", "mv_done", "std_done", "rstd_done", "z_done", "sum_done", "eps_set")
    stats_done, mv_done, std_done, rstd_done, z_done, sum_done, eps_set = (m.sem(n) for n in names)
    with nc.Block() as block:
        @block.sync
        def _(sp):
            def load(g):
                sp.dma_start(x[:, g % 2 * QT:(g % 2 + 1) * QT, :],
                             src[g * SPAN:(g + 1) * SPAN, :].rearrange("(t p) d -> p t d", p=P)
                             ).then_inc(loaded[g % 2], 16)

            load(0)
            load(1)
            for t in range(tiles):
                sp.wait_ge(sum_done, t + 1)
                sp.dma_start(dst[t * P:(t + 1) * P, :], z[:, t % RING, :]).then_inc(stored[t % RING], 16)
                if t % QT == QT - 1 and t // QT + 2 < tiles // QT:
                    load(t // QT + 2)
            for i in range(RING):
                sp.wait_ge(stored[i], 16 * (tiles // RING))

        @block.scalar
        def _(act):
            act.wait_ge(eps_set, 1)
            for t in range(tiles):
                r = t % RING
                act.wait_ge(mv_done, t + 1)
                nc.scalar.activation(std[:, r:r + 1], mv[:, r, 1:2], ACT.Sqrt, bias=eps[:, 0:1]).then_inc(std_done, 1)

        @block.vector
        def _(dve):
            nc.vector.memset(eps[:, :], EPS_LN).then_inc(eps_set, 1)

            for t in range(tiles + LAG):
                if t < tiles:
                    r = t % RING
                    nc.vector.bn_stats(stats[:, r, :], y_of(t)).then_inc(stats_done, 1)
                    dve.wait_ge(stats_done, t + 1)
                    nc.vector.bn_aggr(mv[:, r, :], stats[:, r, :]).then_inc(mv_done, 1)
                if t >= LAG:
                    u = t - LAG
                    r = u % RING
                    dve.wait_ge(std_done, u + 1)
                    nc.vector.reciprocal(rstd[:, r:r + 1], std[:, r:r + 1]).then_inc(rstd_done, 1)
                    dve.wait_ge(rstd_done, u + 1)
                    wait(dve, stored[r], 16 * (u // RING))
                    nc.vector.tensor_scalar(z[:, r, :], y_of(u), mv[:, r, 0:1], rstd[:, r:r + 1],
                                            ALU.subtract, ALU.mult).then_inc(z_done, 1)

        @block.gpsimd
        def _(pool):
            for t in range(tiles):
                r = t % RING
                pool.wait_ge(z_done, t + 1)
                g = t // QT
                pool.wait_ge(loaded[g % 2], 16 * (g // 2 + 1))
                nc.gpsimd.tensor_tensor(z[:, r, :], z[:, r, :], x[:, t % (2 * QT), :], ALU.add
                                            ).then_inc(sum_done, 1)


def project_residual_norm(nc, m, ident, tiles, src, dst, oT, WoT_hl, xT_hl):
    RING = 4
    x = m.sb("x", [P, 2 * QT, D])
    z = m.sb("z", [P, RING, D])
    xn = m.sb("xn", [P, 2, D])
    ot_hl = m.sb("ot_hl", [P, RING, 2, KT, P], F32R)
    stats, mv = m.sb("stats", [P, 2, RING, 6]), m.sb("mv", [P, 2, RING, 2])
    std, rstd = m.sb("std", [P, 2, RING]), m.sb("rstd", [P, 2, RING])
    eps = m.sb("eps", [P, 1])
    ybank = m.ps("ybank", [P, RING, SPAN])
    tbank = m.ps("tbank", [P, RING, SPAN])
    loaded = [m.sem(f"loaded{i}") for i in range(2)]
    stored = [m.sem(f"stored{i}") for i in range(RING)]
    eps_set, o_high, o_low, y_full, z_done, sum_done, normed, turned, high_done, low_done = (m.sem(n) for n in (
        "eps_set", "o_high", "o_low", "y_full", "z_done", "sum_done", "normed", "turned", "high_done", "low_done"))
    stats_done, mv_done, std_done, rstd_done = ([m.sem(f"{n}{i}") for i in range(2)] for n in (
        "stats_done", "mv_done", "std_done", "rstd_done"))
    with nc.Block() as block:
        @block.sync
        def _(sp):
            def load(g):
                sp.dma_start(x[:, g % 2 * QT:(g % 2 + 1) * QT, :],
                             src[g * SPAN:(g + 1) * SPAN, :].rearrange("(t p) d -> p t d", p=P)
                             ).then_inc(loaded[g % 2], 16)

            load(0)
            load(1)
            for t in range(tiles):
                sp.wait_ge(sum_done, t + 1)
                sp.dma_start(dst[t * P:(t + 1) * P, :], z[:, t % RING, :]).then_inc(stored[t % RING], 16)
                if t % QT == QT - 1 and t // QT + 2 < tiles // QT:
                    load(t // QT + 2)
            for i in range(RING):
                sp.wait_ge(stored[i], 16 * (tiles // RING))

        @block.tensor
        def _(pe):
            for i in range(tiles + 5):
                if i < tiles:
                    t = i
                    pe.wait_ge(o_low, t + 1)
                    wait(pe, z_done, t - RING + 1)
                    steps = [(g, a, b) for g in range(KT) for a, b in THREE]
                    for n, (g, a, b) in enumerate(steps):
                        last = pe.matmul(ybank[:, t % RING, :], ot_hl[:, t % RING, a, g, :], WoT_hl[:, b, g, :],
                                         start=(n == 0), stop=(n == len(steps) - 1))
                    last.then_inc(y_full, 1)
                if i >= 5:
                    t = i - 5
                    pe.wait_ge(normed, t + 1)
                    wait(pe, low_done, t - RING + 1)
                    for k in range(KT):
                        last = pe.transpose(tbank[:, t % RING, k * P:(k + 1) * P], xn[:, t % 2, k * P:(k + 1) * P],
                                            ident[:, :])
                    last.then_inc(turned, 1)

        @block.scalar
        def _(act):
            act.wait_ge(eps_set, 1)

            def root(which, t):
                r = t % RING
                act.wait_ge(mv_done[which], t + 1)
                nc.scalar.activation(std[:, which, r:r + 1], mv[:, which, r, 1:2], ACT.Sqrt,
                                     bias=eps[:, 0:1]).then_inc(std_done[which], 1)

            def high(t):
                if t < tiles:
                    wait(act, y_full, t - RING + 1)
                    nc.scalar.copy(ot_hl[:, t % RING, 0], oT(t)).then_inc(o_high, 1)

            for t in range(3):
                high(t)
            for i in range(tiles + 6):
                if 0 <= i - 4 < tiles:
                    root(1, i - 4)
                if 0 <= i - 1 < tiles:
                    root(0, i - 1)
                if 0 <= i - 6 < tiles:
                    t = i - 6
                    act.wait_ge(turned, t + 1)
                    nc.scalar.copy(xT_hl[:, 0, :, t * P:(t + 1) * P],
                                   tbank[:, t % RING, :].rearrange("p (k t) -> p k t", k=KT)).then_inc(high_done, 1)
                high(i + 3)

        @block.vector
        def _(dve):
            nc.vector.memset(eps[:, :], EPS_LN).then_inc(eps_set, 1)

            def statistics(which, t, y):
                r = t % RING
                nc.vector.bn_stats(stats[:, which, r, :], y).then_inc(stats_done[which], 1)

            def aggregate(which, t):
                r = t % RING
                dve.wait_ge(stats_done[which], t + 1)
                nc.vector.bn_aggr(mv[:, which, r, :], stats[:, which, r, :]).then_inc(mv_done[which], 1)

            def inverse(which, t):
                r = t % RING
                dve.wait_ge(std_done[which], t + 1)
                nc.vector.reciprocal(rstd[:, which, r:r + 1], std[:, which, r:r + 1]).then_inc(rstd_done[which], 1)
                dve.wait_ge(rstd_done[which], t + 1)

            for i in range(tiles + 6):
                if 0 <= i - 4 < tiles:
                    t, r = i - 4, (i - 4) % RING
                    inverse(1, t)
                    wait(dve, turned, t - 1)
                    nc.vector.tensor_scalar(xn[:, t % 2, :], z[:, r, :], mv[:, 1, r, 0:1], rstd[:, 1, r:r + 1],
                                            ALU.subtract, ALU.mult).then_inc(normed, 1)
                if 0 <= i - 3 < tiles:
                    dve.wait_ge(sum_done, i - 2)
                    statistics(1, i - 3, z[:, (i - 3) % RING, :])
                if 0 <= i - 6 < tiles:
                    t = i - 6
                    dve.wait_ge(high_done, t + 1)
                    nc.vector.tensor_tensor(xT_hl[:, 1, :, t * P:(t + 1) * P],
                                            tbank[:, t % RING, :].rearrange("p (k t) -> p k t", k=KT),
                                            f32(xT_hl[:, 0, :, t * P:(t + 1) * P]), ALU.subtract).then_inc(low_done, 1)
                if 0 <= i - 3 < tiles:
                    aggregate(1, i - 3)
                if i < tiles:
                    dve.wait_ge(y_full, i + 1)
                    statistics(0, i, ybank[:, i % RING, :])
                if 0 <= i - 1 < tiles:
                    t, r = i - 1, (i - 1) % RING
                    inverse(0, t)
                    wait(dve, stored[r], 16 * (t // RING))
                    nc.vector.tensor_scalar(z[:, r, :], ybank[:, r, :], mv[:, 0, r, 0:1], rstd[:, 0, r:r + 1],
                                            ALU.subtract, ALU.mult).then_inc(z_done, 1)
                if i < tiles:
                    aggregate(0, i)
            dve.wait_ge(low_done, tiles)

        @block.gpsimd
        def _(pool):
            for i in range(-2, tiles + 1):
                if i + 2 < tiles:
                    t = i + 2
                    pool.wait_ge(o_high, t + 1)
                    nc.gpsimd.tensor_tensor(ot_hl[:, t % RING, 1], oT(t), f32(ot_hl[:, t % RING, 0]), ALU.subtract
                                            ).then_inc(o_low, 1)
                if 0 <= i - 1 < tiles:
                    t = i - 1
                    r, g = t % RING, t // QT
                    pool.wait_ge(z_done, t + 1)
                    pool.wait_ge(loaded[g % 2], 16 * (g // 2 + 1))
                    nc.gpsimd.tensor_tensor(z[:, r, :], z[:, r, :], x[:, t % (2 * QT), :], ALU.add
                                            ).then_inc(sum_done, 1)


def qkv_layer0(nc, m, batch, xT_hl, W_hl, rope, q, k, v):
    bank = m.ps("bank", [P, 2, 3, SPAN])
    direct = m.sb("direct", [P, 2, 2, D])
    crossed = m.sb("crossed", [P, 2, 2, D])
    cos, sin = rope
    full = [m.sem(f"full_{n}") for n in "qkv"]
    read = [m.sem(f"read_{n}") for n in "qkv"]
    rotated = m.sem("rotated")
    with nc.Block() as block:
        @block.tensor
        def _(pe):
            for t in range(TB):
                for w in range(3):
                    wait(pe, read[w], t - 1)
                    steps = [(c, xa, wa) for c in range(KT) for xa, wa in THREE]
                    for n, (c, xa, wa) in enumerate(steps):
                        last = pe.matmul(bank[:, t % 2, w, :], xT_hl[:, xa, c, t * P:(t + 1) * P],
                                         W_hl[:, wa, w, c, :], start=(n == 0), stop=(n == len(steps) - 1))
                    last.then_inc(full[w], 1)

        @block.vector
        def _(dve):
            for t in range(TB):
                tt = t
                for w in range(2):
                    src = bank[:, t % 2, w, :].rearrange("p (h j d) -> p h j d", h=NH, j=2)
                    dve.wait_ge(full[w], t + 1)
                    wait(dve, rotated, 2 * (t - 1) + w - 1)
                    cb = cos[:, w, tt, None, :].to_broadcast([P, 2 * NH, HALF0])
                    nc.vector.tensor_tensor(direct[:, t % 2, w, :].rearrange("p (h d) -> p h d", d=HALF0),
                                            bank[:, t % 2, w, :].rearrange("p (h d) -> p h d", d=HALF0),
                                            cb, ALU.mult)
                    dst = crossed[:, t % 2, w, :].rearrange("p (h j d) -> p h j d", h=NH, j=2)
                    for j in range(2):
                        sb = sin[:, w, tt, j, None, :].to_broadcast([P, NH, HALF0])
                        last = nc.vector.tensor_tensor(dst[:, :, j, :], src[:, :, 1 - j, :], sb, ALU.mult)
                    last.then_inc(read[w], 1)

        @block.gpsimd
        def _(pool):
            for t in range(TB):
                b, tt = batch, t
                for w, out in enumerate((q, k)):
                    pool.wait_ge(read[w], t + 1)
                    view = lambda x: x[:, t % 2, w, :].rearrange("p (g d) -> p g d", g=KT)
                    nc.gpsimd.tensor_tensor(out[:, b * KT:(b + 1) * KT, tt, :], view(direct), view(crossed),
                                            ALU.add).then_inc(rotated, 1)

        @block.scalar
        def _(act):
            for t in range(TB):
                b, tt = batch, t
                act.wait_ge(full[2], t + 1)
                nc.scalar.copy(v[:, b * KT:(b + 1) * KT, tt, :],
                               bank[:, t % 2, 2, :].rearrange("p (g d) -> p g d", g=KT)).then_inc(read[2], 1)


KINDS0 = "XCMENDZLPOIQGV"
GROUP_HEADS = 4
STEPS = 3 * QT
AHEAD = 2
RING0 = 4
MAX_PARTS = [(t, c) for t in range(TB) for c in range(0, (t + 1) * P, SPAN)]
M_AT = [0, 3, 2, 1, 1, 1, 1, 1, 1, 1, 0, 0]
E_AT, N_AT, D_AT = (4, 10), (6, 11), 7
O_AT = (5, 1)
I_AT = (2, 8)
G_AT, V_AT = (1, 4), 6
POOL_LOWS = (1, 4, 7, 9, 10)


def step_of(k):
    s, kt = (0, k) if k < QT else (1, k - QT)
    return s, kt, max(0, kt - QT * s) * P, kt >= QT * s


def head_events(h, last_head=None):
    more = lambda head: last_head is None or head <= last_head
    parts = iter(range(len(MAX_PARTS)))
    for k in range(STEPS):
        if k == 0:
            yield "D", h, 1
        if k in (10, 11) and more(h + 2):
            yield from [("C", h + 2, 2 * (k - 10)), ("C", h + 2, 2 * (k - 10) + 1)]
        if k == D_AT and more(h + 1):
            yield "D", h + 1, 0
        j = k + AHEAD
        if more(h + j // STEPS):
            yield "Z", h + j // STEPS, j % STEPS
        j -= 1
        if more(h + j // STEPS):
            yield "L", h + j // STEPS, j % STEPS
        if k in G_AT and more(h + 2):
            yield "G", h + 2, G_AT.index(k)
        if k == V_AT and more(h + 1):
            yield "V", h + 1, 0
        if more(h + 1):
            for _ in range(M_AT[k]):
                yield "M", h + 1, next(parts)
            if k in E_AT:
                yield "E", h + 1, E_AT.index(k)
            if k in N_AT:
                yield "N", h + 1, N_AT.index(k)
        if more(h + 2):
            if k in (9, 10):
                yield from [("X", h + 2, 2 * (k - 9)), ("X", h + 2, 2 * (k - 9) + 1)]
        if k == O_AT[1] and h > 0:
            yield "O", h - 1, 1
        if k in I_AT and h >= GROUP_HEADS:
            yield "I", h, 2 * (h % GROUP_HEADS) + I_AT.index(k)
        if k == STEPS - 1 and h >= GROUP_HEADS and h % 2:
            yield "Q", h, h % GROUP_HEADS // 2
        if k == O_AT[0]:
            yield "O", h, 0
        yield "P", h, k
    if last_head == h:
        yield "O", h, 1
        for n in range(8):
            yield "I", h + 1, n
            if n % 4 == 3:
                yield "Q", h + 1, n // 4


def opening_events():
    yield from [("G", 0, 0), ("G", 0, 1), ("V", 0, 0)]
    for n in range(4):
        yield from [("X", 0, n), ("C", 0, n)]
    yield from [("G", 1, 0), ("G", 1, 1)]
    for n in range(len(MAX_PARTS)):
        yield "M", 0, n
        if n == QT - 1:
            yield from [("E", 0, 0), ("N", 0, 0), ("D", 0, 0), ("Z", 0, 0)]
    yield "E", 0, 1
    for n in range(1, AHEAD):
        yield from [("Z", 0, n), ("L", 0, n - 1)]
    for n in range(4):
        yield from [("X", 1, n), ("C", 1, n)]
    yield "N", 0, 1


def counted(events, before):
    seen = dict(before)
    for kind, h, n in events:
        yield kind, h, n, dict(seen)
        seen[kind] = seen[kind] + 1
        if kind in "XN":
            seen[n % 2] = seen[n % 2] + 1
        if (kind, n) == ("N", 0):
            seen["first maxima"] = seen[0]


def each_head(eng, turns, per_turn, run):
    G = GROUP_HEADS
    first = list(opening_events()) + [e for h in range(G) for e in head_events(h)]
    body = [e for h in range(G, G + per_turn) for e in head_events(h)]
    last = [e for h in range(G, per_turn) for e in head_events(h, last_head=per_turn - 1)]
    keys = list(KINDS0) + [0, 1]
    count = lambda ev, k: sum(e[0] in "XN" and e[2] % 2 == k if isinstance(k, int) else e[0] == k for e in ev)
    start = {k: count(first, k) for k in keys}
    per = {k: count(body, k) for k in keys}
    run(counted(first, {k: 0 for k in keys}), 0)
    with eng.Fori(0, turns - 1) as it:
        run(counted(body, {k: start[k] + it * per[k] for k in keys}), it)
    run(counted(last, {k: start[k] + (turns - 1) * per[k] for k in keys}), turns - 1)


def attention_layer0(nc, m, ident, ident_bf, mask, q, k, v, out, loads):
    HB = 2 * GROUP_HEADS
    turns = B * NH // HB
    QW = 3 * HD0
    KW = QW + 2
    VW = 3 * HD0

    mbank = m.ps("mbank", [P, 2, SPAN])
    sbank = m.ps("sbank", [P, 2, SPAN])
    obank = m.ps("obank", [P, 2, SPAN])
    xbank = m.ps("xbank", [P, 2, SPAN])
    probs = m.sb("probs", [P, RING0, SPAN])
    probs_hl = m.sb("probs_hl", [P, RING0, 2, SPAN], F32R)
    negmax = m.sb("negmax", [P, 2, len(MAX_PARTS)])
    negmax_span = m.sb("negmax_span", [P, QT])
    negmax_hl = m.sb("negmax_hl", [P, 2, 2, QT, 2], F32R)
    q_stage, k_stage = (m.sb(n, [P, TB, QW], F32R) for n in ("q_stage", "k_stage"))
    v_stage = m.sb("v_stage", [P, 2, TB, VW], F32R)
    q_stack, k_stack = (m.sb(n, [P, 2, S], F32R) for n in ("q_stack", "k_stack"))
    o_low_rows = m.sb("o_low_rows", [HD0, 2, SPAN])
    sum_rows = m.sb("sum_rows", [P, 2, 2, SPAN])
    ones = m.sb("ones", [P, 1])
    ident_r = m.sb("ident_r", [P, P], F32R)

    bank_full = [m.sem(f"bank_full{i}") for i in range(2)]
    bank_free = [m.sem(f"bank_free{i}") for i in range(2)]
    max_full = m.sem("max_full")
    max_done = m.sem("max_done")
    max_step = m.sem("max_step")
    max_split = m.sem("max_split")
    scores_full = m.sem("scores_full")
    exp_done = m.sem("exp_done")
    low_done = [m.sem("low_by_dve"), m.sem("low_by_pool")]
    values_done = m.sem("values_done")
    o_high = m.sem("o_high")
    o_read = m.sem("o_read")
    inverse_done = m.sem("inverse_done")
    o_done = m.sem("o_done")
    copied = m.sem("copied")
    qk_staged = m.sem("qk_staged")
    v_staged = m.sem("v_staged")
    ones_set = m.sem("ones_set")
    rows_set = m.sem("rows_set")
    passed = m.sem("passed")

    next_loaded = m.sem("next_loaded")

    by_pool = lambda k: k in POOL_LOWS
    head_of = lambda it, h: it * HB + h

    group_of = lambda it, h: it * (HB // GROUP_HEADS) + h // GROUP_HEADS

    def lows_before(it, h, k):
        pool = by_pool(k)
        mine = [j for j in range(STEPS) if by_pool(j) == pool]
        return int(pool), head_of(it, h) * len(mine) + sum(j <= k for j in mine)

    block = m.ctx.enter_context(nc.Block())

    @block.sync
    def _(sp):
        for dst, src in loads:
            sp.dma_start(dst, src).then_inc(next_loaded, 16)
        sp.wait_ge(next_loaded, 16 * len(loads))

    @block.tensor
    def _(pe):
        pe.sem_inc(values_done, RING0)
        pe.wait_ge(rows_set, 4)

        def run(events, it):
            for kind, h, n, seen in events:
                hp = h % 2
                if kind == "X":
                    pe.wait_ge(bank_free[n % 2], seen[n % 2] + 1)
                    if n == 0:
                        pe.wait_ge(qk_staged, head_of(it, h) * 2 + 2)
                    for i in range(QT):
                        last = pe.transpose(xbank[0:QW, n % 2, i * P:(i + 1) * P],
                                            f32((k_stage if n % 2 else q_stage)[:, n // 2 * QT + i, :]), ident[:, :])
                    last.then_inc(bank_full[n % 2], 1)
                elif kind == "M":
                    t, c = MAX_PARTS[n]
                    end = min(c + SPAN, (t + 1) * P)
                    if n == 0:
                        for slot in range(2):
                            pe.wait_ge(bank_free[slot], seen[slot] + 1)
                    pe.wait_ge(max_done, seen["M"] + 1)
                    diagonal = end == (t + 1) * P
                    last = pe.matmul(mbank[:, n % 2, 0:end - c], q_stack[0:QW, hp, t * P:(t + 1) * P],
                                     k_stack[0:QW, hp, c:end], start=True, stop=not diagonal)
                    if diagonal:
                        last = pe.matmul(mbank[:, n % 2, end - c - P:end - c], ident_bf[:, :], mask[:, :],
                                         start=False, stop=True)
                    last.then_inc(max_full, 1)
                elif kind == "N":
                    pe.wait_ge(max_split, seen["N"] + 1)
                    pe.wait_ge(bank_free[n], seen[n] + 1)
                    for i in range(QT):
                        last = pe.matmul(xbank[0:2, n, i * P:(i + 1) * P], negmax_hl[:, hp, n, i, :], ident_r[:, :],
                                         start=True, stop=True)
                    last.then_inc(bank_full[n], 1)
                elif kind == "Z":
                    s, kt, c, diagonal = step_of(n)
                    if kt == 0:
                        pe.wait_ge(bank_free[s], (seen[1] if s else seen["first maxima"]) + 1)
                    pe.wait_ge(exp_done, seen["Z"] + 1)
                    last = pe.matmul(sbank[:, n % 2, c:SPAN], k_stack[0:KW, hp, kt * P:(kt + 1) * P],
                                     q_stack[0:KW, hp, s * SPAN + c:(s + 1) * SPAN], start=True, stop=not diagonal)
                    if diagonal:
                        last = pe.matmul(sbank[:, n % 2, c:c + P], mask[:, :], ident_bf[:, :], start=False, stop=True)
                    last.then_inc(scores_full, 1)
                elif kind == "P":
                    s, kt, c, _ = step_of(n)
                    if kt == 0:
                        pe.wait_ge(o_read, seen["O"] + 1)
                        pe.wait_ge(v_staged, head_of(it, h) + 1)
                    maker, count = lows_before(it, h, n)
                    pe.wait_ge(low_done[maker], count)
                    for b in range(2):
                        last = pe.matmul(obank[0:VW, s, c:SPAN], v_stage[:, hp, kt, :], probs_hl[:, n % RING0, b, c:SPAN],
                                         start=(kt == 0 and b == 0), stop=(kt == QT * (s + 1) - 1 and b == 1))
                    last.then_inc(values_done, 1)

        each_head(pe, turns, HB, run)

    @block.scalar
    def _(act):
        nc.scalar.copy(ident_r[:, :], ident[:, :]).then_inc(rows_set, 1)
        act.sem_inc(exp_done, 2)
        act.sem_inc(bank_free[0], 1)
        act.sem_inc(bank_free[1], 1)

        def run(events, it):
            for kind, h, n, seen in events:
                hp = h % 2
                if kind == "Z":
                    s, kt, c, _ = step_of(n)
                    r = n % RING0
                    act.wait_ge(scores_full, seen["Z"] + 1)
                    act.wait_ge(values_done, seen["Z"] + 1)
                    nc.scalar.activation(probs[:, r, c:SPAN], sbank[:, n % 2, c:SPAN], ACT.Exp)
                    nc.scalar.activation(probs_hl[:, r, 0, c:SPAN], sbank[:, n % 2, c:SPAN], ACT.Exp
                                         ).then_inc(exp_done, 1)
                elif kind == "C" and n % 2 == 0:
                    act.wait_ge(bank_full[0], seen[0])
                    nc.scalar.copy(q_stack[0:QW, hp, n // 2 * SPAN:(n // 2 + 1) * SPAN], xbank[0:QW, 0, :]
                                   ).then_inc(bank_free[0], 1)
                elif kind == "D":
                    act.wait_ge(bank_full[n], seen[n])
                    nc.scalar.copy(q_stack[QW:KW, hp, n * SPAN:(n + 1) * SPAN], xbank[0:2, n, :]
                                   ).then_inc(bank_free[n], 1)
                elif kind == "O":
                    since = O_AT[0] - QT if n == 0 else O_AT[1]
                    if isinstance(seen["P"], int) and seen["P"] == STEPS * B * NH:
                        since = 0
                    act.wait_ge(values_done, seen["P"] + RING0 - since)
                    act.wait_ge(o_read, seen["O"])
                    j, group = h % GROUP_HEADS, h // GROUP_HEADS % 2
                    if j == 0:
                        act.wait_ge(o_done, seen["Q"] + 1)
                    nc.scalar.copy(o_low_rows[:, n, :], obank[HD0:2 * HD0, n, :])
                    nc.scalar.copy(sum_rows[j * HD0:(j + 1) * HD0, group, n, :], obank[2 * HD0:3 * HD0, n, :]
                                   ).then_inc(o_high, 1)

        each_head(act, turns, HB, run)

    @block.vector
    def _(dve):
        dve.wait_ge(ones_set, 1)
        for par in range(2):
            nc.vector.tensor_copy(k_stack[QW:KW, par, :], ones[QW:KW, :].to_broadcast([2, S])).then_inc(rows_set, 1)
        nc.vector.tensor_copy(v_stage[:, :, :, 2 * HD0:VW].rearrange("p a t c -> p (a t) c"),
                              ones[:, :, None].to_broadcast([P, 2 * TB, HD0])).then_inc(rows_set, 1)
        dve.sem_inc(max_done, 2)
        dve.sem_inc(o_read, 1)

        def run(events, it):
            for kind, h, n, seen in events:
                hp = h % 2
                if kind == "M":
                    t, c = MAX_PARTS[n]
                    dve.wait_ge(max_full, seen["M"] + 1)
                    nc.vector.tensor_reduce(negmax[:, hp, n:n + 1], mbank[:, n % 2, 0:min(SPAN, (t + 1) * P - c)],
                                            AX.X, ALU.max, negate=True).then_inc(max_done, 1)
                elif kind == "E":
                    step = head_of(it, h) * 3 + n
                    dve.wait_ge(max_done, seen["M"] + 2)
                    if n == 0:
                        span = negmax[:, hp, 0:QT]
                    else:
                        span = negmax_span[:, :]
                        halves = negmax[:, hp, QT:3 * QT].rearrange("p (i two) -> p i two", two=2)
                        nc.vector.tensor_tensor(span, halves[:, :, 0], halves[:, :, 1], ALU.min).then_inc(max_step, 1)
                        dve.wait_ge(max_step, step + 1)
                    nc.vector.tensor_copy(negmax_hl[:, hp, n, :, 0], span).then_inc(max_step, 1)
                    dve.wait_ge(max_step, step + 1 + n)
                    nc.vector.tensor_tensor(negmax_hl[:, hp, n, :, 1], span, f32(negmax_hl[:, hp, n, :, 0]),
                                            ALU.subtract).then_inc(max_split, 1)
                elif kind == "L" and not by_pool(n):
                    _, _, c, _ = step_of(n)
                    r = n % RING0
                    dve.wait_ge(exp_done, seen["L"] + 3)
                    nc.vector.tensor_tensor(probs_hl[:, r, 1, c:SPAN], probs[:, r, c:SPAN],
                                            f32(probs_hl[:, r, 0, c:SPAN]), ALU.subtract).then_inc(low_done[0], 1)
                elif kind == "C" and n % 2:
                    dve.wait_ge(bank_full[1], seen[1])
                    nc.vector.tensor_copy(k_stack[0:QW, hp, n // 2 * SPAN:(n // 2 + 1) * SPAN], xbank[0:QW, 1, :]
                                          ).then_inc(bank_free[1], 1)
                elif kind == "O":
                    dve.wait_ge(o_high, seen["O"] + 1)
                    j = h % GROUP_HEADS
                    dst = out[j * HD0:(j + 1) * HD0, bass.ds(group_of(it, h), 1), n * SPAN:(n + 1) * SPAN]
                    nc.vector.tensor_tensor(dst.rearrange("p o t -> p (o t)"), obank[0:HD0, n, :], o_low_rows[:, n, :],
                                            ALU.add).then_inc(o_read, 1)
                elif kind == "I":
                    dve.wait_ge(o_high, seen["O"])
                    part = sum_rows[:, (h // GROUP_HEADS - 1) % 2].rearrange("p s t -> p (s t)")[:, n * P:(n + 1) * P]
                    nc.vector.reciprocal(part, part).then_inc(inverse_done, 1)

        each_head(dve, turns, HB, run)

    @block.gpsimd
    def _(pool):
        nc.gpsimd.memset(ones[:, :], 1.0).then_inc(ones_set, 1)
        pool.wait_ge(ones_set, 1)
        pool.sem_inc(o_done, 1)

        def pool_wait(sem, value):
            wait(pool, sem, value)
            pool.sem_inc(passed, 1)

        def split(dst, x, high_at, low_at, count):
            w = x.shape[-1]
            for i in high_at:
                nc.gpsimd.tensor_tensor(dst[:, :, i * w:(i + 1) * w], x, ones[:, :, None].to_broadcast([P, TB, w]),
                                        ALU.mult).then_inc(copied, 1)
            pool_wait(copied, count + len(high_at))
            return nc.gpsimd.tensor_tensor(dst[:, :, low_at * w:(low_at + 1) * w], x, f32(dst[:, :, 0:w]), ALU.subtract)

        def run(events, it):
            for kind, h, n, seen in events:
                hp = h % 2
                j, g = h % GROUP_HEADS, group_of(it, h)
                rows_of = lambda x: x[:, bass.ds(g, 1), :, j * HD0:(j + 1) * HD0].rearrange("p o t c -> p (o t) c")
                if kind == "G":
                    for slot in range(2):
                        pool_wait(bank_full[slot], seen[slot])
                    count = seen["G"] * 2 + seen["V"]
                    if n == 0:
                        last = split(q_stage[:, :, :], rows_of(q), (0, 2), 1, count)
                    else:
                        last = split(k_stage[:, :, :], rows_of(k), (0, 1), 2, count)
                    last.then_inc(qk_staged, 1)
                elif kind == "V":
                    pool_wait(values_done, seen["P"] - V_AT + RING0)
                    split(v_stage[:, hp], rows_of(v), (0,), 1, seen["G"] * 2 + seen["V"]).then_inc(v_staged, 1)
                elif kind == "L" and by_pool(n):
                    _, _, c, _ = step_of(n)
                    r = n % RING0
                    pool_wait(exp_done, seen["L"] + 3)
                    nc.gpsimd.tensor_tensor(probs_hl[:, r, 1, c:SPAN], probs[:, r, c:SPAN],
                                            f32(probs_hl[:, r, 0, c:SPAN]), ALU.subtract).then_inc(low_done[1], 1)
                elif kind == "Q":
                    pool_wait(inverse_done, seen["I"])
                    rows = out[:, bass.ds(group_of(it, h - GROUP_HEADS), 1), n * SPAN:(n + 1) * SPAN]
                    rows = rows.rearrange("p o t -> p (o t)")
                    nc.gpsimd.tensor_tensor(rows, rows, sum_rows[:, (h // GROUP_HEADS - 1) % 2, n, :],
                                            ALU.mult).then_inc(o_done, 1)

        each_head(pool, turns, HB, run)
        pool.wait_ge(o_done, 2 * B * NH // GROUP_HEADS + 1)


SCORES_AT = [[[0], [1, 2], [3], []], [[0, 1], [], [2], [], [3], [], [], []]]
OUTPUTS_AT = [[[], [], [0, 1], [2, 3]], [[0], [1], [2], [3], [], [], [], []]]


def unit_events(u, last_unit):
    h, s = divmod(u, 2)
    more = lambda head: last_unit is None or head <= last_unit // 2
    follows = last_unit is None or u < last_unit
    nh, ns = divmod(u + 1, 2)
    ev, later = [], []
    if s == 1 and more(h + 2):
        ev.append(("G", h + 2, 0, 0))
    for kt in range(QT * (s + 1)):
        ev.append(("T", h, s, kt))
        ev += later
        later = []
        if follows:
            ev += [("S", nh, ns, n) for n in SCORES_AT[s][kt]]
            later = [("R", nh, ns, n) for n in SCORES_AT[s][kt]]
        if kt:
            ev.append(("P", h, s, kt - 1))
        if u > 0:
            ev += [("Y", (u - 1) // 2, (u - 1) % 2, n) for n in OUTPUTS_AT[s][kt]]
        if s == 1 and kt >= QT and more(h + 2):
            ev.append(("X", h + 2, 0, kt - QT))
    ev.append(("P", h, s, QT * (s + 1) - 1))
    ev += later
    ev.append(("O", h, s, 0))
    return ev


def first_events():
    ev = []
    for h in range(2):
        ev += [("G", h, 0, 0)] + [("X", h, 0, n) for n in range(4)]
    for n in range(QT):
        ev += [("S", 0, 0, n)] + ([("R", 0, 0, n - 1)] if n else [])
    return ev + [("R", 0, 0, QT - 1)] + unit_events(0, None)


def last_events(units):
    ev = []
    for u in range(1, units):
        ev += unit_events(u, units - 1)
    return ev + [("Y", (units - 1) // 2, 1, tt) for tt in range(QT)]


WORK = 3


def numbered(events, before):
    seen, uses, sources = dict(before), 0, {}
    for kind, h, s, n in events:
        now = dict(seen)
        if kind in "TXY":
            slot = now["slot"] = uses % WORK
            uses += 1
            seen[slot] = seen[slot] + 1
            sources[kind, h, s, n] = slot, seen[slot]
        if kind == "P":
            now["source"] = sources["T", h, s, n]
        yield kind, h, s, n, now
        seen[kind] = seen[kind] + 1


def each_turn(eng, turns, units, run):
    first, body = first_events(), [e for u in range(1, units + 1) for e in unit_events(u, None)]
    kinds, slots = "STRPGXOY", range(WORK)

    def counts(ev):
        uses = sum(e[0] in "TXY" for e in ev)
        assert uses % WORK == 0
        return {**{k: sum(e[0] == k for e in ev) for k in kinds}, **{i: uses // WORK for i in slots}}

    start, per = counts(first), counts(body)
    run(numbered(first, {k: 0 for k in start}), 0)
    with eng.Fori(0, turns - 1) as it:
        run(numbered(body, {k: start[k] + it * per[k] for k in start}), it)
    done = turns - 1
    run(numbered(last_events(units), {k: start[k] + done * per[k] for k in start}), done)


def attention_layer1(nc, m, ident, ident_bf, mask, src, out):
    HB = 2
    units = 2 * HB
    turns = NH // HB
    RPT = 3
    S_AHEAD = 2

    scores = m.ps("scores", [P, S_AHEAD, 2 * SPAN])
    work = m.ps("work", [P, WORK, SPAN])
    obank = m.ps("obank", [P, SPAN])
    probs = [m.sb(f"probs{s}", [P, QT * QT * s + QT * (QT + 1) // 2, P]) for s in range(2)]
    pT_hl = m.sb("pT_hl", [P, RPT, 2, SPAN], F32R)
    row = m.sb("row", [P, 3, 4 * QT])
    q_stage = m.sb("q_stage", [P, TB, 2 * ROPE], F32R)
    q_stack = m.sb("q_stack", [P, 2, S], F32R)
    ones = m.sb("ones", [P, 1])
    qa_hl = m.sb("qa_hl", [P, 2, 2, S], F32R)
    oT_hl = m.sb("oT_hl", [P, 2, 2, SPAN], F32R)
    wabs = m.sb("wabs", [P, 2, 2, 3, LAT], F32R)
    wov = m.sb("wov", [P, 2, 2, D], F32R)

    work_full = [m.sem(f"work_full{i}") for i in range(WORK)]
    work_free = [m.sem(f"work_free{i}") for i in range(WORK)]
    scores_full = m.sem("scores_full")
    max_done = m.sem("max_done")
    exp_done = m.sem("exp_done")
    inverse_done = m.sem("inverse_done")
    turned_high = m.sem("turned_high")
    values_done = m.sem("values_done")
    o_high = m.sem("o_high")
    o_read = m.sem("o_read")
    x_high = m.sem("x_high")
    copied = m.sem("copied")
    staged = m.sem("staged")
    zeroed = m.sem("zeroed")
    ones_set = m.sem("ones_set")
    passed = m.sem("passed")
    wabs_loaded = [m.sem(f"wabs_loaded{i}") for i in range(2)]
    wov_loaded = [m.sem(f"wov_loaded{i}") for i in range(2)]

    def tile_of(s, n):
        first = sum(QT * s + i + 1 for i in range(n))
        return first, QT * s + n + 1

    def ring(n, s):
        return (n + QT * s) % RPT

    head_of = lambda it, h: it * HB + h

    block = m.ctx.enter_context(nc.Block())

    @block.sync
    def _(sp):
        def load(h, par, ready=None):
            if ready is not None:
                sp.wait_ge(x_high, 2 * (h - 1))
            sp.dma_start(f32(wabs[:, par]), src["wabs_dram"][bass.ds(h, 1)].rearrange("o p a k c -> p (o a) k c")
                         ).then_inc(wabs_loaded[par], 16)
            if ready is not None:
                sp.wait_ge(o_high, 2 * h - 1)
            sp.dma_start(f32(wov[:, par]), src["wov_dram"][bass.ds(h, 1)].rearrange("o p a c -> p (o a) c")
                         ).then_inc(wov_loaded[par], 16)
        load(0, 0)
        load(1, 1)
        with sp.Fori(1, NH // 2) as i:
            for par in range(2):
                load(2 * i + par, par, ready=True)

    @block.tensor
    def _(pe):
        pe.sem_inc(values_done, RPT)

        def run(events, it):
            for kind, h, s, n, seen in events:
                hp = h % 2
                if kind in "TXY":
                    slot = seen["slot"]
                    pe.wait_ge(work_free[slot], seen[slot] + 1)
                if kind == "X":
                    if n < 2:
                        if n == 0:
                            pe.wait_ge(wabs_loaded[hp], 16 * (it * (HB // 2) + h // 2 + 1))
                        steps = [(j, a, b) for j in range(3) for a, b in THREE]
                        for i, (j, a, b) in enumerate(steps):
                            last = pe.matmul(work[:, slot, :], wabs[:, hp, a, j, :],
                                             src["qT_hl"][:, b, j, n * SPAN:(n + 1) * SPAN],
                                             start=(i == 0), stop=(i == len(steps) - 1))
                    else:
                        if n == 2:
                            pe.wait_ge(staged, head_of(it, h) + 1)
                        for i in range(QT):
                            last = pe.transpose(work[:, slot, i * P:(i + 1) * P],
                                                f32(q_stage[:, n % 2 * QT + i, :]), ident[:, :])
                    last.then_inc(work_full[slot], 1)
                elif kind == "S":
                    if s == 0 and n == 0:
                        for i in range(WORK):
                            pe.wait_ge(work_free[i], seen[i])
                    pe.wait_ge(exp_done, seen["S"] + 1)
                    t = QT * s + n
                    buf = n % S_AHEAD
                    rows = slice(t * P, (t + 1) * P)
                    for c in range(0, (t + 1) * P, SPAN):
                        cols = slice(c, min(c + SPAN, (t + 1) * P))
                        steps = [(qa_hl[:, hp, a, rows], src["kT_hl"][:, b, cols]) for a, b in THREE]
                        steps += [(q_stack[:, hp, rows], src["kpe"][:, part, cols]) for part in range(2)]
                        diagonal = cols.stop == (t + 1) * P
                        for i, (lhs, rhs) in enumerate(steps):
                            last = pe.matmul(scores[:, buf, cols], lhs, rhs, start=(i == 0),
                                             stop=(not diagonal and i == len(steps) - 1))
                        if diagonal:
                            last = pe.matmul(scores[:, buf, t * P:(t + 1) * P], ident_bf[:, :], mask[:, :],
                                             start=False, stop=True)
                    last.then_inc(scores_full, 1)
                elif kind == "T":
                    if n == 0:
                        pe.wait_ge(exp_done, seen["O"] * QT + QT + S_AHEAD)
                    for i in range(max(0, n - QT * s), QT):
                        first, _ = tile_of(s, i)
                        last = pe.transpose(work[:, slot, i * P:(i + 1) * P], probs[s][:, first + n, :], ident[:, :])
                    last.then_inc(work_full[slot], 1)
                elif kind == "P":
                    if n == 0:
                        pe.wait_ge(o_read, seen["O"] + 1)
                    bank, uses = seen["source"]
                    pe.wait_ge(work_free[bank], uses + 1)
                    c = max(0, n - QT * s) * P
                    for i, (a, b) in enumerate(THREE):
                        last = pe.matmul(obank[:, c:SPAN], src["v_hl"][:, a, n, :], pT_hl[:, ring(n, s), b, c:SPAN],
                                         start=(n == 0 and i == 0), stop=(n == QT * (s + 1) - 1 and i == 2))
                    last.then_inc(values_done, 1)
                elif kind == "Y":
                    pe.wait_ge(o_read, seen["O"] + 1)
                    if s == 0 and n == 0:
                        pe.wait_ge(wov_loaded[hp], 16 * (it * (HB // 2) + h // 2 + 1))
                    for i, (a, b) in enumerate(THREE):
                        last = pe.matmul(work[:, slot, :], oT_hl[:, s, a, n * P:(n + 1) * P], wov[:, hp, b, :],
                                         start=(i == 0), stop=(i == 2))
                    last.then_inc(work_full[slot], 1)

        each_turn(pe, turns, units, run)

    @block.scalar
    def _(act):
        act.sem_inc(exp_done, S_AHEAD)

        def run(events, it):
            for kind, h, s, n, seen in events:
                hp, slot = h % 2, seen.get("slot")
                if kind == "S":
                    first, wide = tile_of(s, n)
                    row_slot = (hp * 2 + s) * QT + n
                    act.wait_ge(max_done, seen["S"] + 1)
                    nc.scalar.activation(probs[s][:, first:first + wide, :].rearrange("p k c -> p (k c)"),
                                         scores[:, n % S_AHEAD, 0:wide * P], ACT.Exp, bias=row[:, 0, row_slot:row_slot + 1],
                                         accum_out=row[:, 1, row_slot:row_slot + 1]).then_inc(exp_done, 1)
                elif kind == "T":
                    c = max(0, n - QT * s) * P
                    act.wait_ge(work_full[slot], seen[slot] + 1)
                    act.wait_ge(values_done, seen["T"] + 1)
                    nc.scalar.copy(pT_hl[:, ring(n, s), 0, c:SPAN], work[:, slot, c:SPAN]).then_inc(turned_high, 1)
                elif kind == "X" and n < 3:
                    act.wait_ge(work_full[slot], seen[slot] + 1)
                    if n < 2:
                        nc.scalar.copy(qa_hl[:, hp, 0, n * SPAN:(n + 1) * SPAN], work[:, slot, :]).then_inc(x_high, 1)
                    else:
                        nc.scalar.copy(q_stack[:, hp, 0:SPAN], work[:, slot, :]).then_inc(work_free[slot], 1)
                elif kind == "O":
                    act.wait_ge(values_done, seen["P"] + RPT)
                    for i in range(WORK):
                        act.wait_ge(work_full[i], seen[i])
                    nc.scalar.copy(oT_hl[:, s, 0, :], obank[:, :]).then_inc(o_high, 1)

        each_turn(act, turns, units, run)

    @block.vector
    def _(dve):
        for i in range(WORK):
            dve.sem_inc(work_free[i], 1)
        dve.sem_inc(o_read, 1)
        nc.vector.memset(out[:, :, :], 0.0).then_inc(zeroed, 1)
        dve.wait_ge(zeroed, 1)

        def run(events, it):
            for kind, h, s, n, seen in events:
                hp, slot = h % 2, seen.get("slot")
                row_slot = (hp * 2 + s) * QT + n
                if kind == "S":
                    _, wide = tile_of(s, n)
                    dve.wait_ge(scores_full, seen["S"] + 1)
                    nc.vector.tensor_reduce(row[:, 0, row_slot:row_slot + 1], scores[:, n % S_AHEAD, 0:wide * P],
                                            AX.X, ALU.max, negate=True).then_inc(max_done, 1)
                elif kind == "R":
                    dve.wait_ge(exp_done, seen["R"] + 1 + S_AHEAD)
                    nc.vector.reciprocal(row[:, 2, row_slot:row_slot + 1], row[:, 1, row_slot:row_slot + 1]
                                         ).then_inc(inverse_done, 1)
                elif kind == "T":
                    c = max(0, n - QT * s) * P
                    r = ring(n, s)
                    dve.wait_ge(turned_high, seen["T"] + 1)
                    nc.vector.tensor_tensor(pT_hl[:, r, 1, c:SPAN], work[:, slot, c:SPAN], f32(pT_hl[:, r, 0, c:SPAN]),
                                            ALU.subtract).then_inc(work_free[slot], 1)
                elif kind == "X" and n < 2:
                    cols = slice(n * SPAN, (n + 1) * SPAN)
                    dve.wait_ge(x_high, 2 * head_of(it, h) + n + 1)
                    nc.vector.tensor_tensor(qa_hl[:, hp, 1, cols], work[:, slot, :], f32(qa_hl[:, hp, 0, cols]),
                                            ALU.subtract).then_inc(work_free[slot], 1)
                elif kind == "X" and n == 3:
                    dve.wait_ge(work_full[slot], seen[slot] + 1)
                    nc.vector.tensor_copy(q_stack[:, hp, SPAN:S], work[:, slot, :]).then_inc(work_free[slot], 1)
                elif kind == "Y":
                    dve.wait_ge(work_full[slot], seen[slot] + 1)
                    dve.wait_ge(inverse_done, seen["Y"] + 1)
                    t = QT * s + n
                    nc.vector.scalar_tensor_tensor(out=out[:, t, :], in0=work[:, slot, :],
                                                   scalar=row[:, 2, row_slot:row_slot + 1], in1=out[:, t, :],
                                                   op0=ALU.mult, op1=ALU.add).then_inc(work_free[slot], 1)
                elif kind == "O":
                    dve.wait_ge(o_high, seen["O"] + 1)
                    nc.vector.tensor_tensor(oT_hl[:, s, 1, :], obank[:, :], f32(oT_hl[:, s, 0, :]),
                                            ALU.subtract).then_inc(o_read, 1)

        each_turn(dve, turns, units, run)
        for i in range(WORK):
            dve.wait_ge(work_free[i], 24 * NH // WORK + 1)

    @block.gpsimd
    def _(pool):
        nc.gpsimd.memset(ones[:, :], 1.0).then_inc(ones_set, 1)
        pool.wait_ge(ones_set, 1)

        def pool_wait(sem, value):
            wait(pool, sem, value)
            pool.sem_inc(passed, 1)

        def run(events, it):
            for kind, h, s, n, seen in events:
                if kind == "G":
                    for i in range(WORK):
                        pool_wait(work_full[i], seen[i])
                    x = src["qpe"][:, :, bass.ds(head_of(it, h) * ROPE, ROPE)]
                    nc.gpsimd.tensor_tensor(q_stage[:, :, 0:ROPE], x, ones[:, :, None].to_broadcast([P, TB, ROPE]),
                                            ALU.mult).then_inc(copied, 1)
                    pool_wait(copied, seen["G"] + 1)
                    nc.gpsimd.tensor_tensor(q_stage[:, :, ROPE:2 * ROPE], x, f32(q_stage[:, :, 0:ROPE]), ALU.subtract
                                            ).then_inc(staged, 1)

        each_turn(pool, turns, units, run)


HT = HG // P
SPANS = NT // QT
WBANKS = 3 * HT


def group_events(half, turn_next=True, quantise_after=False, first=False, last=False):
    ev = []
    banks = iter([("W", half, i, 0) for i in range(WBANKS)] if turn_next else [])
    for sp in range(SPANS):
        for ht in range(HT):
            ev.append(("H", half, sp, ht))
            if sp >= 1:
                ev += [e for e in [next(banks, None)] if e]
            if quantise_after and sp < 3:
                ev.append(("AL"[ht], half, sp, False))
            before = (half, sp - 1) if sp else (1 - half, SPANS - 1)
            if sp or not first:
                ev += [("D", *before, t) for t in range(ht * QT // HT, (ht + 1) * QT // HT)]
            ev.append(("K", half, sp, ht))
    return ev + ([("D", half, SPANS - 1, t) for t in range(QT)] if last else [])


def quantised(half):
    return [(k, half, w, True) for w in range(3) for k in "AL"]


def first_ternary_group():
    after = lambda w: [("A", 0, w, False), ("L", 0, w, False)]
    turn = lambda *banks: [("W", 0, i, 0) for i in banks]
    second = quantised(1)
    beside = [second[0:2], second[2:4], second[4:6], after(0), turn(0, 1), turn(2, 3) + after(1), turn(4, 5), after(2)]
    ev = []
    for sp in range(SPANS):
        for ht in range(HT):
            ev += [("H", 0, sp, ht)] + beside[sp * HT + ht]
            if sp:
                ev += [("D", 0, sp - 1, t) for t in range(ht * QT // HT, (ht + 1) * QT // HT)]
            ev.append(("K", 0, sp, ht))
    return ev


def each_group(eng, ternary, run):
    kinds = "HKDWAL"
    opening = (quantised(0) if ternary else []) + [("W", 1, i, 0) for i in range(WBANKS)]
    first = first_ternary_group() if ternary else group_events(0, first=True)
    first += group_events(1, quantise_after=ternary)
    body = group_events(0, quantise_after=ternary) + group_events(1, quantise_after=ternary)
    tail = group_events(0) + group_events(1, turn_next=False, last=True)
    count = lambda ev: {k: sum(e[0] == k for e in ev) for k in kinds}
    at = {k: 0 for k in kinds}
    for events, turn in ((opening, None), (first, 0)):
        run(numbered(events, at), turn)
        at = {k: at[k] + count(events)[k] for k in kinds}
    per = count(body)
    with eng.Fori(1, NG // 2 - 1) as it:
        run(numbered(body, {k: at[k] + (it - 1) * per[k] for k in kinds}), it)
    done = NG // 2 - 1
    run(numbered(tail, {k: at[k] + (done - 1) * per[k] for k in kinds}), done)


def feed_forward(nc, m, ident, xT_hl, acc, gate, up, down, ternary=None):
    PARTS = 1 if ternary is not None else 2
    pairs = [(0, 0), (1, 0)] if ternary is not None else [(0, 0), (1, 0), (0, 1)]
    WC = KT * HG
    raw = m.sb("raw", [P, 2, 3, WC])
    wT = m.sb("wT", [P, 2, PARTS, 3, WC], F32R)
    silu = m.sb("silu", [P, HT, SPAN])
    hid = m.sb("hid", [P, HT, SPAN])
    h_hl = m.sb("h_hl", [P, 2, HT, 2, SPAN], F32R)
    gbank = m.ps("gbank", [P, HT, SPAN])
    ubank = m.ps("ubank", [P, HT, SPAN])
    ybank = m.ps("ybank", [P, 2, SPAN])
    if ternary is None:
        wbank, turned_src, turn_ident = m.ps("wbank", [P, 2, SPAN]), raw, ident
    else:
        ident_bf, squares = ternary
        NGR = WC // GROUP
        wbank = m.ps("wbank", [P, 2, 2 * SPAN], BF16)
        quant = m.sb("quant", [P, 2, 3, WC], BF16)
        wb = m.sb("wb", [P, WC], BF16)
        ratio = m.sb("ratio", [P, WC], BF16)
        lower = m.sb("lower", [P, WC], BF16)
        level = m.sb("level", [P, WC], BF16)
        diff = m.sb("diff", [P, WC], BF16)
        total = m.sb("total", [P, NGR])
        mean = m.sb("mean", [P, NGR], BF16)
        scale = m.sb("scale", [P, NGR], BF16)
        inverse = m.sb("inverse", [P, NGR])
        sq = m.sb("sq", [P, SPAN])
        turned_src, turn_ident = quant, ident_bf
    loaded = [m.sem(f"loaded{i}") for i in range(2)]
    zeroed = m.sem("zeroed")
    w_full = m.sem("w_full")
    w_high = m.sem("w_high")
    w_read = m.sem("w_read")
    g_full, u_full = m.sem("g_full"), m.sem("u_full")
    silu_done = m.sem("silu_done")
    hid_done = m.sem("hid_done")
    h_high = m.sem("h_high")
    h_low = m.sem("h_low")
    y_full = m.sem("y_full")
    y_read = m.sem("y_read")
    squared, sq_added = m.sem("squared"), m.sem("sq_added")
    cast_done = m.sem("cast_done")
    q_step = m.sem("q_step")
    inverse_done = m.sem("inverse_done")
    ratio_done = m.sem("ratio_done")
    lower_done, level_done = m.sem("lower_done"), m.sem("level_done")
    l_step = m.sem("l_step")
    quant_done = m.sem("quant_done")

    def blocks(half, i):
        w, sub = divmod(i, HT)
        if w < 2:
            tile = turned_src[:, half, w, :].rearrange("p (h d) -> p h d", h=HT)
            return [tile[:, sub, c * P:(c + 1) * P] for c in range(KT)]
        tile = turned_src[:, half, 2, :].rearrange("p (o c) -> p o c", o=KT)
        return [tile[:, o, sub * P:(sub + 1) * P] for o in range(KT)]

    def turned_to(half, part, i):
        w, sub = divmod(i, HT)
        if w < 2:
            return wT[:, half, part, w, :].rearrange("p (c h) -> p c h", c=KT)[:, :, sub * P:(sub + 1) * P]
        return wT[:, half, part, 2, sub * D:(sub + 1) * D].rearrange("p (c h) -> p c h", c=KT)

    def bank_view(i):
        return wbank[:, i % 2, 0:SPAN].rearrange("p (c h) -> p c h", c=KT)

    in_groups = lambda x: x[:, :].rearrange("p (n g) -> p n g", g=GROUP)

    def make_ratio(eng, ops, done):
        eng.wait_ge(inverse_done, done + 1)
        ops.tensor_tensor(in_groups(ratio), in_groups(wb), inverse[:, :, None].to_broadcast([P, NGR, GROUP]),
                          ALU.mult).then_inc(ratio_done, 1)

    def make_quantised(eng, ops, half, w, done, turned=None):
        eng.wait_ge(level_done, done + 1)
        ops.tensor_tensor(in_groups(ratio), in_groups(level), scale[:, :, None].to_broadcast([P, NGR, GROUP]),
                          ALU.mult).then_inc(l_step, 1)
        eng.wait_ge(l_step, 2 * done + 1)
        ops.tensor_tensor(diff[:, :], ratio[:, :], wb[:, :], ALU.subtract).then_inc(l_step, 1)
        eng.wait_ge(l_step, 2 * done + 2)
        if turned is not None:
            eng.wait_ge(w_full, turned)
        ops.tensor_tensor(quant[:, half, w, :], wb[:, :], diff[:, :], ALU.add).then_inc(quant_done, 1)

    block = m.ctx.enter_context(nc.Block())

    @block.sync
    def _(sp):
        def load(g, half, again):
            if again and ternary is None:
                sp.wait_ge(w_full, WBANKS * (g - 1))
            elif again:
                sp.wait_ge(cast_done, 3 * (g - 1))
            for w, src in ((0, gate), (1, up)):
                sp.dma_start(raw[:, half, w, :].rearrange("p (h d) -> p h d", h=HT),
                             src[bass.ds(g * HG, HG), :].rearrange("(h p) d -> p h d", p=P)
                             ).then_inc(loaded[half], 16)
            sp.dma_start(raw[:, half, 2, :].rearrange("p (o c) -> p o c", o=KT),
                         down[:, bass.ds(g * HG, HG)].rearrange("(o p) c -> p o c", p=P)
                         ).then_inc(loaded[half], 16)
        load(0, 0, False)
        load(1, 1, False)
        with sp.Fori(1, NG // 2) as i:
            for half in range(2):
                load(2 * i + half, half, True)

    def load_count(it, half):
        return 48 if it is None else 48 * (it + 1 + half)

    @block.tensor
    def _(pe):
        pe.sem_inc(y_full, 1)

        def run(events, it):
            for kind, half, a, b, seen in events:
                if kind == "W":
                    to = 1 - half
                    if a == 0 and ternary is None:
                        pe.wait_ge(loaded[to], load_count(it, half))
                    elif a == 0:
                        pe.wait_ge(quant_done, 4 if it is None else 3 * (2 * it + half + 2) + 1)
                    pe.wait_ge(w_read, seen["W"] + 1)
                    for c, blk in enumerate(blocks(to, a)):
                        last = pe.transpose(wbank[:, a % 2, c * P:(c + 1) * P], blk, turn_ident[:, :])
                    last.then_inc(w_full, 1)
                elif kind == "H":
                    if a == 0 and b == 0:
                        pe.wait_ge(w_read, seen["W"] + 2)
                    pe.wait_ge(hid_done, seen["H"] + 1)
                    for bank, w, full in ((gbank, 0, g_full), (ubank, 1, u_full)):
                        steps = [(c, xa, wa) for c in range(KT) for xa, wa in pairs]
                        for n, (c, xa, wa) in enumerate(steps):
                            last = pe.matmul(bank[:, b, :], wT[:, half, wa, w, c * HG + b * P:c * HG + (b + 1) * P],
                                             xT_hl[:, xa, c, a * SPAN:(a + 1) * SPAN], start=(n == 0),
                                             stop=(n == len(steps) - 1))
                        last.then_inc(full, 1)
                elif kind == "D":
                    if b == 0:
                        pe.wait_ge(h_low, seen["K"] + HT)
                    pe.wait_ge(y_read, seen["D"] + 1)
                    steps = [(ht, ha, wa) for ht in range(HT) for ha, wa in pairs]
                    for n, (ht, ha, wa) in enumerate(steps):
                        last = pe.matmul(ybank[:, b % 2, :], h_hl[:, a % 2, ht, ha, b * P:(b + 1) * P],
                                         wT[:, half, wa, 2, ht * D:(ht + 1) * D],
                                         start=(n == 0), stop=(n == len(steps) - 1))
                    last.then_inc(y_full, 1)

        each_group(pe, ternary is not None, run)

    @block.scalar
    def _(act):
        if ternary is not None:
            act.sem_inc(w_read, 2)

        def run(events, it):
            for kind, half, a, b, seen in events:
                if kind == "W":
                    act.wait_ge(w_full, seen["W"] + 1)
                    nc.scalar.copy(turned_to(1 - half, 0, a), bank_view(a)
                                   ).then_inc(w_high if ternary is None else w_read, 1)
                elif kind == "H":
                    act.wait_ge(g_full, seen["H"] + 1)
                    nc.scalar.activation(silu[:, b, :], gbank[:, b, :], ACT.Silu).then_inc(silu_done, 1)
                elif kind == "K":
                    act.wait_ge(hid_done, seen["K"] + 1 + HT)
                    if ternary is not None:
                        act.wait_ge(sq_added, seen["K"] + 1)
                        nc.scalar.activation(sq[:, :], hid[:, b, :], ACT.Square).then_inc(squared, 1)
                    wait(act, y_full, seen["D"] + 1 - (b + 1) * QT // HT)
                    nc.scalar.copy(h_hl[:, a % 2, b, 0, :], hid[:, b, :]).then_inc(h_high, 1)
                elif kind == "A":
                    act.wait_ge(loaded[half], 48 if b else 48 * (it + 2))
                    act.wait_ge(quant_done, seen["A"] + 1)
                    nc.scalar.copy(wb[:, :], raw[:, half, a, :]).then_inc(cast_done, 1)

        each_group(act, ternary is not None, run)

    @block.vector
    def _(dve):
        if ternary is None:
            dve.sem_inc(w_read, 2)
        else:
            dve.sem_inc(h_low, HT)
        dve.sem_inc(hid_done, HT)
        dve.sem_inc(y_read, 2)
        dve.wait_ge(zeroed, 1)

        def run(events, it):
            for kind, half, a, b, seen in events:
                if kind == "W" and ternary is None:
                    dve.wait_ge(w_high, seen["W"] + 1)
                    nc.vector.tensor_tensor(turned_to(1 - half, 1, a), bank_view(a), f32(turned_to(1 - half, 0, a)),
                                            ALU.subtract).then_inc(w_read, 1)
                elif kind == "H":
                    dve.wait_ge(silu_done, seen["H"] + 1)
                    dve.wait_ge(u_full, seen["H"] + 1)
                    dve.wait_ge(h_low, seen["H"] + 1)
                    nc.vector.tensor_tensor(hid[:, b, :], silu[:, b, :], ubank[:, b, :], ALU.mult
                                            ).then_inc(hid_done, 1)
                elif kind == "K" and ternary is not None:
                    dve.wait_ge(h_high, seen["K"] + 1)
                    nc.vector.tensor_tensor(h_hl[:, a % 2, b, 1, :], hid[:, b, :], f32(h_hl[:, a % 2, b, 0, :]),
                                            ALU.subtract).then_inc(h_low, 1)
                elif kind == "D":
                    dve.wait_ge(y_full, seen["D"] + 1 + 1)
                    y = acc[:, a * QT + b, :]
                    nc.vector.tensor_tensor(y, y, ybank[:, b % 2, :], ALU.add).then_inc(y_read, 1)
                elif kind == "A":
                    dve.wait_ge(cast_done, seen["A"] + 1)
                    nc.vector.tensor_reduce(total[:, :], wb[:, :].rearrange("p (n g) -> p n g", g=GROUP), AX.X,
                                            ALU.add, apply_absolute_value=True).then_inc(q_step, 1)
                    dve.wait_ge(q_step, 3 * seen["A"] + 1)
                    nc.vector.tensor_scalar(mean[:, :], total[:, :], 1.0 / GROUP, None, ALU.mult).then_inc(q_step, 1)
                    dve.wait_ge(q_step, 3 * seen["A"] + 2)
                    nc.vector.tensor_scalar(scale[:, :], mean[:, :], 1e-8, None, ALU.max).then_inc(q_step, 1)
                    dve.wait_ge(q_step, 3 * seen["A"] + 3)
                    nc.vector.reciprocal(inverse[:, :], scale[:, :]).then_inc(inverse_done, 1)
                    if b:
                        make_ratio(dve, nc.vector, seen["A"])
                elif kind == "L":
                    dve.wait_ge(ratio_done, seen["L"] + 1)
                    nc.vector.tensor_scalar(lower[:, :], ratio[:, :], -0.5, None, ALU.is_lt).then_inc(lower_done, 1)
                    dve.wait_ge(lower_done, seen["L"] + 1)
                    nc.vector.scalar_tensor_tensor(out=level[:, :], in0=ratio[:, :], scalar=0.5, in1=lower[:, :],
                                                   op0=ALU.is_gt, op1=ALU.subtract).then_inc(level_done, 1)
                    if b:
                        make_quantised(dve, nc.vector, half, a, seen["L"])

        each_group(dve, ternary is not None, run)
        dve.wait_ge(y_read, NG * NT + 2)

    @block.gpsimd
    def _(pool):
        if ternary is None:
            pool.sem_inc(h_low, HT)
        else:
            pool.sem_inc(quant_done, 1)
            pool.sem_inc(sq_added, 1)
            nc.gpsimd.memset(squares[:, :], 0.0).then_inc(squared, 1)
            pool.wait_ge(squared, 1)
        nc.gpsimd.memset(acc[:, :, :], 0.0).then_inc(zeroed, 1)

        def run(events, it):
            for kind, half, a, b, seen in events:
                if kind == "K" and ternary is not None:
                    pool.wait_ge(squared, seen["K"] + 2)
                    tok = slice(a * SPAN, (a + 1) * SPAN)
                    nc.gpsimd.tensor_tensor(squares[:, tok], squares[:, tok], sq[:, :], ALU.add).then_inc(sq_added, 1)
                elif kind == "K":
                    pool.wait_ge(h_high, seen["K"] + 1)
                    nc.gpsimd.tensor_tensor(h_hl[:, a % 2, b, 1, :], hid[:, b, :], f32(h_hl[:, a % 2, b, 0, :]),
                                            ALU.subtract).then_inc(h_low, 1)
                elif kind == "A" and not b:
                    make_ratio(pool, nc.gpsimd, seen["A"])
                elif kind == "L" and not b:
                    turned = WBANKS * (2 * it + half + 1)
                    make_quantised(pool, nc.gpsimd, half, a, seen["L"], turned)

        each_group(pool, ternary is not None, run)


def scale_rows(nc, m, squares, acc):
    ones = m.sb("ones", [P, 1])
    eps = m.sb("eps", [P, 1])
    root = m.sb("root", [P, NT])
    inv = m.sb("inv", [P, NT])
    bank = m.ps("bank", [P, NT])
    ready, summed, rooted, inverted, scaled = (m.sem(x) for x in ("ready", "summed", "rooted", "inverted", "scaled"))
    with nc.Block() as block:
        @block.vector
        def _(dve):
            nc.vector.memset(ones[:, :], 1.0).then_inc(ready, 1)
            nc.vector.memset(eps[:, :], EPS_F32).then_inc(ready, 1)
            dve.wait_ge(rooted, 1)
            nc.vector.reciprocal(inv[:, :], root[:, :]).then_inc(inverted, 1)
            dve.wait_ge(inverted, 1)
            for t in range(NT):
                nc.vector.tensor_scalar(acc[:, t, :], acc[:, t, :], inv[:, t:t + 1], None, ALU.mult).then_inc(scaled, 1)
            dve.wait_ge(scaled, NT)

        @block.tensor
        def _(pe):
            pe.wait_ge(ready, 2)
            for t in range(NT):
                last = pe.matmul(bank[:, t:t + 1], squares[:, t * P:(t + 1) * P], ones[:, :], start=True, stop=True)
            last.then_inc(summed, 1)

        @block.scalar
        def _(act):
            act.wait_ge(ready, 2)
            act.wait_ge(summed, 1)
            nc.scalar.activation(root[:, :], bank[:, :], ACT.Sqrt, bias=eps[:, 0:1], scale=1.0 / HID
                                 ).then_inc(rooted, 1)


def absorbed_weights(nc, m, q_nope, k_b, v_b, owT, wabs_dram, wov_dram):
    wabs = m.sb("wabs", [P, 2, 2, 3, LAT], F32R)
    wov = m.sb("wov", [P, 2, 2, D], F32R)
    abank = m.ps("abank", [P, 2, SPAN])
    vbank = m.ps("vbank", [P, 2, SPAN])
    full, high, low = m.sem("full"), m.sem("high"), m.sem("low")
    stored = [m.sem(f"stored{i}") for i in range(2)]
    with nc.Block() as block:
        @block.tensor
        def _(pe):
            for h in range(NH):
                wait(pe, low, 2 * (h - 1))
                for j in range(3):
                    last = pe.matmul(abank[:, h % 2, j * P:(j + 1) * P], q_nope[:, h, j * P:(j + 1) * P],
                                     k_b[:, h, :], start=True, stop=True)
                last.then_inc(full, 1)
                pe.matmul(vbank[:, h % 2, :], v_b[:, h, :], owT[:, h, :], start=True, stop=True).then_inc(full, 1)

        def pieces(h):
            par = h % 2
            yield 2 * h, SCALE1, abank[:, par, 0:3 * P].rearrange("p (j c) -> p j c", j=3), wabs[:, par, 0], wabs[:, par, 1]
            yield 2 * h + 1, 1.0, vbank[:, par, :], wov[:, par, 0], wov[:, par, 1]

        @block.scalar
        def _(act):
            for h in range(NH):
                wait(act, stored[h % 2], 32 * (h // 2))
                for n, scale, src, hi, lo in pieces(h):
                    act.wait_ge(full, n + 1)
                    nc.scalar.activation(hi, src, ACT.Copy, scale=scale).then_inc(high, 1)

        @block.vector
        def _(dve):
            for h in range(NH):
                for n, scale, src, hi, lo in pieces(h):
                    dve.wait_ge(high, n + 1)
                    nc.vector.scalar_tensor_tensor(out=lo, in0=src, scalar=scale, in1=f32(hi), op0=ALU.mult,
                                                   op1=ALU.subtract).then_inc(low, 1)

        @block.sync
        def _(sp):
            for h in range(NH):
                par = h % 2
                sp.wait_ge(low, 2 * h + 2)
                sp.dma_start(wabs_dram[h], f32(wabs[:, par])).then_inc(stored[par], 16)
                sp.dma_start(wov_dram[h], f32(wov[:, par])).then_inc(stored[par], 16)
            for par in range(2):
                sp.wait_ge(stored[par], 32 * NH // 2)


def latent_operands(nc, m, ident, xT_hl, waT, wpT, norm_w, rope, out):
    WA = QL + LAT + ROPE
    HW = WA // 2
    down = m.sb("down", [P, 2, WA])
    squares = m.sb("squares", [P, QL])
    sums = m.sb("sums", [P, 2, 2])
    root = m.sb("root", [P, 2, 2])
    inv = m.sb("inv", [P, 2, 2])
    eps = m.sb("eps", [P, 1])
    normed = m.sb("normed", [P, 2, QL + LAT])
    k_parts = m.sb("k_parts", [P, 2, 3, ROPE])
    k_stage = m.sb("k_stage", [P, 2, 2, 2 * ROPE], F32R)
    direct = m.sb("direct", [P, NH * ROPE])
    crossed = m.sb("crossed", [P, NH * ROPE])
    dbank = m.ps("dbank", [P, 2, 2, SPAN])
    tbank = m.ps("tbank", [P, SPAN])
    kbank = m.ps("kbank", [P, 2 * P])
    pbank = m.ps("pbank", [P, 2, SPAN])
    cos, sin = rope
    names = ("eps_set", "d_full", "d_read", "sq_done", "root_done", "inv_done", "norm_done", "k_mul",
             "k_sum", "k_high", "k_staged", "v_high", "v_low", "t_full", "t_high", "t_low", "k_full", "k_read",
             "p_full", "p_read", "p_sum")
    (eps_set, d_full, d_read, sq_done, root_done, inv_done, norm_done, k_mul, k_sum, k_high, k_staged,
     v_high, v_low, t_full, t_high, t_low, k_full, k_read, p_full, p_read, p_sum) = (m.sem(n) for n in names)
    qT_hl, kT_hl, kpe, v_hl, qpe = (out[n] for n in ("qT_hl", "kT_hl", "kpe", "v_hl", "qpe"))
    with nc.Block() as block:
        @block.tensor
        def _(pe):
            for i in range(TB + 2):
                if i < TB:
                    t = i
                    wait(pe, d_read, t - 1)
                    for half in range(2):
                        steps = [(c, a, b) for c in range(KT) for a, b in THREE]
                        for n, (c, a, b) in enumerate(steps):
                            last = pe.matmul(dbank[:, t % 2, half, 0:HW], xT_hl[:, a, c, t * P:(t + 1) * P],
                                             waT[:, b, c, half * HW:(half + 1) * HW],
                                             start=(n == 0), stop=(n == len(steps) - 1))
                    last.then_inc(d_full, 1)
                if 0 <= i - 1 < TB:
                    t = i - 1
                    pe.wait_ge(norm_done, 2 * t + 2)
                    wait(pe, t_low, 2 * t)
                    for c in range(4):
                        last = pe.transpose(tbank[:, c * P:(c + 1) * P], normed[:, t % 2, c * P:(c + 1) * P], ident[:, :])
                    last.then_inc(t_full, 1)
                    pe.wait_ge(k_staged, t + 1)
                    wait(pe, k_read, t)
                    for part in range(2):
                        last = pe.transpose(kbank[:, part * P:(part + 1) * P], f32(k_stage[:, t % 2, part, :]), ident[:, :])
                    last.then_inc(k_full, 1)
                if i >= 2:
                    t = i - 2
                    pe.wait_ge(t_low, 2 * t + 2)
                    wait(pe, p_read, t)
                    for half in range(2):
                        steps = [(j, a, b) for j in range(3) for a, b in THREE]
                        for n, (j, a, b) in enumerate(steps):
                            last = pe.matmul(pbank[:, half, :], qT_hl[:, a, j, t * P:(t + 1) * P],
                                             wpT[:, b, j, half * SPAN:(half + 1) * SPAN],
                                             start=(n == 0), stop=(n == len(steps) - 1))
                    last.then_inc(p_full, 1)

        @block.scalar
        def _(act):
            act.wait_ge(eps_set, 1)
            for i in range(TB + 1):
                if i < TB:
                    t = i
                    act.wait_ge(d_full, t + 1)
                    wait(act, k_sum, t - 1)
                    wait(act, norm_done, 2 * (t - 1))
                    nc.scalar.copy(down[:, t % 2, :].rearrange("p (h c) -> p h c", h=2),
                                   dbank[:, t % 2, :, 0:HW]).then_inc(d_read, 1)
                    act.wait_ge(d_read, t + 1)
                    for n, (a, b) in enumerate(((0, QL), (QL, QL + LAT))):
                        wait(act, sq_done, 2 * t + n)
                        nc.scalar.activation(squares[:, 0:b - a], down[:, t % 2, a:b], ACT.Square,
                                             accum_out=sums[:, t % 2, n:n + 1]).then_inc(sq_done, 1)
                    act.wait_ge(sq_done, 2 * t + 2)
                    for n, size in enumerate((QL, LAT)):
                        nc.scalar.activation(root[:, t % 2, n:n + 1], sums[:, t % 2, n:n + 1], ACT.Sqrt,
                                             bias=eps[:, 0:1], scale=1.0 / size).then_inc(root_done, 1)
                if i >= 1:
                    t = i - 1
                    tok = slice(t * P, (t + 1) * P)
                    act.wait_ge(t_full, t + 1)
                    nc.scalar.copy(qT_hl[:, 0, :, tok], tbank[:, 0:QL].rearrange("p (j t) -> p j t", j=3)
                                   ).then_inc(t_high, 1)
                    nc.scalar.copy(kT_hl[:, 0, tok], tbank[:, QL:QL + P]).then_inc(t_high, 1)
                    act.wait_ge(k_full, t + 1)
                    nc.scalar.copy(kpe[:, :, tok], kbank[:, :].rearrange("p (a t) -> p a t", a=2)).then_inc(k_read, 1)

        @block.vector
        def _(dve):
            nc.vector.memset(eps[:, :], EPS_RMS).then_inc(eps_set, 1)
            for i in range(TB + 2):
                if i < TB:
                    t = i
                    par = t % 2
                    dve.wait_ge(d_read, t + 1)
                    wait(dve, k_staged, t - 1)
                    key = down[:, par, QL + LAT:WA].rearrange("p (j d) -> p j d", j=2)
                    nc.vector.tensor_tensor(k_parts[:, par, 0, :].rearrange("p (j d) -> p j d", j=2), key,
                                            cos[:, 1, t, None, :].to_broadcast([P, 2, HALF1]), ALU.mult).then_inc(k_mul, 1)
                    for j in range(2):
                        nc.vector.tensor_tensor(k_parts[:, par, 1, j * HALF1:(j + 1) * HALF1], key[:, 1 - j, :],
                                                sin[:, 1, t, j, :], ALU.mult).then_inc(k_mul, 1)
                    dve.wait_ge(root_done, 2 * t + 2)
                    nc.vector.reciprocal(inv[:, par, :], root[:, par, :]).then_inc(inv_done, 1)
                    dve.wait_ge(inv_done, t + 1)
                    wait(dve, t_full, t - 1)
                    wait(dve, v_low, t - 1)
                    for n, (a, b) in enumerate(((0, QL), (QL, QL + LAT))):
                        nc.vector.scalar_tensor_tensor(out=normed[:, par, a:b], in0=down[:, par, a:b],
                                                       scalar=inv[:, par, n:n + 1], in1=norm_w[:, a:b],
                                                       op0=ALU.mult, op1=ALU.mult).then_inc(norm_done, 1)
                if 0 <= i - 1 < TB:
                    t = i - 1
                    tok = slice(t * P, (t + 1) * P)
                    dve.wait_ge(t_high, 2 * t + 2)
                    nc.vector.tensor_tensor(qT_hl[:, 1, :, tok], tbank[:, 0:QL].rearrange("p (j t) -> p j t", j=3),
                                            f32(qT_hl[:, 0, :, tok]), ALU.subtract).then_inc(t_low, 1)
                    nc.vector.tensor_tensor(kT_hl[:, 1, tok], tbank[:, QL:QL + P], f32(kT_hl[:, 0, tok]),
                                            ALU.subtract).then_inc(t_low, 1)
                if i >= 2:
                    t = i - 2
                    dve.wait_ge(p_full, t + 1)
                    wait(dve, p_sum, t)
                    src = pbank[:, :, :].rearrange("p a (h j d) -> p (a h) j d", j=2, d=HALF1)
                    flat = pbank[:, :, :].rearrange("p a (h d) -> p (a h) d", d=HALF1)
                    nc.vector.tensor_tensor(direct[:, :].rearrange("p (h d) -> p h d", d=HALF1), flat,
                                            cos[:, 0, t, None, :].to_broadcast([P, 2 * NH, HALF1]), ALU.mult)
                    dst = crossed[:, :].rearrange("p (h j d) -> p h j d", j=2, d=HALF1)
                    for j in range(2):
                        last = nc.vector.tensor_tensor(dst[:, :, j, :], src[:, :, 1 - j, :],
                                                       sin[:, 0, t, j, None, :].to_broadcast([P, NH, HALF1]), ALU.mult)
                    last.then_inc(p_read, 1)
            dve.wait_ge(t_low, 2 * TB)

        @block.gpsimd
        def _(pool):
            for i in range(TB + 2):
                if i < TB:
                    t = i
                    par = t % 2
                    pool.wait_ge(k_mul, 3 * t + 3)
                    nc.gpsimd.tensor_tensor(k_parts[:, par, 2, :], k_parts[:, par, 0, :], k_parts[:, par, 1, :],
                                            ALU.add).then_inc(k_sum, 1)
                    pool.wait_ge(k_sum, t + 1)
                    wait(pool, k_full, t - 1)
                    for n in range(2):
                        nc.gpsimd.tensor_copy(k_stage[:, par, 0, n * ROPE:(n + 1) * ROPE], k_parts[:, par, 2, :]
                                              ).then_inc(k_high, 1)
                    pool.wait_ge(k_high, 3 * t + 2)
                    nc.gpsimd.tensor_tensor(k_stage[:, par, 1, 0:ROPE], k_parts[:, par, 2, :],
                                            f32(k_stage[:, par, 0, 0:ROPE]), ALU.subtract).then_inc(k_high, 1)
                    pool.wait_ge(k_high, 3 * t + 3)
                    nc.gpsimd.tensor_tensor(k_stage[:, par, 1, ROPE:2 * ROPE], k_parts[:, par, 2, :],
                                            f32(k_stage[:, par, 0, 0:ROPE]), ALU.subtract).then_inc(k_staged, 1)
                    pool.wait_ge(norm_done, 2 * t + 2)
                    nc.gpsimd.tensor_copy(v_hl[:, 0, t, :], normed[:, par, QL:QL + LAT]).then_inc(v_high, 1)
                    pool.wait_ge(v_high, t + 1)
                    nc.gpsimd.tensor_tensor(v_hl[:, 1, t, :], normed[:, par, QL:QL + LAT], f32(v_hl[:, 0, t, :]),
                                            ALU.subtract).then_inc(v_low, 1)
                if i >= 2:
                    t = i - 2
                    pool.wait_ge(p_read, t + 1)
                    nc.gpsimd.tensor_tensor(qpe[:, t, :], direct[:, :], crossed[:, :], ALU.add
                                            ).then_inc(p_sum, 1)


def two_layers(nc, a, out):
    from contextlib import contextmanager

    sems = []

    @contextmanager
    def phase(tag):
        with ExitStack() as ctx:
            yield Mem(nc, ctx, tag, sems)

    def clear_semaphores():
        nc.clear_and_free_semaphores(sems)
        sems.clear()
        nc.all_engine_barrier()

    def dram(name, shape, dt=F32):
        return nc.dram_tensor(name, shape, dt, kind="Internal").ap()

    tables = lambda cos, sin, layer: [(dst[:, i], a[f"{name}_{w}{layer}"]) for dst, name in ((cos, "cos"), (sin, "sin"))
                                      for i, w in enumerate("qk")]
    rows = lambda x: x.rearrange("b s d -> (b s) d")
    x0, y_out = rows(a["L0_attn_hidden_states"]), rows(out)
    x1, x2, x3 = (dram(f"x{i}", [NT * P, D]) for i in (1, 2, 3))
    wabs_dram = dram("wabs_dram", [NH, P, 2, 3, LAT])
    wov_dram = dram("wov_dram", [NH, P, 2, D])
    waT_dram = dram("waT_dram", [P, 2, KT, QL + LAT + ROPE])
    wpT_dram = dram("wpT_dram", [P, 2, 3, NH * ROPE])

    with phase("all") as top:
        ident, mask = top.sb("ident", [P, P]), top.sb("mask", [P, P], BF16)
        ident_bf = top.sb("ident_bf", [P, P], BF16)
        with phase("const") as m:
            constants(nc, m, ident, ident_bf, mask)

        view = lambda n: a[n].rearrange("(o p) i -> p o i", p=P)
        with phase("x0") as after:
            with phase("l0") as keep:
                v = keep.sb("v", [P, B * KT, TB, P])
                with phase("l0qk") as high:
                    q, k = (high.sb(n, [P, B * KT, TB, P], side="right") for n in "qk")
                    with phase("l0w") as w:
                        Wqkv = w.sb("Wqkv", [P, 2, 3, KT, D], F32R)
                        with phase("l0wt") as m:
                            raw = m.sb("raw", [P, 3, KT, D])
                            names = ("L0_attn_Wq", "L0_attn_Wk", "L0_attn_Wv")
                            jobs = [j for i in range(3) for j in square_jobs(raw[:, i], Wqkv, i, i)]
                            transpose_weights(nc, m, ident, jobs, [(raw[:, i], view(n)) for i, n in enumerate(names)])
                        for b in range(B):
                            with phase(f"l0x{b}") as x:
                                xT = x.sb("xT", [P, 2, KT, S], F32R)
                                cos, sin = x.sb("cos", [P, 2, TB, HALF0]), x.sb("sin", [P, 2, TB, 2, HALF0])
                                with phase(f"l0n{b}") as m:
                                    norm_transposed(nc, m, ident, x0[b * S:(b + 1) * S], TB, xT, tables(cos, sin, 0))
                                with phase(f"l0p{b}") as m:
                                    qkv_layer0(nc, m, b, xT, Wqkv, (cos, sin), q, k, v)
                    oT = keep.sb("oT", [P, B * KT, S])
                    raw = keep.sb("raw", [P, KT, D])
                    with phase("l0a") as m:
                        attention_layer0(nc, m, ident, ident_bf, mask, q, k, v, oT,
                                         [(raw[:, :, :], view("L0_attn_Wo"))])
                xT0 = after.sb("xT0", [P, 2, KT, NT * P], F32R, side="right")
                WoT = keep.sb("WoT", [P, 2, 1, KT, D], F32R)
                with phase("l0ot") as m:
                    transpose_weights(nc, m, ident, square_jobs(raw, WoT, 0, -1), [])
                with phase("l0o") as m:
                    tile_oT = lambda t: oT[:, t // TB * KT:(t // TB + 1) * KT, t % TB * P:(t % TB + 1) * P]
                    project_residual_norm(nc, m, ident, NT, x0, x1, tile_oT, WoT[:, :, 0], xT0)
            clear_semaphores()

            with phase("f0") as keep:
                acc = keep.sb("acc", [P, NT, D])
                with phase("f0f") as m:
                    feed_forward(nc, m, ident, xT0, acc, a["L0_ffn_w_gate"], a["L0_ffn_w_up"], a["L0_ffn_w_down"])
                with phase("f0r") as m:
                    residual(nc, m, NT, x1, x2, lambda t: acc[:, t, :])
        clear_semaphores()

        with phase("w1") as w:
            q_nope = w.sb("q_nope", [P, NH, QL])
            k_b, v_b = w.sb("k_b", [P, NH, LAT]), w.sb("v_b", [P, NH, LAT])
            owT = w.sb("owT", [P, NH, D])
            waT = w.sb("waT", [P, 2, KT, QL + LAT + ROPE], F32R)
            wpT = w.sb("wpT", [P, 2, 3, NH * ROPE], F32R)
            with phase("w1t") as m:
                qa = m.sb("qa", [P, 3, D])
                kva = m.sb("kva", [P, 2, D])
                qp = m.sb("qp", [P, NH // 2, QL])
                ow = m.sb("ow", [P, KT, NH * VD // 2])
                q_b = a["L1_attn_q_b_w"].rearrange("(h r) j -> r h j", r=QHD)
                kv_b = a["L1_attn_kv_b_w"].rearrange("(h t d) c -> t d h c", t=2, d=NOPE)
                o_w = a["L1_attn_o_w"].rearrange("(o p) v -> p o v", p=P)
                pe_rows = q_b[NOPE:QHD].rearrange("r (n e) j -> e r n j", e=2)
                loads = [(qa[:, :, :], a["L1_attn_q_a_w"].rearrange("(o p) i -> p o i", p=P)),
                         (kva[:, 0, :], a["L1_attn_kv_a_w"][0:P]),
                         (kva[0:ROPE, 1, :], a["L1_attn_kv_a_w"][P:P + ROPE]),
                         (qp[0:ROPE], pe_rows[0]), (qp[ROPE:P], pe_rows[1]),
                         (q_nope[:, :, :], q_b[0:NOPE]), (k_b[:, :, :], kv_b[0]), (v_b[:, :, :], kv_b[1]),
                         (ow[:, :, :], o_w[:, :, 0:NH * VD // 2])]
                jobs = [([(qa[:, i, c * P:(c + 1) * P], i * P) for i in range(3)] + [(kva[:, 0, c * P:(c + 1) * P], 3 * P)],
                         whole(SPAN), waT[:, 0, c, 0:SPAN], waT[:, 1, c, 0:SPAN], 1) for c in range(KT)]
                jobs.append(([(kva[0:ROPE, 1, c * P:(c + 1) * P], c * ROPE) for c in range(KT)],
                             lambda bank: bank[:, 0:KT * ROPE].rearrange("p (c r) -> p c r", c=KT),
                             waT[:, 0, :, SPAN:SPAN + ROPE], waT[:, 1, :, SPAN:SPAN + ROPE], 2))
                jobs += [([(qp[:, 4 * g + i, j * P:(j + 1) * P], i * P) for i in range(4)], whole(SPAN),
                          wpT[:, 0, j, g * SPAN:(g + 1) * SPAN], wpT[:, 1, j, g * SPAN:(g + 1) * SPAN], 4)
                         for j in range(3) for g in range(2)]
                jobs += [([(ow[:, o, h * P:(h + 1) * P], o * P) for o in range(KT)], whole(SPAN), owT[:, h, :], None, 8)
                         for h in range(NH // 2)]
                transpose_weights(nc, m, ident, jobs, loads)
            with phase("w1u") as m:
                ow = m.sb("ow", [P, KT, NH * VD // 2])
                transpose_weights(nc, m, ident,
                                  [([(ow[:, o, h * P:(h + 1) * P], o * P) for o in range(KT)], whole(SPAN),
                                    owT[:, NH // 2 + h, :], None, 0) for h in range(NH // 2)],
                                  [(ow[:, :, :], o_w[:, :, NH * VD // 2:])],
                                  [(waT_dram, f32(waT[:, :, :, :])), (wpT_dram, f32(wpT[:, :, :, :]))])
            with phase("w1a") as m:
                absorbed_weights(nc, m, q_nope, k_b, v_b, owT, wabs_dram, wov_dram)
        clear_semaphores()
        for b in range(B):
            with phase(f"l1_{b}") as keep:
                acc = keep.sb("acc", [P, TB, D])
                with phase(f"l1k{b}") as mid:
                    ops = {"qT_hl": mid.sb("qT_hl", [P, 2, 3, S], F32R), "kT_hl": mid.sb("kT_hl", [P, 2, S], F32R),
                           "kpe": mid.sb("kpe", [P, 2, S], F32R), "v_hl": mid.sb("v_hl", [P, 2, TB, LAT], F32R),
                           "qpe": mid.sb("qpe", [P, TB, NH * ROPE]), "wabs_dram": wabs_dram, "wov_dram": wov_dram}
                    with phase(f"l1x{b}") as x:
                        xT = x.sb("xT", [P, 2, KT, S], F32R)
                        cos, sin = x.sb("cos", [P, 2, TB, HALF1]), x.sb("sin", [P, 2, TB, 2, HALF1])
                        waT = x.sb("waT", [P, 2, KT, QL + LAT + ROPE], F32R)
                        wpT = x.sb("wpT", [P, 2, 3, NH * ROPE], F32R)
                        norm_w = x.sb("norm_w", [P, QL + LAT])
                        operands = [(f32(waT[:, :, :, :]), waT_dram), (f32(wpT[:, :, :, :]), wpT_dram),
                                    (norm_w[:, 0:QL], a["L1_attn_q_a_ln_w"].partition_broadcast(P)),
                                    (norm_w[:, QL:QL + LAT], a["L1_attn_kv_a_ln_w"].partition_broadcast(P))]
                        with phase(f"l1n{b}") as m:
                            norm_transposed(nc, m, ident, x2[b * S:(b + 1) * S], TB, xT,
                                            tables(cos, sin, 1) + operands)
                        with phase(f"l1p{b}") as m:
                            latent_operands(nc, m, ident, xT, waT, wpT, norm_w, (cos, sin), ops)
                    with phase(f"l1a{b}") as m:
                        attention_layer1(nc, m, ident, ident_bf, mask, ops, acc)
                with phase(f"l1r{b}") as m:
                    residual(nc, m, TB, x2[b * S:(b + 1) * S], x3[b * S:(b + 1) * S], lambda t: acc[:, t, :])
            clear_semaphores()

        with phase("f1") as keep:
            acc = keep.sb("acc", [P, NT, D])
            with phase("f1x") as x:
                squares = x.sb("squares", [P, NT * P])
                xT = x.sb("xT", [P, 2, KT, NT * P], F32R)
                with phase("f1n") as m:
                    norm_transposed(nc, m, ident, x3, NT, xT)
                with phase("f1f") as m:
                    w = a["L1_ffn_w_gate_up"]
                    feed_forward(nc, m, ident, xT, acc, w[0:HID], w[HID:2 * HID], a["L1_ffn_w_proj"],
                                 (ident_bf, squares))
                with phase("f1s") as m:
                    scale_rows(nc, m, squares, acc)
            with phase("f1r") as m:
                residual(nc, m, NT, x3, y_out, lambda t: acc[:, t, :])
        clear_semaphores()


_INS = ['L0_attn_hidden_states', 'L0_attn_Wq', 'L0_attn_Wk', 'L0_attn_Wv', 'L0_attn_Wo', 'L0_ffn_w_gate',
        'L0_ffn_w_up', 'L0_ffn_w_down', 'L1_attn_q_a_w', 'L1_attn_q_a_ln_w', 'L1_attn_q_b_w', 'L1_attn_kv_a_w',
        'L1_attn_kv_a_ln_w', 'L1_attn_kv_b_w', 'L1_attn_o_w', 'L1_ffn_w_gate_up', 'L1_ffn_w_proj']


def rotary_tables(width, scale):
    freq = (1.0 / 10000.0 ** (np.arange(0, width, 2, dtype=np.float32) / width)).astype(np.float32)
    angle = np.outer(np.arange(S, dtype=np.float32), freq).astype(np.float32)
    tiles = lambda x: x.astype(np.float32).reshape(TB, P, width // 2).transpose(1, 0, 2)
    cos, sin = tiles(np.cos(angle) * np.float32(scale)), tiles(np.sin(angle) * np.float32(scale))
    return np.ascontiguousarray(cos), np.ascontiguousarray(np.stack([-sin, sin], axis=2))


def kernel(**inputs):
    import concourse.bacc as _bacc
    from concourse.bass_utils import run_bass_kernel_spmd as _run

    nc = _bacc.Bacc("TRN2", target_bir_lowering=False, num_devices=1)
    host = {n: np.ascontiguousarray(inputs[n]) for n in _INS}
    for i, (width, scale) in enumerate(((HD0, SCALE0), (ROPE, SCALE1))):
        host[f"cos_k{i}"], host[f"sin_k{i}"] = rotary_tables(width, 1.0)
        host[f"cos_q{i}"], host[f"sin_q{i}"] = rotary_tables(width, scale)
    aps = {n: nc.dram_tensor(f"in_{n}", x.shape, mybir.dt.from_np(x.dtype), kind="ExternalInput").ap()
           for n, x in host.items()}
    out = nc.dram_tensor("out_0", (B, S, D), F32, kind="ExternalOutput").ap()
    two_layers(nc, aps, out)
    r = _run(nc, [{f"in_{n}": x for n, x in host.items()}], core_ids=[0])
    return r.results[0]["out_0"]
```
